# Optimizing a Trainium2 kernel written in Bass

```python
import numpy as np
import jax
import jax.numpy as jnp

def _softmax(x, axis=-1):
    return jax.nn.softmax(x, axis=axis)

def _gelu(x):
    return jax.nn.gelu(x, approximate=True)

def _silu(x):
    return jax.nn.silu(x)

def _sigmoid(x):
    return jax.nn.sigmoid(x)

def _layernorm(x, axis=-1, eps=1e-05):
    m = jnp.mean(x, axis=axis, keepdims=True)
    v = jnp.var(x, axis=axis, keepdims=True)
    return (x - m) / jnp.sqrt(v + eps)

def _scatter_add(tgt, idx, src, axis=0):
    return tgt.at[idx].add(src)

def _segment_sum(src, seg, n):
    return jax.ops.segment_sum(src, seg, n)
kernel_name = 'mk_perceiver_d2_seqx_r4_0d64d1'

def setup_inputs(seed: int=0):
    np.random.seed(seed)
    _w = jnp.asarray

    def _rec_inputs():
        import jax
        import jax.numpy as jnp
        _rk = jax.random.key(seed)
        x = -0.0002928 + 1 * jax.random.normal(jax.random.fold_in(_rk, 1), (16, 64, 256), jnp.float32)
        _lenS = 64 - jax.random.randint(jax.random.fold_in(_rk, 7), (16,), 0, max(1, 64 // 4) + 1, jnp.int32)
        _lenS2 = 256 - jax.random.randint(jax.random.fold_in(_rk, 8), (16,), 0, max(1, 256 // 4) + 1, jnp.int32)
        _ctx_1024P = jax.random.normal(jax.random.fold_in(_rk, 11), (16, 16, 256), jnp.float32)
        _ctx_1024c = jax.random.dirichlet(jax.random.fold_in(_rk, 511), 0.3 * jnp.ones((16,), jnp.float32), (16, 256))
        _ctx_1024t = jnp.einsum('bsk,bkd->bsd', _ctx_1024c, _ctx_1024P)
        _ctx_1024t = _ctx_1024t * jax.lax.rsqrt(jnp.mean(jnp.square(_ctx_1024t)) + 1e-12) * 0.953939
        ctx_1024 = -1.39393e-06 + 0.999914 * (_ctx_1024t + 0.3 * jax.random.normal(jax.random.fold_in(_rk, 611), (16, 256, 256), jnp.float32))
        itok_BxS_0_1023 = jax.random.randint(jax.random.fold_in(_rk, 13), (16, 64), 0, 256, jnp.int32)
        itok_BxS2_0_2047 = jax.random.randint(jax.random.fold_in(_rk, 14), (16, 256), 0, 512, jnp.int32)
        _validS = jnp.arange(64)[None, :] < _lenS[:, None]
        _validS2 = jnp.arange(256)[None, :] < _lenS2[:, None]
        _causal = jnp.tril(jnp.ones((64, 64), dtype=bool))
        mask_1x1xSxS2_bk0 = jnp.logical_not(jnp.broadcast_to(_validS2[0:1, None, None, :], (1, 1, 64, 256)))
        return (x, ctx_1024, itok_BxS_0_1023, itok_BxS2_0_2047, mask_1x1xSxS2_bk0)
    x, ctx_1024, itok_BxS_0_1023, itok_BxS2_0_2047, mask_1x1xSxS2_bk0 = _rec_inputs()

    def _L0_xattn_setup():
        import jax, jax.numpy as jnp
        import numpy as np
        D_MODEL = 256
        H = 16
        D_K = D_MODEL // H
        NEG = -1000000000.0

        def _split_heads(x):
            B, S, _ = x.shape
            return x.reshape(B, S, H, D_K).transpose(0, 2, 1, 3)
        key = jax.random.key(seed)
        ks = jax.random.split(key, 12)
        B, S, D = (2, 512, D_MODEL)
        scale = 1.0 / np.sqrt(D)
        inp = {'q': jax.random.normal(ks[0], (B, S, D), jnp.float32), 'k': jax.random.normal(ks[1], (B, S, D), jnp.float32), 'v': jax.random.normal(ks[2], (B, S, D), jnp.float32), 'mask': jnp.tril(jnp.ones((S, S), bool))[None, None], 'Wq': jax.random.normal(ks[3], (D, D), jnp.float32) * scale, 'bq': jax.random.normal(ks[4], (D,), jnp.float32) * scale, 'Wk': jax.random.normal(ks[5], (D, D), jnp.float32) * scale, 'bk': jax.random.normal(ks[6], (D,), jnp.float32) * scale, 'Wv': jax.random.normal(ks[7], (D, D), jnp.float32) * scale, 'bv': jax.random.normal(ks[8], (D,), jnp.float32) * scale, 'Wo': jax.random.normal(ks[9], (D, D), jnp.float32) * scale, 'bo': jax.random.normal(ks[10], (D,), jnp.float32) * scale}
        return inp
    _L0_xattn_all = _L0_xattn_setup()
    _L0_xattn_in = {k: v for k, v in _L0_xattn_all.items() if k in ('Wq', 'bq', 'Wk', 'bk', 'Wv', 'bv', 'Wo', 'bo')}
    del _L0_xattn_all

    def _L0_attn_setup():
        import jax, jax.numpy as jnp
        import numpy as np
        EMBED_DIM = 256
        NUM_HEADS = 16
        CONTEXT = 250
        MAX_PERIOD = 10000.0
        HEAD_DIM = EMBED_DIM // NUM_HEADS

        def _apply_rope(q, k):
            B, H, T, D = q.shape
            ds = jnp.arange(D // 2, dtype=jnp.float32)
            freqs = jnp.exp(ds * (-np.log(MAX_PERIOD) * 2.0 / D))
            ts = jnp.arange(T, dtype=jnp.float32)
            ang = ts[:, None] * freqs[None, :]
            cos = jnp.cos(ang)
            sin = jnp.sin(ang)

            def rot(x):
                xr = x.reshape(B, H, T, D // 2, 2)
                xa, xb = (xr[..., 0], xr[..., 1])
                ya = xa * cos - xb * sin
                yb = xa * sin + xb * cos
                return jnp.stack([ya, yb], axis=-1).reshape(B, H, T, D)
            return (rot(q), rot(k))
        key = jax.random.key(seed)
        k1, k2, k3 = jax.random.split(key, 3)
        B, T = (2, 512)
        query = jax.random.normal(k1, (B, T, EMBED_DIM), jnp.float32)
        in_proj_w = jax.random.normal(k2, (3 * EMBED_DIM, EMBED_DIM), jnp.float32) * EMBED_DIM ** (-0.5)
        out_proj_w = jax.random.normal(k3, (EMBED_DIM, EMBED_DIM), jnp.float32) * EMBED_DIM ** (-0.5)
        return {'query': query, 'in_proj_w': in_proj_w, 'out_proj_w': out_proj_w}
    _L0_attn_all = _L0_attn_setup()
    _L0_attn_in = {k: v for k, v in _L0_attn_all.items() if k in ('in_proj_w', 'out_proj_w')}
    del _L0_attn_all

    def _L0_ffn_setup():
        import jax, jax.numpy as jnp
        import numpy as np
        B, S, D, H, E, K, F = (1, 256, 256, 16, 8, 2, 1024)

        def layernorm(x, g, b, eps=1e-05):
            m = x.mean(-1, keepdims=True)
            v = ((x - m) ** 2).mean(-1, keepdims=True)
            return (x - m) * jax.lax.rsqrt(v + eps) * g + b
        key = jax.random.key(seed)
        ks = jax.random.split(key, 8)
        n = lambda k, shape, sc: jax.random.normal(k, shape, dtype=jnp.float32) * sc
        return {'x': n(ks[0], (B, S, D), 1.0), 'w_qkv': n(ks[1], (D, 3 * D), D ** (-0.5)), 'w_o': n(ks[2], (D, D), D ** (-0.5)), 'g1': jnp.ones((D,), jnp.float32), 'b1': jnp.zeros((D,), jnp.float32), 'wg': n(ks[3], (D, E), D ** (-0.5)), 'w1': n(ks[4], (E, D, F), D ** (-0.5)), 'bb1': jnp.zeros((E, F), jnp.float32), 'w2': n(ks[5], (E, F, D), F ** (-0.5)), 'bb2': jnp.zeros((E, D), jnp.float32), 'g2': jnp.ones((D,), jnp.float32), 'b2': jnp.zeros((D,), jnp.float32)}
    _L0_ffn_all = _L0_ffn_setup()
    _L0_ffn_in = {k: v for k, v in _L0_ffn_all.items() if k in ('w_qkv', 'w_o', 'g1', 'b1', 'wg', 'w1', 'bb1', 'w2', 'bb2', 'g2', 'b2')}
    del _L0_ffn_all

    def _L1_xattn_setup():
        import jax, jax.numpy as jnp
        import numpy as np
        DIM = 256
        H = 16
        HD = DIM // H
        SCALE = HD ** (-0.5)
        LAMBDA_INIT = 0.1
        EPS = 1e-06

        def _split_heads(x, B, N):
            return x.reshape(B, N, H, HD).transpose(0, 2, 1, 3)
        key0 = jax.random.key(seed)
        ks = jax.random.split(key0, 12)
        B, Nq, Nk = (2, 256, 512)
        w = 0.02
        inp = {'query': jax.random.normal(ks[0], (B, Nq, DIM), jnp.float32), 'key': jax.random.normal(ks[1], (B, Nk, DIM), jnp.float32), 'value': jax.random.normal(ks[2], (B, Nk, DIM), jnp.float32), 'qpos': jax.random.randint(ks[3], (B, Nq), 0, Nq, jnp.int32), 'kpos': jax.random.randint(ks[4], (B, Nk), 0, Nk, jnp.int32), 'q1_w': jax.random.normal(ks[5], (DIM, DIM), jnp.float32) * w, 'q2_w': jax.random.normal(ks[6], (DIM, DIM), jnp.float32) * w, 'kv1_w': jax.random.normal(ks[7], (2 * DIM, DIM), jnp.float32) * w, 'kv2_w': jax.random.normal(ks[8], (2 * DIM, DIM), jnp.float32) * w, 'proj_w': jax.random.normal(ks[9], (DIM, DIM), jnp.float32) * w, 'proj_b': jnp.zeros((DIM,), jnp.float32), 'norm_w': jnp.ones((DIM,), jnp.float32), 'lambda_1': jnp.ones((1, H, 1, 1), jnp.float32), 'lambda_2': jnp.full((1, H, 1, 1), 1.0 - LAMBDA_INIT * (1.0 / 12.0), jnp.float32)}
        return inp
    _L1_xattn_all = _L1_xattn_setup()
    _L1_xattn_in = {k: v for k, v in _L1_xattn_all.items() if k in ('q1_w', 'q2_w', 'kv1_w', 'kv2_w', 'proj_w', 'proj_b', 'norm_w', 'lambda_1', 'lambda_2')}
    del _L1_xattn_all

    def _L1_attn_setup():
        import jax, jax.numpy as jnp
        import numpy as np
        from jax import lax
        D_MODEL = 256
        KERNEL = 5
        PAD = (KERNEL - 1) // 2
        key = jax.random.key(seed)
        k1, k2, k3, k4, k5 = jax.random.split(key, 5)
        B, T, D = (8, 1024, D_MODEL)
        x = jax.random.normal(k1, (B, T, D), dtype=jnp.float32)
        decay_logit = jnp.zeros((D,), dtype=jnp.float32)
        lim = 1.0 / np.sqrt(D)
        W = jax.random.uniform(k2, (D, D), minval=-lim, maxval=lim, dtype=jnp.float32)
        b = jax.random.uniform(k3, (D,), minval=-lim, maxval=lim, dtype=jnp.float32)
        limc = 1.0 / np.sqrt(KERNEL)
        conv_w = jax.random.uniform(k4, (D, 1, KERNEL), minval=-limc, maxval=limc, dtype=jnp.float32)
        conv_b = jax.random.uniform(k5, (D,), minval=-limc, maxval=limc, dtype=jnp.float32)
        return {'x': x, 'decay_logit': decay_logit, 'W': W, 'b': b, 'conv_w': conv_w, 'conv_b': conv_b}
    _L1_attn_all = _L1_attn_setup()
    _L1_attn_in = {k: v for k, v in _L1_attn_all.items() if k in ('decay_logit', 'W', 'b', 'conv_w', 'conv_b')}
    del _L1_attn_all

    def _L1_ffn_setup():
        import jax, jax.numpy as jnp
        import numpy as np
        DIM = 256
        DEPTH = 7
        PAR = 8
        N_NODES = 2 ** (DEPTH + 1) - 1
        WIDTH = PAR * N_NODES
        key = jax.random.key(seed)
        k1, k2, k3, k4 = jax.random.split(key, 4)
        init_k = float(np.sqrt(1.0 / DIM))
        init_k2 = float(np.sqrt(1.0 / ((DEPTH + 1) * PAR)))
        oldx = jax.random.normal(k1, (4, 512, DIM), dtype=jnp.float32)
        W_in = jax.random.uniform(k2, (WIDTH, DIM), jnp.float32, -init_k, init_k)
        b_in = jax.random.uniform(k3, (WIDTH,), jnp.float32, -init_k, init_k)
        W_out = jax.random.uniform(k4, (DIM, WIDTH), jnp.float32, -init_k2, init_k2)
        return {'oldx': oldx, 'W_in': W_in, 'b_in': b_in, 'W_out': W_out}
    _L1_ffn_all = _L1_ffn_setup()
    _L1_ffn_in = {k: v for k, v in _L1_ffn_all.items() if k in ('W_in', 'b_in', 'W_out')}
    del _L1_ffn_all
    return {'x': x, 'ctx_1024': ctx_1024, 'itok_BxS_0_1023': itok_BxS_0_1023, 'itok_BxS2_0_2047': itok_BxS2_0_2047, 'mask_1x1xSxS2_bk0': mask_1x1xSxS2_bk0, 'L0_xattn_Wq': _L0_xattn_in['Wq'], 'L0_xattn_bq': _L0_xattn_in['bq'], 'L0_xattn_Wk': _L0_xattn_in['Wk'], 'L0_xattn_bk': _L0_xattn_in['bk'], 'L0_xattn_Wv': _L0_xattn_in['Wv'], 'L0_xattn_bv': _L0_xattn_in['bv'], 'L0_xattn_Wo': _L0_xattn_in['Wo'], 'L0_xattn_bo': _L0_xattn_in['bo'], 'L0_attn_in_proj_w': _L0_attn_in['in_proj_w'], 'L0_attn_out_proj_w': _L0_attn_in['out_proj_w'], 'L0_ffn_w_qkv': _L0_ffn_in['w_qkv'], 'L0_ffn_w_o': _L0_ffn_in['w_o'], 'L0_ffn_g1': _L0_ffn_in['g1'], 'L0_ffn_b1': _L0_ffn_in['b1'], 'L0_ffn_wg': _L0_ffn_in['wg'], 'L0_ffn_w1': _L0_ffn_in['w1'], 'L0_ffn_bb1': _L0_ffn_in['bb1'], 'L0_ffn_w2': _L0_ffn_in['w2'], 'L0_ffn_bb2': _L0_ffn_in['bb2'], 'L0_ffn_g2': _L0_ffn_in['g2'], 'L0_ffn_b2': _L0_ffn_in['b2'], 'L1_xattn_q1_w': _L1_xattn_in['q1_w'], 'L1_xattn_q2_w': _L1_xattn_in['q2_w'], 'L1_xattn_kv1_w': _L1_xattn_in['kv1_w'], 'L1_xattn_kv2_w': _L1_xattn_in['kv2_w'], 'L1_xattn_proj_w': _L1_xattn_in['proj_w'], 'L1_xattn_proj_b': _L1_xattn_in['proj_b'], 'L1_xattn_norm_w': _L1_xattn_in['norm_w'], 'L1_xattn_lambda_1': _L1_xattn_in['lambda_1'], 'L1_xattn_lambda_2': _L1_xattn_in['lambda_2'], 'L1_attn_decay_logit': _L1_attn_in['decay_logit'], 'L1_attn_W': _L1_attn_in['W'], 'L1_attn_b': _L1_attn_in['b'], 'L1_attn_conv_w': _L1_attn_in['conv_w'], 'L1_attn_conv_b': _L1_attn_in['conv_b'], 'L1_ffn_W_in': _L1_ffn_in['W_in'], 'L1_ffn_b_in': _L1_ffn_in['b_in'], 'L1_ffn_W_out': _L1_ffn_in['W_out']}

def reference(x, ctx_1024, itok_BxS_0_1023, itok_BxS2_0_2047, mask_1x1xSxS2_bk0, L0_xattn_Wq, L0_xattn_bq, L0_xattn_Wk, L0_xattn_bk, L0_xattn_Wv, L0_xattn_bv, L0_xattn_Wo, L0_xattn_bo, L0_attn_in_proj_w, L0_attn_out_proj_w, L0_ffn_w_qkv, L0_ffn_w_o, L0_ffn_g1, L0_ffn_b1, L0_ffn_wg, L0_ffn_w1, L0_ffn_bb1, L0_ffn_w2, L0_ffn_bb2, L0_ffn_g2, L0_ffn_b2, L1_xattn_q1_w, L1_xattn_q2_w, L1_xattn_kv1_w, L1_xattn_kv2_w, L1_xattn_proj_w, L1_xattn_proj_b, L1_xattn_norm_w, L1_xattn_lambda_1, L1_xattn_lambda_2, L1_attn_decay_logit, L1_attn_W, L1_attn_b, L1_attn_conv_w, L1_attn_conv_b, L1_ffn_W_in, L1_ffn_b_in, L1_ffn_W_out):
    import jax
    import jax.numpy as jnp

    def _L0_xattn_ref(q, k, v, mask, Wq, bq, Wk, bk, Wv, bv, Wo, bo):
        import jax, jax.numpy as jnp
        import numpy as np
        D_MODEL = 256
        H = 16
        D_K = D_MODEL // H
        NEG = -1000000000.0

        def _split_heads(x):
            B, S, _ = x.shape
            return x.reshape(B, S, H, D_K).transpose(0, 2, 1, 3)
        query = _split_heads(q @ Wq.T + bq)
        key_ = _split_heads(k @ Wk.T + bk)
        value = _split_heads(v @ Wv.T + bv)
        scores = jnp.einsum('bhqd,bhkd->bhqk', query, key_) / jnp.sqrt(jnp.asarray(D_K, jnp.float32))
        scores = jnp.where(mask, scores, NEG)
        attn = jax.nn.softmax(scores, axis=-1)
        x = jnp.einsum('bhqk,bhkd->bhqd', attn, value)
        B, _, S, _ = x.shape
        x = x.transpose(0, 2, 1, 3).reshape(B, S, D_MODEL)
        return x @ Wo.T + bo

    def _L0_attn_ref(query, in_proj_w, out_proj_w):
        import jax, jax.numpy as jnp
        import numpy as np
        EMBED_DIM = 256
        NUM_HEADS = 16
        CONTEXT = 250
        MAX_PERIOD = 10000.0
        HEAD_DIM = EMBED_DIM // NUM_HEADS

        def _apply_rope(q, k):
            B, H, T, D = q.shape
            ds = jnp.arange(D // 2, dtype=jnp.float32)
            freqs = jnp.exp(ds * (-np.log(MAX_PERIOD) * 2.0 / D))
            ts = jnp.arange(T, dtype=jnp.float32)
            ang = ts[:, None] * freqs[None, :]
            cos = jnp.cos(ang)
            sin = jnp.sin(ang)

            def rot(x):
                xr = x.reshape(B, H, T, D // 2, 2)
                xa, xb = (xr[..., 0], xr[..., 1])
                ya = xa * cos - xb * sin
                yb = xa * sin + xb * cos
                return jnp.stack([ya, yb], axis=-1).reshape(B, H, T, D)
            return (rot(q), rot(k))
        B, T, E = query.shape
        H, D = (NUM_HEADS, HEAD_DIM)
        proj = query @ in_proj_w.T
        qkv = proj.reshape(B, T, 3, H, D)
        q = jnp.transpose(qkv[:, :, 0], (0, 2, 1, 3))
        k = jnp.transpose(qkv[:, :, 1], (0, 2, 1, 3))
        v = jnp.transpose(qkv[:, :, 2], (0, 2, 1, 3))
        q, k = _apply_rope(q, k)
        pos = jnp.arange(T)
        delta = pos[:, None] - pos[None, :]
        mask = (delta >= 0) & (delta < CONTEXT)
        scores = jnp.einsum('bhtd,bhsd->bhts', q, k) * D ** (-0.5)
        scores = jnp.where(mask[None, None, :, :], scores, jnp.finfo(scores.dtype).min)
        attn = jax.nn.softmax(scores, axis=-1)
        x = jnp.einsum('bhts,bhsd->bhtd', attn, v)
        x = jnp.transpose(x, (0, 2, 1, 3)).reshape(B, T, E)
        return x @ out_proj_w.T

    def _L0_ffn_ref(x, w_qkv, w_o, g1, b1, wg, w1, bb1, w2, bb2, g2, b2):
        import jax, jax.numpy as jnp
        import numpy as np
        B, S, D, H, E, K, F = (1, 256, 256, 16, 8, 2, 1024)

        def layernorm(x, g, b, eps=1e-05):
            m = x.mean(-1, keepdims=True)
            v = ((x - m) ** 2).mean(-1, keepdims=True)
            return (x - m) * jax.lax.rsqrt(v + eps) * g + b
        b, s, d = x.shape
        hd = d // H
        qkv = x @ w_qkv
        q, k, v = jnp.split(qkv, 3, axis=-1)
        to_heads = lambda t: t.reshape(b, s, H, hd).transpose(0, 2, 1, 3)
        q, k, v = (to_heads(q), to_heads(k), to_heads(v))
        scores = jnp.einsum('bhqd,bhkd->bhqk', q, k) / jnp.sqrt(jnp.float32(hd))
        causal = jnp.tril(jnp.ones((s, s), bool))
        scores = jnp.where(causal, scores, jnp.finfo(scores.dtype).min)
        attn = jax.nn.softmax(scores, axis=-1)
        o = jnp.einsum('bhqk,bhkd->bhqd', attn, v)
        o = o.transpose(0, 2, 1, 3).reshape(b, s, d) @ w_o
        h = layernorm(x + o, g1, b1)
        probs = jax.nn.softmax(h @ wg, axis=-1)
        topv, topi = jax.lax.top_k(probs, K)
        topv = topv / topv.sum(-1, keepdims=True)
        w = (topv[..., None] * jax.nn.one_hot(topi, E, dtype=h.dtype)).sum(-2)
        h1 = jax.nn.gelu(jnp.einsum('bsd,edf->ebsf', h, w1) + bb1[:, None, None, :])
        y = jnp.einsum('ebsf,efd->ebsd', h1, w2) + bb2[:, None, None, :]
        moe = jnp.einsum('ebsd,bse->bsd', y, w)
        return layernorm(h + moe, g2, b2)

    def _L1_xattn_ref(query, key, value, qpos, kpos, q1_w, q2_w, kv1_w, kv2_w, proj_w, proj_b, norm_w, lambda_1, lambda_2):
        import jax, jax.numpy as jnp
        import numpy as np
        DIM = 256
        H = 16
        HD = DIM // H
        SCALE = HD ** (-0.5)
        LAMBDA_INIT = 0.1
        EPS = 1e-06

        def _split_heads(x, B, N):
            return x.reshape(B, N, H, HD).transpose(0, 2, 1, 3)
        B, Nq, C = query.shape
        Nk = key.shape[1]
        q1 = _split_heads(query @ q1_w.T, B, Nq)
        q2 = _split_heads(query @ q2_w.T, B, Nq)
        kv1 = (key @ kv1_w.T).reshape(B, Nk, 2, H, HD).transpose(2, 0, 3, 1, 4)
        k1, v1 = (kv1[0], kv1[1])
        kv2 = (key @ kv2_w.T).reshape(B, Nk, 2, H, HD).transpose(2, 0, 3, 1, 4)
        k2 = kv2[0]
        attn1 = jax.nn.softmax(jnp.einsum('bhqd,bhkd->bhqk', q1, k1) * SCALE, axis=-1)
        attn2 = jax.nn.softmax(jnp.einsum('bhqd,bhkd->bhqk', q2, k2) * SCALE, axis=-1)
        lambda_full = lambda_1 - lambda_2 + LAMBDA_INIT
        diff_attn = attn1 - lambda_full * attn2
        x = jnp.einsum('bhqk,bhkd->bhqd', diff_attn, v1)
        x = x.transpose(0, 2, 1, 3).reshape(B, Nq, C)
        xf = x.astype(jnp.float32)
        xf = xf * jax.lax.rsqrt(jnp.mean(xf * xf, axis=-1, keepdims=True) + EPS) * norm_w
        x = xf.astype(x.dtype)
        return x @ proj_w.T + proj_b

    def _L1_attn_ref(x, decay_logit, W, b, conv_w, conv_b):
        import jax, jax.numpy as jnp
        import numpy as np
        from jax import lax
        D_MODEL = 256
        KERNEL = 5
        PAD = (KERNEL - 1) // 2
        B, T, D = x.shape
        a = jax.nn.sigmoid(decay_logit)

        def step(s, xt):
            s = a * s + (1.0 - a) * xt
            return (s, s)
        s0 = jnp.zeros((B, D), dtype=x.dtype)
        _, S = lax.scan(step, s0, jnp.swapaxes(x, 0, 1))
        y_ret = jnp.einsum('tbd,ed->tbe', S, W) + b
        y_ret = jnp.swapaxes(y_ret, 0, 1)
        xc = jnp.swapaxes(x, 1, 2)
        y_loc = lax.conv_general_dilated(xc, conv_w, window_strides=(1,), padding=[(PAD, PAD)], feature_group_count=D)
        y_loc = y_loc + conv_b[None, :, None]
        y_loc = jnp.swapaxes(y_loc, 1, 2)
        return y_ret + y_loc

    def _L1_ffn_ref(oldx, W_in, b_in, W_out):
        import jax, jax.numpy as jnp
        import numpy as np
        DIM = 256
        DEPTH = 7
        PAR = 8
        N_NODES = 2 ** (DEPTH + 1) - 1
        WIDTH = PAR * N_NODES
        x = oldx.reshape(-1, DIM)
        B = x.shape[0]
        logits = x @ W_in.T + b_in
        decisions = (logits > 0).astype(jnp.int32).reshape(B, PAR, N_NODES)
        acts = jax.nn.silu(logits).reshape(B, PAR, N_NODES)
        current = jnp.zeros((B, PAR), dtype=jnp.int32)
        dmap = jax.nn.one_hot(current, N_NODES, dtype=acts.dtype)
        for d in range(DEPTH):
            cur_platform = 2 ** d - 1
            next_platform = 2 ** (d + 1) - 1
            moves = jnp.take_along_axis(decisions, current[..., None], axis=2)[..., 0]
            current = (current - cur_platform) * 2 + moves + next_platform
            dmap = dmap + jax.nn.one_hot(current, N_NODES, dtype=acts.dtype)
        masked = acts * jax.lax.stop_gradient(dmap)
        out = masked.reshape(B, WIDTH) @ W_out.T
        return out.reshape(oldx.shape)
    x = x + _L0_xattn_ref(_layernorm(x, axis=-1), ctx_1024, ctx_1024, mask_1x1xSxS2_bk0, L0_xattn_Wq, L0_xattn_bq, L0_xattn_Wk, L0_xattn_bk, L0_xattn_Wv, L0_xattn_bv, L0_xattn_Wo, L0_xattn_bo)
    x = x + _L0_attn_ref(_layernorm(x, axis=-1), L0_attn_in_proj_w, L0_attn_out_proj_w)
    x = x + _L0_ffn_ref(_layernorm(x, axis=-1), L0_ffn_w_qkv, L0_ffn_w_o, L0_ffn_g1, L0_ffn_b1, L0_ffn_wg, L0_ffn_w1, L0_ffn_bb1, L0_ffn_w2, L0_ffn_bb2, L0_ffn_g2, L0_ffn_b2)
    x = x + _L1_xattn_ref(_layernorm(x, axis=-1), ctx_1024, ctx_1024, itok_BxS_0_1023, itok_BxS2_0_2047, L1_xattn_q1_w, L1_xattn_q2_w, L1_xattn_kv1_w, L1_xattn_kv2_w, L1_xattn_proj_w, L1_xattn_proj_b, L1_xattn_norm_w, L1_xattn_lambda_1, L1_xattn_lambda_2)
    x = x + _L1_attn_ref(_layernorm(x, axis=-1), L1_attn_decay_logit, L1_attn_W, L1_attn_b, L1_attn_conv_w, L1_attn_conv_b)
    x = x + _L1_ffn_ref(_layernorm(x, axis=-1), L1_ffn_W_in, L1_ffn_b_in, L1_ffn_W_out)
    return x

_drawn_inputs = setup_inputs


def setup_inputs(seed=0):
    import zlib

    import numpy as np

    out = dict(_drawn_inputs(seed))
    spreads = {'L0_ffn_g1': (1.0, 0.2),
     'L0_ffn_b1': (0.0, 0.1),
     'L0_ffn_bb1': (0.0, 0.288),
     'L0_ffn_bb2': (0.0, 0.1),
     'L0_ffn_g2': (1.0, 0.2),
     'L0_ffn_b2': (0.0, 0.1),
     'L1_xattn_proj_b': (0.0, 0.1),
     'L1_xattn_norm_w': (1.0, 0.2),
     'L1_xattn_lambda_1': (1.0, 0.2),
     'L1_xattn_lambda_2': (0.9916666746139526, 0.2),
     'L1_attn_decay_logit': (0.0, 0.8)}
    factors = {'L0_xattn_bk': 64.0,
     'L1_xattn_q1_w': 5.156,
     'L1_xattn_q2_w': 8.0,
     'L1_xattn_kv2_w': 8.0,
     'L1_attn_b': 2.672}
    for name, (base, spread) in spreads.items():
        noise = np.random.default_rng([zlib.crc32(name.encode()), seed]).standard_normal(out[name].shape)
        drawn = base * np.exp(spread * noise) if base else spread * noise
        out[name] = jnp.asarray(drawn.astype(out[name].dtype))
    for name, factor in factors.items():
        out[name] = (out[name] * factor).astype(out[name].dtype)
    return out
```

```python
from contextlib import ExitStack

import numpy as np

import concourse.bass as bass
from concourse import mybir

F32 = mybir.dt.float32
U8 = mybir.dt.uint8
ALU = mybir.AluOpType
ACT = mybir.ActivationFunctionType
X_AXIS = mybir.AxisListType.X

P = 128
B, S, D = 16, 64, 256
SK = 256
N = B * S
H, HD = 16, 16
C = D // P
TILES = N // P
HG = H // C
PAIRS = HG // 2
E, F = 8, 1024
M = F // P
TREES, NODES, DEPTH = 8, 255, 7
WIDTH = TREES * NODES
NB = (WIDTH + P - 1) // P
TAPS = 5
SCALE = float(HD) ** -0.5
MASKED = -1.0e30
BANK = 512


VEC = {}
_at = 0
for _name, _n in (("bq", C), ("bk", C), ("bv", C), ("decay", C), ("ret_b", C), ("conv_b", C), ("conv_w", C * TAPS),
                  ("lam1", 2 * PAIRS), ("lam2", 2 * PAIRS), ("norm_w", C), ("bb1", E * M)):
    VEC[_name] = (_at, _at + _n)
    _at += _n
NVEC = _at
CON = {}
_at = 0
for _name, _n in (("ident", P), ("head", HG), ("even", 1), ("odd", 1), ("causal", S), ("cos", S), ("sin", S),
                  ("ones", 1), ("batch", 2), ("before", E * E)):
    CON[_name] = (_at, _at + _n)
    _at += _n
NCON = _at
ROWS = ["xattn_bo", "ffn_g1", "ffn_b1", "ffn_g2", "ffn_b2", "proj_b"]


def wge(eng, sem, value):
    if not isinstance(value, int) or value > 0:
        eng.wait_ge(sem, value)


def run_pipelined(eng, body, n, chain=None):
    base = chain.at if chain else 0
    body(0)
    per = chain.at - base if chain else 0
    if n > 2:
        with eng.Fori(1, n - 1) as i:
            if chain:
                chain.at = i * per + base
            body(i)
        if chain:
            assert isinstance(base, int)
            chain.at = base + (n - 1) * per
    body(n - 1)


class Chain:

    def __init__(self, eng, sem):
        self.eng, self.sem, self.at = eng, sem, 0

    def link(self, ins):
        ins.then_inc(self.sem, 1)
        self.at = self.at + 1
        self.eng.wait_ge(self.sem, self.at)


class Ring:

    def __init__(self, filled, drained, banks):
        self.filled, self.drained, self.banks = filled, drained, banks
        self.fills = self.drains = 0

    def to_fill(self, pe):
        wge(pe, self.drained, self.fills - len(self.banks) + 1)
        self.fills += 1
        return self.banks[(self.fills - 1) % len(self.banks)]

    def to_drain(self, eng):
        self.drains += 1
        eng.wait_ge(self.filled, self.drains)
        return self.banks[(self.drains - 1) % len(self.banks)]


def build(nc, a, out):
    ctx = ExitStack()
    with ctx:
        def sb(name, shape, dt=F32):
            return ctx.enter_context(nc.sbuf_tensor(name, shape, dt))

        def sem(name):
            return ctx.enter_context(nc.semaphore(name))

        X = sb("X", [P, TILES, D])
        XN = sb("XN", [P, TILES, D])
        XT = sb("XT", [P, C, N])
        QT = sb("QT", [P, C, N])
        KT = sb("KT", [P, C, N])
        AT = sb("AT", [P, C, N])
        weights = sb("weights", [P, 2, 6, C, D])
        wgate = sb("wgate", [P, C, E])
        ctxs = sb("ctxs", [P, 2, C, SK])
        kts = sb("kts", [P, 2, 2, C, SK])
        VT = kts[:].rearrange("p s m c n -> p (s m c n)").rearrange("p (t d) -> p t d", t=TILES)
        vs = sb("vs", [P, 2, 2, D])
        qm = sb("qm", [P, 2, 2, C, HG, S])
        sm = sb("sm", [P, 2, BANK])
        p1 = sb("p1", [P, 2, BANK])
        p2 = sb("p2", [P, 2, BANK])
        pts = sb("pts", [P, 2, BANK])
        stat = sb("stat", [P, TILES, 6])
        mv = sb("mv", [P, TILES, 2])
        rstd = sb("rstd", [P, TILES])
        std = sb("std", [P, TILES])
        mx = sb("mx", [P, 4, 8])
        rs = sb("rs", [P, 4, 8])
        ri = sb("ri", [P, 2, 8])
        tmp = sb("tmp", [P, 2, S])
        vec = sb("vec", [P, NVEC])
        con = sb("con", [P, NCON])
        sel = sb("sel", [E, E, P])
        rows = sb("rows", [P, len(ROWS), D])
        bb2 = sb("bb2", [E, C, P])
        maskb = sb("maskb", [P, SK], U8)
        bias_x = sb("bias_x", [P, SK])
        lam = sb("lam", [P, 2 * PAIRS])
        big_a = sb("big_a", [P, 8192])
        big_b = sb("big_b", [P, 8192])
        w1s = big_a[:, 0:4096].rearrange("p (s c f) -> p s c f", s=2, c=C)
        w2s = big_a[:, 4096:8192].rearrange("p (s m d) -> p s m d", s=2, m=M)
        gates = big_b[:, :].rearrange("p (e n) -> p e n", e=E)
        ps = ctx.enter_context(nc.psum_tensor("ps", [P, 8, BANK], F32))

        def v(name):
            lo, hi = VEC[name]
            return vec[:, lo:hi]

        def k(name):
            lo, hi = CON[name]
            return con[:, lo:hi]

        ident = k("ident")

        s_in = {n: sem("in_" + n) for n in ("x", "con", "vec", "rows", "mask", "sel", "bb2", "wg")}
        s_w = [sem(f"weights_in_{i}") for i in range(2)]
        s_tree_w = sem("tree_weights_in")
        s_out = sem("out_stored")
        s_dve = sem("vector_step")
        s_act = sem("scalar_step")
        s_pool = sem("gpsimd_step")
        s_var = sem("variance_ready")
        s_std = sem("deviation_ready")
        s_xn = sem("normalised_tile")
        s_xt = sem("transposed_block_in_sbuf")
        s_fa, s_da = sem("bank_filled_for_scalar"), sem("bank_drained_by_scalar")
        s_fd, s_dd = sem("bank_filled_for_vector"), sem("bank_drained_by_vector")
        s_resid = sem("bias_added_to_residual")
        s_w_free = sem("stage_weights_free")
        ringA = Ring(s_fa, s_da, [0, 1, 2, 3])
        ringD = Ring(s_fd, s_dd, [4, 5, 6, 7])

        names = ["l0x", "l0a", "l0f", "l1x"]
        st = {}
        for n in names:
            st[n] = {m: sem(f"{n}_{m}") for m in (
                "qk_ready", "qm_ready", "s_done", "mx_ready", "exp_done", "p_ready", "pt_filled", "pt_drained",
                "pv_done", "o_drained", "kv_filled", "kv_drained", "ctx0", "ctx1", "v_ready", "s_read")}
        s_router = sem("router_ready")
        s_gw = sem("gate_weights_ready")
        s_gwT = sem("gate_weights_transposed")
        s_gb = sem("gates_broadcast")
        s_e_in = [sem(f"expert_in_{i}") for i in range(2)]
        s_hid = sem("hidden_filled")
        s_gelu = sem("gelu_done")
        s_h1 = sem("hidden_gated")
        s_y = sem("expert_block_done")
        s_bb1 = sem("hidden_biases_ready")
        s_acc = sem("moe_sum_in_sbuf")
        s_ret = sem("retention_ready")
        s_sq = sem("squares_ready")
        s_norm = sem("rms_ready")
        s_projw = sem("scaled_projection_ready")
        s_xslot = sem("tile_copied")
        s_logit = sem("logits_filled")
        s_lread = sem("logits_read")
        s_act_in = sem("tree_logits_ready")
        s_silu = sem("silu_done")
        s_path = sem("path_masked")
        s_tt = sem("tree_block_transposed")
        s_tc = sem("tree_block_in_sbuf")
        s_ty = sem("tree_out_filled")
        s_tx = sem("tree_out_added")

        W = {"l0x": weights[:, 0], "l0a": weights[:, 1], "l0f": weights[:, 0], "l1x": weights[:, 1], "l1a": weights[:, 0]}
        WSLOT = {"l0x": (0, 16), "l0a": (1, 16), "l0f": (0, 32), "l1x": (1, 32), "l1a": (0, 48)}

        win = big_a[:, 0:C * WIDTH].rearrange("p (c w) -> p c w", c=C)
        wout = big_a[:, 4096:8192].rearrange("p (j d) -> p j d", j=NB)
        qm_flat = qm[:].rearrange("p a b c h s -> p (a b c h s)")
        bin_b = qm_flat[:, 0:WIDTH]
        mT = qm_flat[:, 2048:4096].rearrange("p (j t) -> p j t", j=NB)
        logit, dec, path, acts = (big_b[:, 2048 * i:2048 * i + WIDTH] for i in range(4))
        xslot = ctxs[:, 0].rearrange("p c n -> p (c n)")[:, 0:2 * P].rearrange("p (c n) -> p c n", c=C)

        gw = sb("gw", [P, TILES, E])
        gwT = qm_flat[0:E, 0:N]
        hg = p2[:, 0:2, :]
        gact = p1[:, 0:2, :]
        router = sb("router", [P, 4, TILES, E])
        rk = sm
        bb1s = sb("bb1s", [P, 2 * M])
        dk = sb("dk", [P, 8])

        block = ctx.enter_context(nc.Block())

        @block.sync
        def _(sp):
            sp.dma_start(con[:], a["con"]).then_inc(s_in["con"], 16)
            sp.dma_start(X[:], a["x"].rearrange("b s d -> (b s) d").rearrange("(t p) d -> p t d", p=P)).then_inc(s_in["x"], 16)
            sp.dma_start(W["l0x"][:, 0:4], a["w_l0x"].rearrange("p (w c d) -> p w c d", w=4, c=C)).then_inc(s_w[0], 16)
            sp.dma_start(vec[:], a["vec"]).then_inc(s_in["vec"], 16)
            sp.dma_start(maskb[:], a["mask"]).then_inc(s_in["mask"], 16)

            def load_ctx(s, b, sl):
                dst = ctxs[:, sl]
                src = a["ctxT"][b] if isinstance(b, int) else a["ctxT"][bass.ds(b, 1)].rearrange("o p n -> (o p) n")
                sp.dma_start(dst, src.rearrange("p (c n) -> p c n", c=C)).then_inc(s[f"ctx{sl}"], 16)

            def ctx_loop(s, fills):
                load_ctx(s, 0, 0)
                load_ctx(s, 1, 1)

                def body(i):
                    for sl in range(2):
                        sp.wait_ge(s["kv_filled"], i * (2 * fills) + fills * (sl + 1))
                        load_ctx(s, i * 2 + 2 + sl, sl)
                with sp.Fori(0, B // 2 - 1) as i:
                    body(i)

            load_ctx_first = st["l0x"]
            sp.dma_start(rows[:], a["rows"].partition_broadcast(P).rearrange("p (r d) -> p r d", d=D)).then_inc(s_in["rows"], 16)
            sp.dma_start(W["l0a"][:, 0:6], a["w_l0a"].rearrange("p (w c d) -> p w c d", w=6, c=C)).then_inc(s_w[1], 16)
            ctx_loop(load_ctx_first, 2)
            for n, key, dst in (("sel", "sel", sel[:].rearrange("k e p -> k (e p)")), ("bb2", "bb2", bb2[:].rearrange("e c p -> e (c p)")),
                                ("wg", "wg", wgate[:].rearrange("p c e -> p (c e)"))):
                sp.dma_start(dst, a[key]).then_inc(s_in[n], 16)

            def load_expert(e, sl):
                for dst, key in ((w1s[:, sl].rearrange("p c f -> p (c f)"), "w1"), (w2s[:, sl].rearrange("p m d -> p (m d)"), "w2")):
                    src = a[key][e] if isinstance(e, int) else a[key][bass.ds(e, 1)].rearrange("o p n -> (o p) n")
                    sp.dma_start(dst, src).then_inc(s_e_in[sl], 16)

            load_expert(0, 0)
            load_expert(1, 1)
            sp.wait_ge(s_w_free, 1)
            sp.dma_start(W["l0f"][:, 0:4], a["w_l0f"].rearrange("p (w c d) -> p w c d", w=4, c=C)).then_inc(s_w[0], 16)
            sp.wait_ge(s_w_free, 2)
            sp.dma_start(W["l1x"][:, 0:6], a["w_l1x"].rearrange("p (w c d) -> p w c d", w=6, c=C)).then_inc(s_w[1], 16)
            sp.wait_ge(s_w_free, 3)
            sp.dma_start(W["l1a"][:, 0], a["w_l1a"].rearrange("p (c d) -> p c d", c=C)).then_inc(s_w[0], 16)
            with sp.Fori(0, E // 2 - 1) as i:
                for sl in range(2):
                    sp.wait_ge(s_y, i * (4 * M) + 2 * M * (sl + 1))
                    load_expert(i * 2 + 2 + sl, sl)
            ctx_loop(st["l1x"], 3)
            sp.wait_ge(s_y, E * 2 * M)
            sp.dma_start(win[:], a["w_in"].rearrange("p (c w) -> p c w", c=C)).then_inc(s_tree_w, 16)
            sp.dma_start(wout[:], a["w_out"].rearrange("p (j d) -> p j d", j=NB)).then_inc(s_tree_w, 16)
            sp.wait_ge(st["l1x"]["s_done"], B * 4)
            sp.dma_start(bin_b, a["b_in"].partition_broadcast(P)).then_inc(s_tree_w, 16)
            sp.wait_ge(s_tx, TILES)
            sp.dma_start(out.rearrange("b s d -> (b s) d").rearrange("(t p) d -> p t d", p=P), X[:]).then_inc(s_out, 16)
            sp.wait_ge(s_out, 16)

        @block.tensor
        def _(pe):
            ln = [0]

            def transpose_tokens():
                for t in range(TILES):
                    pe.wait_ge(s_xn, ln[0] * TILES + t + 1)
                    if t % 2 == 0:
                        bank = ringA.to_fill(pe)
                    for c in range(C):
                        i = pe.transpose(ps[:, bank, (t % 2 * C + c) * P:(t % 2 * C + c + 1) * P], XN[:, t, c * P:(c + 1) * P], ident)
                    if t % 2:
                        i.then_inc(s_fa, 1)
                ln[0] += 1
                pe.wait_ge(s_xt, ln[0] * TILES // 2)

            def project_features(w, ring, src=XT):
                for o in range(C):
                    for h in range(2):
                        bank = ring.to_fill(pe)
                        for c in range(C):
                            i = pe.matmul(ps[:, bank, :], w[:, c, o * P:(o + 1) * P], src[:, c, h * BANK:(h + 1) * BANK],
                                          start=(c == 0), stop=(c == C - 1))
                        i.then_inc(ring.filled, 1)

            def project_tokens(w, ring, src, free=None):
                for t in range(TILES):
                    if t % 2 == 0:
                        bank = ring.to_fill(pe)
                    for c in range(C):
                        i = pe.matmul(ps[:, bank, t % 2 * D:(t % 2 + 1) * D], src[:, c, t * P:(t + 1) * P], w[:, c, :],
                                      start=(c == 0), stop=(c == C - 1))
                    if t % 2:
                        i.then_inc(ring.filled, 1)
                if free:
                    pe.wait_ge(ring.filled, ring.fills)
                    pe.sem_inc(free, 1)

            def cross(s, maps, wk, lag_ring):
                items = [wk[0], "v"] + wk[1:]
                fills = len(items)

                def kv(b, sl):
                    pe.wait_ge(s[f"ctx{sl}"], (b // 2 + 1) * 16 if isinstance(b, int) else b)
                    return None

                def project_kv(i, sl_b):
                    sl = sl_b % 2
                    pe.wait_ge(s[f"ctx{sl}"], (i + sl_b // 2) * 16 + 16)
                    for n, w in enumerate(items):
                        wge(pe, s["kv_drained"], (i * 2 + sl_b) * fills + n)
                        if w == "v":
                            for half in range(2):
                                for c in range(C):
                                    m = pe.matmul(ps[:, 7, half * D:(half + 1) * D], ctxs[:, sl, c, half * P:(half + 1) * P],
                                                  wv[:, c, :], start=(c == 0), stop=(c == C - 1))
                        else:
                            for o in range(C):
                                for c in range(C):
                                    m = pe.matmul(ps[:, 7, o * SK:(o + 1) * SK], w[:, c, o * P:(o + 1) * P], ctxs[:, sl, c, :],
                                                  start=(c == 0), stop=(c == C - 1))
                        m.then_inc(s["kv_filled"], 1)

                wv = s["wv"]

                def scores(i, u):
                    U, sl, g, hp = i * 8 + u, u // 4 % 2, u // 2 % 2, u % 2
                    pe.wait_ge(s["qm_ready"], i * 4 + u // 2 + 1)
                    pe.wait_ge(s["kv_drained"], (i * 2 + u // 4) * fills + (1 if maps == 1 else fills))
                    wge(pe, s["s_read"] if maps == 1 else s["exp_done"], U - lag_ring + 1)
                    for mp in range(maps):
                        bank = (u % lag_ring) * maps + mp
                        for j in range(2):
                            pr = hp * 2 + j
                            lhs = qm[:, sl, mp, g, 2 * pr:2 * pr + 2, :].rearrange("p h s -> p (h s)")
                            m = pe.matmul(ps[:, bank, j * SK:(j + 1) * SK], lhs, kts[:, sl, mp, g, :], start=True, stop=True)
                    m.then_inc(s["s_done"], 1)

                def transposes(i, u):
                    U = i * 8 + u
                    pe.wait_ge(s["p_ready"], U + 1)
                    wge(pe, s["pt_drained"], U - 1)
                    for j in range(2):
                        for half in range(2):
                            m = pe.transpose(ps[:, 4 + u % 2, (j * 2 + half) * P:(j * 2 + half + 1) * P],
                                             p1[:, u % 8 % 2, j * SK + half * P:j * SK + (half + 1) * P], ident)
                    m.then_inc(s["pt_filled"], 1)

                def values(i, u):
                    U, sl, g, hp = i * 8 + u, u // 4 % 2, u // 2 % 2, u % 2
                    pe.wait_ge(s["pt_drained"], U + 1)
                    pe.wait_ge(s["kv_drained"], (i * 2 + u // 4) * fills + 2)
                    if hp == 0:
                        wge(pe, s["o_drained"], i * 4 + u // 2)
                    for j in range(2):
                        pr = hp * 2 + j
                        for half in range(2):
                            m = pe.matmul(ps[32 * pr:32 * pr + 32, 6, 0:P], vs[:, sl, half, g * P + 32 * pr:g * P + 32 * pr + 32],
                                          pts[:, u % 2, (j * 2 + half) * P:(j * 2 + half + 1) * P],
                                          start=(half == 0), stop=(half == 1), tile_position=(0, 32 * pr))
                    m.then_inc(s["pv_done"], 1)

                project_kv(0, 0)
                for u in range(3):
                    scores(0, u)
                transposes(0, 0)

                def body(i):
                    last = isinstance(i, int) and i == B // 2 - 1
                    for u in range(8):
                        if u % 4 == 0 and not (last and u == 4):
                            project_kv(i, u // 4 + 1)
                        if not (last and u + 3 >= 8):
                            scores(i, u + 3)
                        if not (last and u + 1 >= 8):
                            transposes(i, u + 1)
                        values(i, u)
                run_pipelined(pe, body, B // 2)

            def self_attention(s):
                def scores(i, u):
                    U, g, sl = i * 4 + u, u % 2, u % 2
                    pe.wait_ge(s["qm_ready"], U + 1)
                    wge(pe, s["s_read"], U - 3)
                    for b in range(2):
                        for pr in range(PAIRS):
                            lhs = qm[:, sl, b, 0, 2 * pr:2 * pr + 2, :].rearrange("p h s -> p (h s)")
                            m = pe.matmul(ps[:, u % 4, (pr * 2 + b) * S:(pr * 2 + b + 1) * S], lhs,
                                          KT[:, g, bass.ds((i * 2 + u // 2) * P + b * S, S)], start=True, stop=True)
                    m.then_inc(s["s_done"], 1)

                def transposes(i, u):
                    U = i * 4 + u
                    pe.wait_ge(s["p_ready"], U + 1)
                    wge(pe, s["pt_drained"], U - 1)
                    for pr in range(PAIRS):
                        m = pe.transpose(ps[:, 4 + u % 2, pr * P:(pr + 1) * P], p1[:, u % 2, pr * P:(pr + 1) * P], ident)
                    m.then_inc(s["pt_filled"], 1)

                def values(i, u):
                    U, g = i * 4 + u, u % 2
                    pe.wait_ge(s["pt_drained"], U + 1)
                    pe.wait_ge(s["v_ready"], i * 2 + u // 2 + 1)
                    wge(pe, s["o_drained"], U)
                    for pr in range(PAIRS):
                        for b in range(2):
                            m = pe.matmul(ps[32 * pr:32 * pr + 32, 6 + b, 0:P],
                                          vs[:, u // 2 % 2, b, g * P + 32 * pr:g * P + 32 * pr + 32],
                                          pts[:, u % 2, pr * P:(pr + 1) * P], start=True, stop=True,
                                          tile_position=(0, 32 * pr))
                    m.then_inc(s["pv_done"], 1)

                for u in range(3):
                    scores(0, u)
                transposes(0, 0)
                n = TILES // 2

                def body(i):
                    last = isinstance(i, int) and i == n - 1
                    for u in range(4):
                        if not (last and u + 3 >= 4):
                            scores(i, u + 3)
                        if not (last and u + 1 >= 4):
                            transposes(i, u + 1)
                        values(i, u)
                run_pipelined(pe, body, n)

            def wait_weights(n):
                pe.wait_ge(s_w[WSLOT[n][0]], WSLOT[n][1])

            pe.wait_ge(s_in["con"], 16)
            transpose_tokens()
            wait_weights("l0x")
            w = W["l0x"]
            project_features(w[:, 0], ringA)
            s = st["l0x"]
            s["wv"] = w[:, 2]
            pe.wait_ge(s["qk_ready"], 4)
            cross(s, 1, [w[:, 1]], 4)
            pe.wait_ge(s["o_drained"], B * C)
            project_tokens(w[:, 3], ringD, AT, s_w_free)

            transpose_tokens()
            wait_weights("l0a")
            w = W["l0a"]
            for o in range(C):
                for h in range(2):
                    for n in (0, 3, 1, 4):
                        bank = ringD.to_fill(pe)
                        for c in range(C):
                            i = pe.matmul(ps[:, bank, :], w[:, n, c, o * P:(o + 1) * P], XT[:, c, h * BANK:(h + 1) * BANK],
                                          start=(c == 0), stop=(c == C - 1))
                        i.then_inc(s_fd, 1)
            project_tokens(w[:, 2], ringA, XT)
            s = st["l0a"]
            pe.wait_ge(s["qk_ready"], 1)
            pe.wait_ge(s["kv_drained"], 4)
            self_attention(s)
            pe.wait_ge(s["o_drained"], TILES * C)
            project_tokens(w[:, 5], ringD, AT, s_w_free)

            transpose_tokens()
            wait_weights("l0f")
            w = W["l0f"]
            project_features(w[:, 0], ringA)
            project_features(w[:, 1], ringA)
            project_tokens(w[:, 2], ringA, XT)
            s = st["l0f"]
            pe.wait_ge(s["qk_ready"], 8)
            pe.wait_ge(s["kv_drained"], 4)
            self_attention(s)
            pe.wait_ge(s["o_drained"], TILES * C)
            project_tokens(w[:, 3], ringD, AT, s_w_free)
            transpose_tokens()
            bank = ringD.to_fill(pe)
            pe.wait_ge(s_in["wg"], 16)
            for t in range(TILES):
                for c in range(C):
                    i = pe.matmul(ps[:, bank, t * E:(t + 1) * E], XT[:, c, t * P:(t + 1) * P], wgate[:, c, :],
                                  start=(c == 0), stop=(c == C - 1))
            i.then_inc(s_fd, 1)
            pe.wait_ge(s_gw, 1)
            for h in range(2):
                bank = ringA.to_fill(pe)
                for t in range(4):
                    i = pe.transpose(ps[0:E, bank, t * P:(t + 1) * P], gw[:, h * 4 + t, :], ident)
                i.then_inc(s_fa, 1)
            pe.wait_ge(s_gwT, 2)
            pe.wait_ge(s_in["sel"], 16)
            pe.wait_ge(s_in["bb2"], 16)
            for e in range(E):
                for h in range(2):
                    bank = ringD.to_fill(pe) if h else ringA.to_fill(pe)
                    pe.matmul(ps[:, bank, :], sel[:, e, :], gwT[:, h * BANK:(h + 1) * BANK], start=True, stop=True)\
                        .then_inc(s_fd if h else s_fa, 1)
            pe.wait_ge(s_gb, 2 * E)
            for h in range(2):
                for o in range(C):
                    pe.matmul(ps[:, h * C + o, :], bb2[:, o, :], gwT[:, h * BANK:(h + 1) * BANK], start=True, stop=False)

            def hidden(i, u):
                sl, h, m = u // (2 * M) % 2, u // M % 2, u % M
                if u % (2 * M) == 0:
                    pe.wait_ge(s_e_in[sl], (i + u // (4 * M)) * 32 + 32)
                wge(pe, s_gelu, i * (4 * M) + u - 3)
                for c in range(C):
                    x = pe.matmul(ps[:, 4 + u % 4, :], w1s[:, sl, c, m * P:(m + 1) * P], XT[:, c, h * BANK:(h + 1) * BANK],
                                  start=(c == 0), stop=(c == C - 1))
                x.then_inc(s_hid, 1)

            def expert_out(i, u):
                sl, h, m = u // (2 * M) % 2, u // M % 2, u % M
                pe.wait_ge(s_h1, i * (4 * M) + u + 1)
                last = isinstance(i, int) and i == E // 2 - 1 and u // (2 * M) == 1 and m == M - 1
                for o in range(C):
                    x = pe.matmul(ps[:, h * C + o, :], w2s[:, sl, m, o * P:(o + 1) * P], hg[:, u % 2, :], start=False, stop=last)
                x.then_inc(s_y, 1)

            def experts(i):
                last = isinstance(i, int) and i == E // 2 - 1
                for u in range(4 * M):
                    if not (last and u + 2 >= 4 * M):
                        hidden(i, u + 2)
                    expert_out(i, u)
            hidden(0, 0)
            hidden(0, 1)
            run_pipelined(pe, experts, E // 2)
            pe.wait_ge(s_acc, 4)
            for t in range(TILES):
                if t % 2 == 0:
                    bank = ringD.to_fill(pe)
                for c in range(C):
                    i = pe.transpose(ps[:, bank, (t % 2 * C + c) * P:(t % 2 * C + c + 1) * P], QT[:, c, t * P:(t + 1) * P], ident)
                if t % 2:
                    i.then_inc(s_fd, 1)

            transpose_tokens()
            wait_weights("l1x")
            w = W["l1x"]
            project_features(w[:, 0], ringA)
            project_features(w[:, 1], ringA)
            s = st["l1x"]
            s["wv"] = w[:, 3]
            pe.wait_ge(s["qk_ready"], 8)
            cross(s, 2, [w[:, 2], w[:, 4]], 2)
            pe.wait_ge(s["o_drained"], B * C)
            pe.wait_ge(s_sq, 1)
            bank = ringD.to_fill(pe)
            for t in range(TILES):
                for c in range(C):
                    i = pe.matmul(ps[:, bank, t:t + 1], QT[:, c, t * P:(t + 1) * P], k("ones"), start=(c == 0), stop=(c == C - 1))
            i.then_inc(s_fd, 1)
            pe.wait_ge(s_projw, 1)
            project_tokens(w[:, 5], ringD, AT)

            transpose_tokens()
            wait_weights("l1a")
            pe.wait_ge(s_ret, 1)
            project_features(W["l1a"][:, 0], ringD, KT)
            pe.wait_ge(s_ret, 2)
            for t in range(TILES):
                if t % 2 == 0:
                    bank = ringD.to_fill(pe)
                for c in range(C):
                    i = pe.transpose(ps[:, bank, (t % 2 * C + c) * P:(t % 2 * C + c + 1) * P], AT[:, c, t * P:(t + 1) * P], ident)
                if t % 2:
                    i.then_inc(s_fd, 1)

            transpose_tokens()
            pe.wait_ge(s_tree_w, 48)

            def tree_logits(i):
                pe.wait_ge(s_xslot, i + 1)
                wge(pe, s_lread, i)
                for q in range(4):
                    w0 = q * (WIDTH // 4)
                    for c in range(C):
                        m = pe.matmul(ps[:, q, 0:WIDTH // 4], xslot[:, c, :], win[:, c, w0:w0 + WIDTH // 4],
                                      start=(c == 0), stop=(c == C - 1))
                m.then_inc(s_logit, 1)

            def tree_rest(i, last):
                pe.wait_ge(s_path, i + 1)
                for q in range(4):
                    wge(pe, s_tc, i * 4 + q - 1)
                    for j in range(4):
                        n = q * 4 + j
                        rows_n = min(P, WIDTH - n * P)
                        m = pe.transpose(ps[0:rows_n, 4 + q % 2, j * P:(j + 1) * P], acts[:, n * P:n * P + rows_n], ident)
                    m.then_inc(s_tt, 1)
                if not last:
                    tree_logits(i + 1)
                pe.wait_ge(s_tc, i * 4 + 4)
                wge(pe, s_tx, i)
                for n in range(NB):
                    rows_n = min(P, WIDTH - n * P)
                    m = pe.matmul(ps[:, 6, 0:D], mT[0:rows_n, n, :], wout[0:rows_n, n, :], start=(n == 0), stop=(n == NB - 1))
                m.then_inc(s_ty, 1)

            tree_logits(0)
            run_pipelined(pe, lambda i: tree_rest(i, isinstance(i, int) and i == TILES - 1), TILES)


        @block.scalar
        def _(act):
            chain = Chain(act, s_act)
            ln = [0]

            def deviation():
                ln[0] += 1
                act.wait_ge(s_var, ln[0])
                act.activation(std[:], rstd[:], ACT.Sqrt).then_inc(s_std, 1)

            def drain_transposes():
                for tt in range(TILES // 2):
                    bank = ringA.to_drain(act)
                    src = ps[:, bank, :].rearrange("p (t c n) -> p t c n", t=2, c=C)
                    dst = XT[:, :, tt * 2 * P:(tt + 1) * 2 * P].rearrange("p c (t n) -> p t c n", t=2)
                    act.activation(dst, src, ACT.Copy).then_inc(s_xt, 1)
                    act.wait_ge(s_xt, ln_x[0] * TILES // 2 + tt + 1)
                    act.sem_inc(s_da, 1)
                ln_x[0] += 1
            ln_x = [0]

            def drain_features(dst, done, bias=None):
                for o in range(C):
                    for h in range(2):
                        bank = ringA.to_drain(act)
                        d = dst[:, o, h * BANK:(h + 1) * BANK]
                        if bias is None:
                            i = act.activation(d, ps[:, bank, :], ACT.Copy)
                        else:
                            i = act.activation(d, ps[:, bank, :], ACT.Identity, bias=bias[:, o:o + 1])
                        i.then_inc(s_da, 1)
                act.wait_ge(s_da, ringA.drains)
                act.sem_inc(done, 4)

            def drain_tokens(dst, done):
                for tt in range(TILES // 2):
                    bank = ringA.to_drain(act)
                    act.activation(dst[:, 2 * tt:2 * tt + 2, :].rearrange("p t d -> p (t d)"), ps[:, bank, :], ACT.Copy).then_inc(s_da, 1)
                act.wait_ge(s_da, ringA.drains)
                act.sem_inc(done, 4)

            def cross(s, maps, bias):
                fills = maps + 1

                def kv(i, sl_b):
                    sl = sl_b % 2
                    for n in range(fills):
                        act.wait_ge(s["kv_filled"], (i * 2 + sl_b) * fills + n + 1)
                        if n == 1:
                            x = act.activation(vs[:, sl].rearrange("p h d -> p (h d)"), ps[:, 7, :], ACT.Copy)
                        elif bias is None:
                            x = act.activation(kts[:, sl, n // 2].rearrange("p c n -> p (c n)"), ps[:, 7, :], ACT.Copy)
                        else:
                            for o in range(C):
                                x = act.activation(kts[:, sl, n // 2, o], ps[:, 7, o * SK:(o + 1) * SK], ACT.Identity, bias=bias[:, o:o + 1])
                        x.then_inc(s["kv_drained"], 1)

                def exps(i, u):
                    U = i * 8 + u
                    act.wait_ge(s["mx_ready"], U + 1)
                    for mp in range(maps):
                        for j in range(2):
                            if maps == 1:
                                src = sm[:, u % 2, j * SK:(j + 1) * SK]
                            else:
                                src = ps[:, (u % 2) * 2 + mp, j * SK:(j + 1) * SK]
                            dst = (p1, p2)[mp][:, u % 2, j * SK:(j + 1) * SK]
                            n = mp * 2 + j
                            x = act.activation(dst, src, ACT.Exp, bias=mx[:, u % 4, n:n + 1], scale=SCALE,
                                               accum_out=rs[:, u % 4, n:n + 1])
                    x.then_inc(s["exp_done"], 1)

                def evac(i, u):
                    U = i * 8 + u
                    act.wait_ge(s["pt_filled"], U + 1)
                    wge(act, s["pv_done"], U - 1)
                    act.activation(pts[:, u % 2, :], ps[:, 4 + u % 2, :], ACT.Copy).then_inc(s["pt_drained"], 1)

                kv(0, 0)
                exps(0, 0)
                exps(0, 1)
                act.wait_ge(s["pt_filled"], 1)
                exps(0, 2)
                evac(0, 0)

                def body(i):
                    last = isinstance(i, int) and i == B // 2 - 1
                    for u in range(8):
                        if u % 4 == 0 and not (last and u == 4):
                            kv(i, u // 4 + 1)
                        if not (last and u + 1 >= 8):
                            evac(i, u + 1)
                        if not (last and u + 3 >= 8):
                            exps(i, u + 3)
                run_pipelined(act, body, B // 2)

            def self_attention(s):
                def exps(i, u):
                    U = i * 4 + u
                    act.wait_ge(s["mx_ready"], U + 1)
                    act.activation(p1[:, u % 2, :], sm[:, u % 2, :], ACT.Exp, scale=SCALE).then_inc(s["exp_done"], 1)

                def evac(i, u):
                    U = i * 4 + u
                    act.wait_ge(s["pt_filled"], U + 1)
                    wge(act, s["pv_done"], U - 1)
                    act.activation(pts[:, u % 2, :], ps[:, 4 + u % 2, :], ACT.Copy).then_inc(s["pt_drained"], 1)

                exps(0, 0)
                exps(0, 1)
                act.wait_ge(s["pt_filled"], 1)
                exps(0, 2)
                evac(0, 0)
                n = TILES // 2

                def body(i):
                    last = isinstance(i, int) and i == n - 1
                    for u in range(4):
                        if not (last and u + 1 >= 4):
                            evac(i, u + 1)
                        if not (last and u + 3 >= 4):
                            exps(i, u + 3)
                run_pipelined(act, body, n)

            deviation()
            drain_transposes()
            act.wait_ge(s_in["vec"], 16)
            drain_features(QT, st["l0x"]["qk_ready"], v("bq"))
            cross(st["l0x"], 1, v("bk"))
            deviation()
            drain_transposes()
            drain_tokens(VT, st["l0a"]["kv_drained"])
            self_attention(st["l0a"])
            deviation()
            drain_transposes()
            drain_features(QT, st["l0f"]["qk_ready"])
            drain_features(KT, st["l0f"]["qk_ready"])
            drain_tokens(VT, st["l0f"]["kv_drained"])
            self_attention(st["l0f"])
            deviation()
            drain_transposes()
            act.wait_ge(s_router, 1)
            act.activation(router[:, 1], router[:, 0], ACT.Exp).then_inc(s_router, 1)
            for h in range(2):
                bank = ringA.to_drain(act)
                act.activation(gwT[:, h * BANK:(h + 1) * BANK], ps[0:E, bank, :], ACT.Copy).then_inc(s_da, 1)
                act.wait_ge(s_da, ringA.drains)
                act.sem_inc(s_gwT, 1)
            for e in range(E):
                bank = ringA.to_drain(act)
                act.activation(gates[:, e, 0:BANK], ps[:, bank, :], ACT.Copy).then_inc(s_da, 1)
                act.wait_ge(s_da, ringA.drains)
                act.sem_inc(s_gb, 1)

            def gelus(i):
                for u in range(4 * M):
                    sl, h, m = u // (2 * M) % 2, u // M % 2, u % M
                    act.wait_ge(s_hid, i * (4 * M) + u + 1)
                    wge(act, s_h1, i * (4 * M) + u - 1)
                    if u == 0:
                        act.wait_ge(s_bb1, i + 1)
                    bias = bb1s[:, sl * M + m:sl * M + m + 1]
                    act.activation(gact[:, u % 2, :], ps[:, 4 + u % 4, :], ACT.Gelu_apprx_tanh, bias=bias).then_inc(s_gelu, 1)
            run_pipelined(act, gelus, E // 2)
            act.wait_ge(s_y, E * 2 * M)
            for h in range(2):
                for o in range(C):
                    act.activation(QT[:, o, h * BANK:(h + 1) * BANK], ps[:, h * C + o, :], ACT.Copy).then_inc(s_acc, 1)
            deviation()
            deviation()
            drain_transposes()
            drain_features(QT, st["l1x"]["qk_ready"])
            drain_features(KT, st["l1x"]["qk_ready"])
            cross(st["l1x"], 2, None)
            act.wait_ge(st["l1x"]["o_drained"], B * C)
            act.activation(QT[:], AT[:], ACT.Square).then_inc(s_sq, 1)
            deviation()
            act.wait_ge(s_in["vec"], 16)
            act.activation(dk[:, 0:2], v("decay"), ACT.Exp, scale=-1.0).then_inc(s_norm, 1)
            deviation()
            drain_transposes()
            deviation()
            drain_transposes()

            def trees(i):
                act.wait_ge(s_act_in, i + 1)
                act.activation(acts, logit, ACT.Silu).then_inc(s_silu, 1)
                for q in range(4):
                    act.wait_ge(s_tt, i * 4 + q + 1)
                    if q == 0:
                        wge(act, s_ty, i)
                    full = 4 if q < 3 else 3
                    x = act.activation(mT[:, 4 * q:4 * q + full, :].rearrange("p j t -> p (j t)"), ps[:, 4 + q % 2, 0:full * P], ACT.Copy)
                    if q == 3:
                        r = WIDTH - (NB - 1) * P
                        x = act.activation(mT[0:r, NB - 1, :], ps[0:r, 4 + q % 2, 3 * P:4 * P], ACT.Copy)
                    x.then_inc(s_tc, 1)
            run_pipelined(act, trees, TILES)


        @block.vector
        def _(dve):
            chain = Chain(dve, s_dve)
            link = chain.link
            ln = [0]

            def stats(src):
                for t in range(TILES):
                    i = dve.bn_stats(stat[:, t, :], src[:, t, :])
                link(i)
                for t in range(TILES):
                    i = dve.bn_aggr(mv[:, t, :], stat[:, t, :])
                link(i)
                ln[0] += 1
                dve.tensor_scalar(rstd[:], mv[:, :, 1], 1e-5, None, ALU.add).then_inc(s_var, 1)
                dve.wait_ge(s_std, ln[0])
                link(dve.reciprocal(rstd[:], std[:]))

            def normalise(src, dst, done=None):
                for t in range(TILES):
                    i = dve.tensor_scalar(dst[:, t, :], src[:, t, :], mv[:, t, 0:1], rstd[:, t:t + 1], ALU.subtract, ALU.mult)
                    if done is not None:
                        i.then_inc(done, 1)
                if done is None:
                    link(i)

            def row(n):
                return rows[:, ROWS.index(n), :].unsqueeze(1).broadcast_to([P, TILES, D])

            def add_tokens(dst):
                for tt in range(TILES // 2):
                    bank = ringD.to_drain(dve)
                    d = dst[:, 2 * tt:2 * tt + 2, :].rearrange("p t d -> p (t d)")
                    i = dve.tensor_tensor(d, ps[:, bank, :], d, ALU.add)
                    i.then_inc(s_dd, 1)
                dve.wait_ge(s_dd, ringD.drains)

            def cross(s, maps, bias):
                def maxes(i, u):
                    U = i * 8 + u
                    dve.wait_ge(s["s_done"], U + 1)
                    if maps == 1:
                        wge(dve, s["exp_done"], U - 1)
                        x = dve.tensor_tensor(sm[:, u % 2, :].rearrange("p (j n) -> p j n", j=2),
                                              ps[:, u % 4, :].rearrange("p (j n) -> p j n", j=2),
                                              bias_x[:].unsqueeze(1).broadcast_to([P, 2, SK]), ALU.add)
                        x.then_inc(s["s_read"], 1)
                        dve.wait_ge(s["s_read"], U + 1)
                        link(dve.tensor_reduce(rs[:, u % 4, 4:6], sm[:, u % 2, :].rearrange("p (j n) -> p j n", j=2), X_AXIS, ALU.max))
                    else:
                        for mp in range(2):
                            x = dve.tensor_reduce(rs[:, u % 4, 4 + 2 * mp:6 + 2 * mp],
                                                  ps[:, (u % 2) * 2 + mp, :].rearrange("p (j n) -> p j n", j=2), X_AXIS, ALU.max)
                        link(x)
                    dve.tensor_scalar(mx[:, u % 4, 0:2 * maps], rs[:, u % 4, 4:4 + 2 * maps], -SCALE, None, ALU.mult).then_inc(s["mx_ready"], 1)

                def norms(i, u):
                    U = i * 8 + u
                    dve.wait_ge(s["exp_done"], U + 1)
                    link(dve.reciprocal(ri[:, u % 2, 0:2 * maps], rs[:, u % 4, 0:2 * maps]))
                    if maps == 2:
                        pr = u % 4 * 2
                        link(dve.tensor_tensor(ri[:, u % 2, 2:4], ri[:, u % 2, 2:4], lam[:, pr:pr + 2], ALU.mult))
                        for j in range(2):
                            x = dve.tensor_scalar(p2[:, u % 2, j * SK:(j + 1) * SK], p2[:, u % 2, j * SK:(j + 1) * SK],
                                                  ri[:, u % 2, 2 + j:3 + j], None, ALU.mult)
                        link(x)
                    for j in range(2):
                        d = p1[:, u % 2, j * SK:(j + 1) * SK]
                        if maps == 1:
                            x = dve.tensor_scalar(d, d, ri[:, u % 2, j:j + 1], None, ALU.mult)
                        else:
                            x = dve.scalar_tensor_tensor(out=d, in0=d, scalar=ri[:, u % 2, j:j + 1],
                                                         in1=p2[:, u % 2, j * SK:(j + 1) * SK], op0=ALU.mult, op1=ALU.subtract)
                    x.then_inc(s["p_ready"], 1)

                def extract(i, u):
                    U, g, b = i * 8 + u, u // 2 % 2, i * 2 + u // 4
                    dve.wait_ge(s["pv_done"], U + 1)
                    even, odd = k("even"), k("odd")
                    if bias is None:
                        link(dve.tensor_scalar(tmp[:, 0, :], ps[:, 6, 0:S], even, None, ALU.mult))
                    else:
                        link(dve.tensor_scalar(tmp[:, 0, :], ps[:, 6, 0:S], even, bias[:, g:g + 1], ALU.mult, ALU.add))
                    dve.scalar_tensor_tensor(out=AT[:, g, bass.ds(b * S, S)], in0=ps[:, 6, S:2 * S], scalar=odd, in1=tmp[:, 0, :],
                                             op0=ALU.mult, op1=ALU.add).then_inc(s["o_drained"], 1)

                maxes(0, 0)
                maxes(0, 1)
                norms(0, 0)
                maxes(0, 2)
                norms(0, 1)

                def body(i):
                    last = isinstance(i, int) and i == B // 2 - 1
                    for u in range(8):
                        if not (last and u + 3 >= 8):
                            maxes(i, u + 3)
                        if not (last and u + 2 >= 8):
                            norms(i, u + 2)
                        if u % 2:
                            extract(i, u)
                run_pipelined(dve, body, B // 2, chain)

            def self_attention(s):
                causal = k("causal").unsqueeze(1).broadcast_to([P, 8, S])

                def maxes(i, u):
                    U = i * 4 + u
                    dve.wait_ge(s["s_done"], U + 1)
                    wge(dve, s["exp_done"], U - 1)
                    m3 = sm[:, u % 2, :].rearrange("p (j n) -> p j n", j=8)
                    dve.tensor_tensor(m3, ps[:, u % 4, :].rearrange("p (j n) -> p j n", j=8), causal, ALU.add).then_inc(s["s_read"], 1)
                    dve.wait_ge(s["s_read"], U + 1)
                    link(dve.tensor_reduce(mx[:, u % 4, :], m3, X_AXIS, ALU.max))
                    dve.tensor_tensor(m3, m3, mx[:, u % 4, :].unsqueeze(2).broadcast_to([P, 8, S]), ALU.subtract).then_inc(s["mx_ready"], 1)

                def norms(i, u):
                    U = i * 4 + u
                    dve.wait_ge(s["exp_done"], U + 1)
                    p3 = p1[:, u % 2, :].rearrange("p (j n) -> p j n", j=8)
                    link(dve.tensor_reduce(rs[:, u % 4, :], p3, X_AXIS, ALU.add))
                    link(dve.reciprocal(ri[:, u % 2, :], rs[:, u % 4, :]))
                    dve.tensor_tensor(p3, p3, ri[:, u % 2, :].unsqueeze(2).broadcast_to([P, 8, S]), ALU.mult).then_inc(s["p_ready"], 1)

                def extract(i, u):
                    U, g, t = i * 4 + u, u % 2, i * 2 + u // 2
                    dve.wait_ge(s["pv_done"], U + 1)
                    link(dve.tensor_scalar(tmp[:, :, :], ps[:, 6:8, 0:S], k("even"), None, ALU.mult))
                    dst = AT[:, g, bass.ds(t * P, P)].rearrange("p (b q) -> p b q", b=2)
                    dve.scalar_tensor_tensor(out=dst, in0=ps[:, 6:8, S:2 * S], scalar=k("odd"), in1=tmp[:, :, :],
                                             op0=ALU.mult, op1=ALU.add).then_inc(s["o_drained"], 1)

                maxes(0, 0)
                maxes(0, 1)
                norms(0, 0)
                maxes(0, 2)
                norms(0, 1)
                n = TILES // 2

                def body(i):
                    last = isinstance(i, int) and i == n - 1
                    for u in range(4):
                        if not (last and u + 3 >= 4):
                            maxes(i, u + 3)
                        if not (last and u + 2 >= 4):
                            norms(i, u + 2)
                        extract(i, u)
                run_pipelined(dve, body, n, chain)

            dve.wait_ge(s_in["x"], 16)
            stats(X)
            normalise(X, XN, s_xn)
            dve.wait_ge(s_in["mask"], 16)
            dve.wait_ge(s_in["con"], 16)
            dve.wait_ge(s_in["vec"], 16)
            dve.wait_ge(s_in["rows"], 16)
            link(dve.tensor_scalar(bias_x[:], maskb[:], 1.0, -MASKED, ALU.subtract, ALU.mult))
            dve.wait_ge(s_xn, TILES)
            link(dve.tensor_tensor(X[:], X[:], row("xattn_bo"), ALU.add))
            link(dve.tensor_tensor(lam[:], v("lam1"), v("lam2"), ALU.subtract))
            link(dve.tensor_scalar(lam[:], lam[:], 0.1, None, ALU.add))
            cross(st["l0x"], 1, v("bv"))
            add_tokens(X)

            stats(X)
            normalise(X, XN, s_xn)
            cos = k("cos").unsqueeze(1).broadcast_to([P, BANK // S, S])
            sin = k("sin").unsqueeze(1).broadcast_to([P, BANK // S, S])
            dve.wait_ge(s_xn, 2 * TILES)
            for o in range(C):
                for h in range(2):
                    for dst in (QT, KT):
                        d = dst[:, o, h * BANK:(h + 1) * BANK].rearrange("p (b s) -> p b s", s=S)
                        bank = ringD.to_drain(dve)
                        dve.tensor_tensor(d, ps[:, bank, :].rearrange("p (b s) -> p b s", s=S), cos, ALU.mult).then_inc(s_dd, 1)
                        bank = ringD.to_drain(dve)
                        t3 = sm[:, 0, :].rearrange("p (b s) -> p b s", s=S)
                        dve.tensor_tensor(t3, ps[:, bank, :].rearrange("p (b s) -> p b s", s=S), sin, ALU.mult).then_inc(s_dd, 1)
                        dve.wait_ge(s_dd, ringD.drains)
                        i = dve.tensor_tensor(d, d, t3, ALU.add)
                        if o == C - 1 and h == 1 and dst is KT:
                            i.then_inc(st["l0a"]["qk_ready"], 1)
                        else:
                            link(i)
            dve.wait_ge(st["l0a"]["qk_ready"], 1)
            self_attention(st["l0a"])
            add_tokens(X)

            stats(X)
            normalise(X, XN, s_xn)
            dve.wait_ge(s_xn, 3 * TILES)
            self_attention(st["l0f"])
            add_tokens(XN)
            stats(XN)
            normalise(XN, XN)
            link(dve.tensor_tensor(XN[:], XN[:], row("ffn_g1"), ALU.mult))
            dve.tensor_tensor(XN[:], XN[:], row("ffn_b1"), ALU.add).then_inc(s_xn, TILES)
            bank = ringD.to_drain(dve)
            lg = ps[:, bank, 0:TILES * E].rearrange("p (t e) -> p t e", e=E)
            r0, r1, r2, r3 = (router[:, n] for n in range(4))
            link(dve.tensor_reduce(ri[:, 0, :], lg, X_AXIS, ALU.max))
            dve.tensor_tensor(r0, lg, ri[:, 0, :].unsqueeze(2).broadcast_to([P, TILES, E]), ALU.subtract).then_inc(s_router, 1)
            dve.wait_ge(s_router, 2)
            dve.sem_inc(s_dd, 1)
            link(dve.tensor_reduce(ri[:, 0, :], r1, X_AXIS, ALU.add))
            link(dve.reciprocal(ri[:, 1, :], ri[:, 0, :]))
            link(dve.tensor_tensor(r2, r1, ri[:, 1, :].unsqueeze(2).broadcast_to([P, TILES, E]), ALU.mult))
            mine = r2.unsqueeze(3).broadcast_to([P, TILES, E, E])
            other = r2.unsqueeze(2).broadcast_to([P, TILES, E, E])
            g4 = rk[:, 0, :].rearrange("p (t e j) -> p t e j", t=TILES, e=E)
            e4 = rk[:, 1, :].rearrange("p (t e j) -> p t e j", t=TILES, e=E)
            dve.tensor_tensor(g4, other, mine, ALU.is_gt)
            link(dve.tensor_tensor(e4, other, mine, ALU.is_equal))
            bef = k("before").unsqueeze(1).broadcast_to([P, TILES, E * E])
            e3 = rk[:, 1, :].rearrange("p (t n) -> p t n", t=TILES)
            link(dve.tensor_tensor(e3, e3, bef, ALU.mult))
            link(dve.tensor_tensor(rk[:, 0, :], rk[:, 0, :], rk[:, 1, :], ALU.add))
            link(dve.tensor_reduce(r3, g4, X_AXIS, ALU.add))
            link(dve.tensor_scalar(r3, r3, 1.5, None, ALU.is_lt))
            link(dve.tensor_tensor(r3, r3, r2, ALU.mult))
            link(dve.tensor_reduce(ri[:, 0, :], r3, X_AXIS, ALU.add))
            link(dve.reciprocal(ri[:, 1, :], ri[:, 0, :]))
            dve.tensor_tensor(gw[:], r3, ri[:, 1, :].unsqueeze(2).broadcast_to([P, TILES, E]), ALU.mult).then_inc(s_gw, 1)
            for e in range(E):
                bank = ringD.to_drain(dve)
                dve.tensor_copy(gates[:, e, BANK:2 * BANK], ps[:, bank, :]).then_inc(s_dd, 1)
                dve.wait_ge(s_dd, ringD.drains)
                dve.sem_inc(s_gb, 1)
            dve.wait_ge(s_gb, 2 * E)

            def gating(i):
                for u in range(4 * M):
                    sl, h = u // (2 * M) % 2, u // M % 2
                    dve.wait_ge(s_gelu, i * (4 * M) + u + 1)
                    wge(dve, s_y, i * (4 * M) + u - 1)
                    if isinstance(i, int):
                        gt = gates[:, i * 2 + sl, h * BANK:(h + 1) * BANK]
                    else:
                        gt = big_b[:, bass.ds((i * 2 + sl) * N + h * BANK, BANK)]
                    dve.tensor_tensor(hg[:, u % 2, :], gact[:, u % 2, :], gt, ALU.mult).then_inc(s_h1, 1)
            run_pipelined(dve, gating, E // 2)
            add_tokens(XN)
            stats(XN)
            normalise(XN, XN)
            link(dve.tensor_tensor(XN[:], XN[:], row("ffn_g2"), ALU.mult))
            link(dve.tensor_tensor(XN[:], XN[:], row("ffn_b2"), ALU.add))
            link(dve.tensor_tensor(X[:], X[:], XN[:], ALU.add))

            stats(X)
            normalise(X, XN, s_xn)
            dve.wait_ge(s_xn, 5 * TILES)
            link(dve.tensor_tensor(X[:], X[:], row("proj_b"), ALU.add))
            cross(st["l1x"], 2, None)
            dve.wait_ge(s_w[1], 32)
            for c in range(C):
                wp = W["l1x"][:, 5, c, :]
                i = dve.tensor_scalar(wp, wp, v("norm_w")[:, c:c + 1], None, ALU.mult)
            i.then_inc(s_projw, 1)
            bank = ringD.to_drain(dve)
            ln[0] += 1
            dve.tensor_scalar(rstd[:], ps[:, bank, 0:TILES], 1.0 / D, 1e-6, ALU.mult, ALU.add).then_inc(s_var, 1)
            dve.wait_ge(s_std, ln[0])
            dve.sem_inc(s_dd, 1)
            link(dve.reciprocal(rstd[:], std[:]))
            for tt in range(TILES // 2):
                bank = ringD.to_drain(dve)
                for t in range(2):
                    i = dve.scalar_tensor_tensor(out=X[:, 2 * tt + t, :], in0=ps[:, bank, t * D:(t + 1) * D],
                                                 scalar=rstd[:, 2 * tt + t:2 * tt + t + 1], in1=X[:, 2 * tt + t, :],
                                                 op0=ALU.mult, op1=ALU.add)
                i.then_inc(s_dd, 1)
            dve.wait_ge(s_dd, ringD.drains)

            stats(X)
            normalise(X, XN, s_xn)
            dve.wait_ge(s_norm, 1)
            dve.wait_ge(s_xn, 6 * TILES)
            link(dve.tensor_scalar(dk[:, 2:4], dk[:, 0:2], 1.0, None, ALU.add))
            link(dve.reciprocal(dk[:, 4:6], dk[:, 2:4]))
            link(dve.tensor_scalar(dk[:, 6:8], dk[:, 4:6], -1.0, 1.0, ALU.mult, ALU.add))
            link(dve.tensor_tensor(dk[:, 0:2], v("ret_b"), v("conv_b"), ALU.add))
            da = big_b[:, 0:C * N].rearrange("p (c n) -> p c n", c=C)
            dx = big_b[:, C * N:2 * C * N].rearrange("p (c n) -> p c n", c=C)
            dve.wait_ge(s_xt, 6 * TILES // 2)
            for c in range(C):
                dve.tensor_scalar(dx[:, c, :], XT[:, c, :], dk[:, 6 + c:7 + c], None, ALU.mult)
                dve.tensor_scalar(da[:, c, :], XT[:, c, :], 0.0, dk[:, 4 + c:5 + c], ALU.mult, ALU.add)
            link(dve.memset(tmp[:, 0, :], 0.0))
            link(dve.tensor_copy(da.rearrange("p c (b s) -> p (c b) s", s=S)[:, :, 0], tmp[:, 0, 0:C * B]))
            for c in range(C):
                i = dve.tensor_tensor_scan(KT[:, c, :], da[:, c, :], dx[:, c, :], 0.0, ALU.mult, ALU.add)
            i.then_inc(s_ret, 1)
            for c in range(C):
                xt = XT[:, c, :].rearrange("p (b s) -> p b s", s=S)
                y = QT[:, c, :].rearrange("p (b s) -> p b s", s=S)
                for tap in (2, 0, 1, 3, 4):
                    w = v("conv_w")[:, c * TAPS + tap:c * TAPS + tap + 1]
                    sh = tap - TAPS // 2
                    if sh == 0:
                        link(dve.tensor_scalar(y, xt, w, dk[:, c:c + 1], ALU.mult, ALU.add))
                    else:
                        lo, hi = max(0, -sh), S - max(0, sh)
                        link(dve.scalar_tensor_tensor(out=y[:, :, lo:hi], in0=xt[:, :, lo + sh:hi + sh], scalar=w,
                                                      in1=y[:, :, lo:hi], op0=ALU.mult, op1=ALU.add))
            for o in range(C):
                for h in range(2):
                    bank = ringD.to_drain(dve)
                    i = dve.tensor_tensor(AT[:, o, h * BANK:(h + 1) * BANK], ps[:, bank, :], QT[:, o, h * BANK:(h + 1) * BANK], ALU.add)
                    i.then_inc(s_dd, 1)
            dve.wait_ge(s_dd, ringD.drains)
            dve.sem_inc(s_ret, 1)
            add_tokens(X)

            stats(X)
            normalise(X, XN, s_xn)
            dve.wait_ge(s_tree_w, 48)

            def tree3(ap):
                return ap.rearrange("p (t n) -> p t n", t=TREES)

            def trees(i):
                dve.wait_ge(s_logit, i + 1)
                wge(dve, s_silu, i)
                q3 = ps[:, 0:4, 0:WIDTH // 4]
                dve.tensor_tensor(logit.rearrange("p (q n) -> p q n", q=4), q3, bin_b.rearrange("p (q n) -> p q n", q=4), ALU.add)\
                   .then_inc(s_lread, 1)
                dve.wait_ge(s_lread, i + 1)
                wge(dve, s_tt, i * 4)
                dve.sem_inc(s_act_in, 1)
                link(dve.tensor_scalar(dec, logit, 0.0, None, ALU.is_gt))
                link(dve.tensor_scalar(tree3(path)[:, :, 0:1], tree3(logit)[:, :, 0:1], 0.0, 1.0, ALU.mult, ALU.add))
                for d in range(DEPTH):
                    n0, n1, w = 2 ** d - 1, 2 ** (d + 1) - 1, 2 ** d
                    par, de = tree3(path)[:, :, n0:n0 + w], tree3(dec)[:, :, n0:n0 + w]
                    kids = tree3(path)[:, :, n1:n1 + 2 * w]
                    left, right = kids[:, :, 0:2 * w:2], kids[:, :, 1:2 * w:2]
                    link(dve.tensor_tensor(right, par, de, ALU.mult))
                    link(dve.tensor_tensor(left, par, right, ALU.subtract))
                dve.wait_ge(s_silu, i + 1)
                dve.tensor_tensor(acts, acts, path, ALU.mult).then_inc(s_path, 1)
                dve.wait_ge(s_ty, i + 1)
                xt = X[:, i, :] if isinstance(i, int) else X[:].rearrange("p t d -> p (t d)")[:, bass.ds(i * D, D)]
                dve.tensor_tensor(xt, ps[:, 6, 0:D], xt, ALU.add).then_inc(s_tx, 1)
            run_pipelined(dve, trees, TILES, chain)

        @block.gpsimd
        def _(pool):
            head = k("head").unsqueeze(2).broadcast_to([P, HG, S])

            def queries(src, off):
                return src[:, bass.ds(off, S)].unsqueeze(1).broadcast_to([P, HG, S])

            def mask_cross(s, maps):
                pool.wait_ge(s["qk_ready"], 4 * maps)

                def body(i):
                    for sl in range(2):
                        wge(pool, s["s_done"], i * 8 + 4 * (sl - 1))
                        for g in range(C):
                            for mp in range(maps):
                                src = (QT, KT)[mp][:, g, :]
                                x = pool.tensor_tensor(qm[:, sl, mp, g], queries(src, (i * 2 + sl) * S), head, ALU.mult)
                            x.then_inc(s["qm_ready"], 1)
                run_pipelined(pool, body, B // 2)

            def mask_self(s):
                pool.wait_ge(s["kv_drained"], 4)

                def tile_values(i, tu):
                    wge(pool, s["pv_done"], i * 4 + tu * 2 - 2)
                    for b in range(2):
                        x = pool.tensor_tensor(vs[:, tu % 2, b, :], VT.rearrange("p t d -> p (t d)")[:, bass.ds(i * (2 * D) + tu * D, D)],
                                               k("batch")[:, b:b + 1].broadcast_to([P, D]), ALU.mult)
                    x.then_inc(s["v_ready"], 1)

                def body(i):
                    for u in range(4):
                        wge(pool, s["s_done"], i * 4 + u - 1)
                        for b in range(2):
                            x = pool.tensor_tensor(qm[:, u % 2, b, 0], queries(QT[:, u % 2, :], (i * 2 + u // 2) * P + b * S), head, ALU.mult)
                        x.then_inc(s["qm_ready"], 1)
                        if u % 2 == 0 and not (isinstance(i, int) and i == 0 and u == 0):
                            tile_values(i, u // 2 - 1)
                run_pipelined(pool, body, TILES // 2)
                tile_values(TILES // 2, -1)

            pool.wait_ge(s_in["con"], 16)
            mask_cross(st["l0x"], 1)
            pool.wait_ge(st["l0a"]["qk_ready"], 1)
            mask_self(st["l0a"])
            pool.wait_ge(st["l0f"]["qk_ready"], 8)
            mask_self(st["l0f"])

            def hidden_biases(i):
                wge(pool, s_gelu, i * (4 * M))
                pool.tensor_copy(bb1s[:], vec[:, bass.ds(i * (2 * M) + VEC["bb1"][0], 2 * M)]).then_inc(s_bb1, 1)
            run_pipelined(pool, hidden_biases, E // 2)
            mask_cross(st["l1x"], 2)
            pool.wait_ge(s_xt, 7 * TILES // 2)

            def slots(i):
                wge(pool, s_logit, i)
                pool.tensor_copy(xslot, XT[:, :, bass.ds(i * P, P)]).then_inc(s_xslot, 1)
            run_pipelined(pool, slots, TILES)


def _kmaj(w):
    i, o = w.shape
    return np.ascontiguousarray(w.reshape(i // P, P, o).transpose(1, 0, 2).reshape(P, -1))


def _col(v):
    return np.ascontiguousarray(v.reshape(-1, P).T)


def _constants():
    con = np.zeros((P, NCON), np.float32)
    p = np.arange(P)

    def put(name, val):
        lo, hi = CON[name]
        con[:, lo:hi] = val
    put("ident", np.eye(P))
    put("head", (p[:, None] // HD) == np.arange(HG)[None, :])
    put("even", ((p // HD) % 2 == 0)[:, None])
    put("odd", ((p // HD) % 2 == 1)[:, None])
    put("causal", np.where(np.arange(S)[None, :] <= (p % S)[:, None], 0.0, MASKED))
    freqs = np.exp(np.arange(HD // 2, dtype=np.float32) * np.float32(-np.log(10000.0) * 2.0 / HD)).astype(np.float32)
    ang = (np.arange(S, dtype=np.float32)[None, :] * freqs[(p % HD) // 2][:, None]).astype(np.float32)
    put("cos", np.cos(ang))
    put("sin", np.sin(ang) * np.where(p % 2 == 0, -1.0, 1.0)[:, None])
    put("ones", 1.0)
    put("batch", (p // S)[:, None] == np.arange(2)[None, :])
    put("before", np.broadcast_to((np.arange(E)[None, :] < np.arange(E)[:, None]).reshape(1, -1), (P, E * E)))
    sel = np.zeros((E, E, P), np.float32)
    for e in range(E):
        sel[e, e] = 1.0
    return con, sel.reshape(E, E * P)


def kernel(**inputs):
    import concourse.bacc as _bacc
    from concourse.bass_utils import run_bass_kernel_spmd as _run

    i = {n: np.asarray(x) for n, x in inputs.items()}
    con, sel = _constants()
    swap = np.arange(D) ^ 1
    ipw = i["L0_attn_in_proj_w"]
    kv1, kv2 = i["L1_xattn_kv1_w"], i["L1_xattn_kv2_w"]

    def pair_rows(v):
        return np.concatenate([np.broadcast_to(v.reshape(-1)[n::2], (P // 2, H // 2)) for n in range(2)], 0)

    arrays = {
        "x": i["x"],
        "ctxT": np.ascontiguousarray(i["ctx_1024"].transpose(0, 2, 1).reshape(B, C, P, SK).transpose(0, 2, 1, 3).reshape(B, P, C * SK)),
        "mask": np.ascontiguousarray(np.concatenate([i["mask_1x1xSxS2_bk0"][0, 0]] * 2, 0)),
        "con": con, "sel": sel,
        "w_l0x": np.concatenate([_kmaj(i["L0_xattn_" + n].T) for n in ("Wq", "Wk", "Wv", "Wo")], 1),
        "w_l0a": np.concatenate([_kmaj(w.T) for w in (ipw[:D], ipw[D:2 * D], ipw[2 * D:], ipw[:D][swap], ipw[D:2 * D][swap],
                                                      i["L0_attn_out_proj_w"])], 1),
        "w_l0f": np.concatenate([_kmaj(w) for w in (i["L0_ffn_w_qkv"][:, :D], i["L0_ffn_w_qkv"][:, D:2 * D],
                                                    i["L0_ffn_w_qkv"][:, 2 * D:], i["L0_ffn_w_o"])], 1),
        "w_l1x": np.concatenate([_kmaj(w.T) for w in (i["L1_xattn_q1_w"], i["L1_xattn_q2_w"], kv1[:D], kv1[D:], kv2[:D],
                                                      i["L1_xattn_proj_w"])], 1),
        "w_l1a": _kmaj(i["L1_attn_W"].T),
        "wg": _kmaj(i["L0_ffn_wg"]),
        "w1": np.ascontiguousarray(i["L0_ffn_w1"].reshape(E, C, P, F).transpose(0, 2, 1, 3).reshape(E, P, C * F)),
        "w2": np.ascontiguousarray(i["L0_ffn_w2"].reshape(E, M, P, D).transpose(0, 2, 1, 3).reshape(E, P, M * D)),
        "bb2": i["L0_ffn_bb2"],
        "w_in": _kmaj(i["L1_ffn_W_in"].T),
        "w_out": _kmaj(np.concatenate([i["L1_ffn_W_out"].T, np.zeros((NB * P - WIDTH, D), np.float32)], 0)),
        "b_in": i["L1_ffn_b_in"],
        "rows": np.concatenate([i[n] for n in ("L0_xattn_bo", "L0_ffn_g1", "L0_ffn_b1", "L0_ffn_g2", "L0_ffn_b2", "L1_xattn_proj_b")]),
        "vec": np.concatenate([
            _col(i["L0_xattn_bq"]), _col(i["L0_xattn_bk"]), _col(i["L0_xattn_bv"]), _col(i["L1_attn_decay_logit"]),
            _col(i["L1_attn_b"]), _col(i["L1_attn_conv_b"]),
            i["L1_attn_conv_w"].reshape(C, P, TAPS).transpose(1, 0, 2).reshape(P, -1),
            pair_rows(i["L1_xattn_lambda_1"]), pair_rows(i["L1_xattn_lambda_2"]), _col(i["L1_xattn_norm_w"]),
            i["L0_ffn_bb1"].reshape(E * M, P).T], 1),
    }
    nc = _bacc.Bacc("TRN2", target_bir_lowering=False, num_devices=1)
    feeds, args = {}, {}
    for n, arr in arrays.items():
        arr = np.ascontiguousarray(arr)
        feeds["in_" + n] = arr
        args[n] = nc.dram_tensor("in_" + n, arr.shape, mybir.dt.from_np(arr.dtype), kind="ExternalInput").ap()
    out = nc.dram_tensor("out_0", (B, S, D), F32, kind="ExternalOutput").ap()
    build(nc, args, out)
    r = _run(nc, [feeds], core_ids=[0])
    return r.results[0]["out_0"]
```

```python
from contextlib import ExitStack

import numpy as np

import concourse.bass as bass
from concourse import mybir

F32 = mybir.dt.float32
I32 = mybir.dt.int32
F32R = mybir.dt.float32r
U8 = mybir.dt.uint8
ALU = mybir.AluOpType
ACT = mybir.ActivationFunctionType
X_AXIS = mybir.AxisListType.X

P = 128
B, S, D = 16, 64, 256
SK = 256
N = B * S
H, HD = 16, 16
C = D // P
TILES = N // P
HG = H // C
PAIRS = HG // 2
E, F = 8, 1024
M = F // P
TREES, NODES, DEPTH = 8, 255, 7
WIDTH = TREES * NODES
NB = (WIDTH + P - 1) // P
TAPS = 5
TOP = 2
SLOTS = 256
NBLK = (N * TOP - E) // SLOTS + E
NSLOT = NBLK * SLOTS
UB = M // 2
CH = 4
FAR = 8192.0
SCALE = float(HD) ** -0.5
MASKED = -1.0e30
BANK = 512
MG = 4
WG = C * MG * P + MG * D


VEC = {}
_at = 0
for _name, _n in (("bq", C), ("bk", C), ("bv", C), ("decay", C), ("ret_b", C), ("conv_b", C), ("conv_w", C * TAPS),
                  ("lam1", 2 * PAIRS), ("lam2", 2 * PAIRS), ("norm_w", C)):
    VEC[_name] = (_at, _at + _n)
    _at += _n
NVEC = _at
CON = {}
_at = 0
for _name, _n in (("ident", P), ("head", HG), ("even", 1), ("odd", 1), ("causal", S), ("cos", S), ("sin", S),
                  ("ones", 1), ("half", 2),
                  ("earlier", P), ("all", P), ("steps", N // SLOTS), ("blocks", NBLK), ("before", E * E)):
    CON[_name] = (_at, _at + _n)
    _at += _n
NCON = _at
ROWS = ["xattn_bo", "ffn_g1", "ffn_b1", "ffn_g2", "ffn_b2", "proj_b"]


def wge(eng, sem, value):
    if not isinstance(value, int) or value > 0:
        eng.wait_ge(sem, value)


def run_pipelined(eng, body, n, chain=None):
    base = chain.at if chain else 0
    body(0)
    per = chain.at - base if chain else 0
    if n > 2:
        with eng.Fori(1, n - 1) as i:
            if chain:
                chain.at = i * per + base
            body(i)
        if chain:
            assert isinstance(base, int)
            chain.at = base + (n - 1) * per
    body(n - 1)


def kv_first(maps):
    return [(0, m) for m in range(maps)] + [(0, "v")] + [(1, m) for m in range(maps)]


def kv_step(maps, u, last):
    b, first = u // 4, 2 * maps + 1 + u // 4 * (maps + 1)
    if last and b == 1:
        return []
    if u % 4 == 0:
        return [(b + 1, "v", first)]
    return [(b + 2, u % 4 - 1, first + u % 4)] if u % 4 <= maps and not last else []


class Chain:

    def __init__(self, eng, sem):
        self.eng, self.sem, self.at = eng, sem, 0

    def link(self, ins):
        ins.then_inc(self.sem, 1)
        self.at = self.at + 1
        self.eng.wait_ge(self.sem, self.at)


class Ring:

    def __init__(self, filled, drained, banks):
        self.filled, self.drained, self.banks = filled, drained, banks
        self.fills = self.drains = 0

    def to_fill(self, pe):
        wge(pe, self.drained, self.fills - len(self.banks) + 1)
        self.fills += 1
        return self.banks[(self.fills - 1) % len(self.banks)]

    def to_drain(self, eng):
        self.drains += 1
        eng.wait_ge(self.filled, self.drains)
        return self.banks[(self.drains - 1) % len(self.banks)]


def build(nc, a, out):
    ctx = ExitStack()
    with ctx:
        def sb(name, shape, dt=F32):
            return ctx.enter_context(nc.sbuf_tensor(name, shape, dt))

        def sem(name):
            return ctx.enter_context(nc.semaphore(name))

        X = sb("X", [P, TILES, D])
        KB = 1024
        slab = nc.sbuf_base
        sb("slab", [P, 68 * KB // 4])

        def at(name, kb, shape, dt=F32):
            return nc.alloc_sbuf_tensor_at(name, shape, dt, offset=slab + kb * KB)

        QT = at("QT", 0, [P, C, N])
        KT = at("KT", 8, [P, C, N])
        AT = at("AT", 16, [P, C, N])
        kts = at("kts", 24, [P, 2, 2, C, SK])
        qm = at("qm", 32, [P, 2, 2, C, HG, S])
        p1 = at("p1", 48, [P, 4, BANK])
        p2 = at("p2", 56, [P, 4, BANK])
        sm = p2
        pts = at("pts", 64, [P, 2, BANK])
        w_hi = at("w_hi", 0, [P, 4, WG], F32R)
        w_lo = at("w_lo", 32, [P, 4, WG], F32R)
        gwT = at("gwT", 64, [E, N])
        XN = sb("XN", [P, TILES, D])
        XT = sb("XT", [P, C, N])
        weights = sb("weights", [P, 2, 6, C, D])
        wgate = sb("wgate", [P, C, E])
        ctxs = sb("ctxs", [P, 2, C, SK])
        km = at("km", 24, [P, 2, 2, HG, S])
        qs = at("qs", 32, [P, 4, P])
        vs = sb("vs", [P, 2, 2, D])
        stat = sb("stat", [P, TILES, 6])
        mv = sb("mv", [P, TILES, 2])
        rstd = sb("rstd", [P, TILES])
        std = sb("std", [P, TILES])
        mx = sb("mx", [P, 4, 8])
        rs = sb("rs", [P, 4, 8])
        ri = sb("ri", [P, 2, 8])
        tmp = sb("tmp", [P, 2, S])
        vec = sb("vec", [P, NVEC])
        con = sb("con", [P, NCON])
        rows = sb("rows", [P, len(ROWS), D])
        bb2 = sb("bb2", [E, D])
        maskb = sb("maskb", [P, SK], U8)
        bias_x = sb("bias_x", [P, SK])
        lam = sb("lam", [P, 2 * PAIRS])
        big_a = sb("big_a", [P, 8192])
        slab = nc.sbuf_base
        big_b = sb("big_b", [P, 8192])
        xb_hi = at("xb_hi", 0, [P, 2, C, SLOTS], F32R)
        xb_lo = at("xb_lo", 4, [P, 2, C, SLOTS], F32R)
        gact = at("gact", 8, [P, 2, BANK])
        h_hi = at("h_hi", 12, [P, 2, BANK], F32R)
        h_lo = at("h_lo", 16, [P, 2, BANK], F32R)
        yb = at("yb", 20, [P, 2, 2, D])
        xs = at("xs", 24, [P, 2, 2, D])
        picked = big_b[:, :].rearrange("p (k t d) -> p k t d", k=2, t=2 * TILES)[:, :, 0:TILES, :]
        VT = big_a[:, 0:TILES * D].rearrange("p (t d) -> p t d", t=TILES)
        VH = big_a[:, TILES * D:3 * TILES * D].rearrange("p (t b d) -> p t b d", t=TILES, b=2)
        wraw = big_a[:, :].rearrange("p (s w) -> p s w", s=4)
        ps = ctx.enter_context(nc.psum_tensor("ps", [P, 8, BANK], F32))

        def v(name):
            lo, hi = VEC[name]
            return vec[:, lo:hi]

        def k(name):
            lo, hi = CON[name]
            return con[:, lo:hi]

        ident = k("ident")

        s_in = {n: sem("in_" + n) for n in ("x", "con", "vec", "rows", "mask", "bb2", "wg")}
        s_w = [sem(f"weights_in_{i}") for i in range(2)]
        s_tree_w = sem("tree_weights_in")
        s_out = sem("out_stored")
        s_dve = sem("vector_step")
        s_act = sem("scalar_step")
        s_pool = sem("gpsimd_step")
        s_var = sem("variance_ready")
        s_std = sem("deviation_ready")
        s_xn = sem("normalised_tile")
        s_xt = sem("transposed_block_in_sbuf")
        s_fa, s_da = sem("bank_filled_for_scalar"), sem("bank_drained_by_scalar")
        s_fd, s_dd = sem("bank_filled_for_vector"), sem("bank_drained_by_vector")
        s_resid = sem("bias_added_to_residual")
        s_w_free = sem("stage_weights_free")
        ringA = Ring(s_fa, s_da, [0, 1, 2, 3])
        ringD = Ring(s_fd, s_dd, [4, 5, 6, 7])

        names = ["l0x", "l0a", "l0f", "l1x"]
        st = {}
        for n in names:
            st[n] = {m: sem(f"{n}_{m}") for m in (
                "qk_ready", "qm_ready", "s_done", "mx_ready", "exp_done", "p_ready", "pt_filled", "pt_drained",
                "pv_done", "o_drained", "kv_drained", "ri_ready")
                + (("kv_filled", "ctx0", "ctx1", "even_ready") if n in ("l0x", "l1x") else ("v_ready", "v_doubled", "max_ready", "sum_ready"))
                + (("p2_ready",) if n == "l1x" else ("s_read",))}
        s_router = sem("router_ready")
        s_sel = sem("chosen_experts_ready")
        s_gw = sem("gate_weights_ready")
        s_gwT = sem("gate_weights_transposed")
        s_slot = sem("slots_ready")
        s_zero = sem("slots_zeroed")
        s_zmem = sem("zeros_ready")
        s_scat = sem("tokens_scattered")
        s_pick = [sem(f"outputs_picked_{t}") for t in range(TILES)]
        s_e_in = [sem(f"expert_weights_in_{i}") for i in range(4)]
        s_b_in = [sem(f"hidden_biases_in_{i}") for i in range(2)]
        s_x_in = [sem(f"block_tokens_in_{i}") for i in range(2)]
        s_xbT = sem("block_tokens_transposed")
        s_xhi = sem("block_tokens_rounded")
        s_xlo = sem("block_tokens_split")
        s_whi = sem("weights_rounded")
        s_wlo = sem("weights_split")
        s_hid = sem("hidden_filled")
        s_gelu = sem("gelu_done")
        s_hhi = sem("hidden_rounded")
        s_h1 = sem("hidden_split")
        s_y = sem("expert_unit_done")
        s_yev = sem("block_output_in_sbuf")
        s_ys = [sem(f"block_output_stored_{b}") for b in range(2)]
        s_ret = sem("retention_ready")
        s_sq = sem("squares_ready")
        s_norm = sem("rms_ready")
        s_projw = sem("scaled_projection_ready")
        s_xslot = sem("tile_copied")
        s_logit = sem("logits_filled")
        s_lread = sem("logits_read")
        s_silu = sem("silu_done")
        s_path = sem("path_masked")
        s_tt = sem("tree_block_transposed")
        s_tc = sem("tree_block_in_sbuf")
        s_ty = sem("tree_out_filled")
        s_tx = sem("tree_out_added")

        W = {"l0x": weights[:, 0], "l0a": weights[:, 1], "l0f": weights[:, 0], "l1x": weights[:, 1], "l1a": weights[:, 0]}
        WSLOT = {"l0x": (0, 16), "l0a": (1, 16), "l0f": (0, 32), "l1x": (1, 32), "l1a": (0, 48)}

        win = big_a[:, 0:C * WIDTH].rearrange("p (c w) -> p c w", c=C)
        wout = big_a[:, 4096:8192].rearrange("p (j d) -> p j d", j=NB)
        qm_flat = qm[:].rearrange("p a b c h s -> p (a b c h s)")
        bin_b = qm_flat[:, 0:WIDTH]
        mT = qm_flat[:, 2048:4096].rearrange("p (j t) -> p j t", j=NB)
        logit, dec, path, acts = (big_b[:, 2048 * i:2048 * i + WIDTH] for i in range(4))
        xslot = ctxs[:, 0].rearrange("p c n -> p (c n)")[:, 0:2 * P].rearrange("p (c n) -> p c n", c=C)

        gw = sb("gw", [P, TILES, E])
        router = sb("router", [P, 4, TILES, E])
        rk = sm[:, 0:2, :]
        bb1s = sb("bb1s", [P, 2, M])
        rt = sb("rt", [P, 6, TILES * E])
        off = sb("off", [P, TILES + 1, E])
        rb = sb("rb", [P, 6, E])
        rc = sb("rc", [P, NBLK * E])
        gate = sb("gate", [P, TOP, TILES])
        slotf = sb("slotf", [P, TOP, TILES])
        slot = sb("slot", [P, TOP, TILES], I32)
        blkf = sb("blkf", [P, NBLK])
        blk = sb("blk", [P, NBLK], I32)
        moe_in = nc.dram_tensor("moe_in", (NSLOT, D), F32, kind="Internal").ap()
        moe_out = nc.dram_tensor("moe_out", (NSLOT, D), F32, kind="Internal").ap()
        dk = sb("dk", [P, 8])

        PAIRS_B = (NBLK + 1) // 2

        def run_blocks(eng, body):
            body(0)
            with eng.Fori(1, PAIRS_B - 2) as i:
                body(i)
            body(PAIRS_B - 2)
            body(PAIRS_B - 1)

        def left(i, u):
            return not isinstance(i, int) or i * 2 * UB + u < NBLK * UB

        block = ctx.enter_context(nc.Block())

        @block.sync
        def _(sp):
            sp.dma_start(con[:], a["con"]).then_inc(s_in["con"], 16)
            sp.dma_start(X[:], a["x"].rearrange("b s d -> (b s) d").rearrange("(t p) d -> p t d", p=P)).then_inc(s_in["x"], 16)
            sp.dma_start(W["l0x"][:, 0:4], a["w_l0x"].rearrange("p (w c d) -> p w c d", w=4, c=C)).then_inc(s_w[0], 16)
            sp.dma_start(vec[:], a["vec"]).then_inc(s_in["vec"], 16)
            sp.dma_start(maskb[:], a["mask"]).then_inc(s_in["mask"], 16)

            def load_ctx(s, b, sl):
                dst = ctxs[:, sl]
                src = a["ctxT"][b] if isinstance(b, int) else a["ctxT"][bass.ds(b, 1)].rearrange("o p n -> (o p) n")
                sp.dma_start(dst, src.rearrange("p (c n) -> p c n", c=C)).then_inc(s[f"ctx{sl}"], 16)

            def ctx_loop(s, fills):
                load_ctx(s, 0, 0)
                load_ctx(s, 1, 1)

                def body(i):
                    for sl in range(2):
                        sp.wait_ge(s["kv_filled"], i * (2 * fills) + fills * (sl + 1))
                        load_ctx(s, i * 2 + 2 + sl, sl)
                with sp.Fori(0, B // 2 - 1) as i:
                    body(i)

            def double_values(s):
                sp.wait_ge(s["kv_drained"], 4)
                for half in range(2):
                    for b in range(2):
                        sp.dma_start(VH[half * S:(half + 1) * S, :, b, :], VT[b * S:(b + 1) * S]).then_inc(s["v_doubled"], 16)

            load_ctx_first = st["l0x"]
            sp.dma_start(rows[:], a["rows"].partition_broadcast(P).rearrange("p (r d) -> p r d", d=D)).then_inc(s_in["rows"], 16)
            sp.dma_start(W["l0a"][:, 0:6], a["w_l0a"].rearrange("p (w c d) -> p w c d", w=6, c=C)).then_inc(s_w[1], 16)
            ctx_loop(load_ctx_first, 2)
            sp.wait_ge(s_zmem, 1)
            sp.dma_start(moe_in.rearrange("(p a) d -> p (a d)", p=P), big_b[:, 0:NSLOT // P * D]).then_inc(s_zero, 16)
            for n, key, dst in (("bb2", "bb2", bb2[:]), ("wg", "wg", wgate[:].rearrange("p c e -> p (c e)"))):
                sp.dma_start(dst, a[key]).then_inc(s_in[n], 16)

            sp.wait_ge(s_w_free, 1)
            sp.dma_start(W["l0f"][:, 0:4], a["w_l0f"].rearrange("p (w c d) -> p w c d", w=4, c=C)).then_inc(s_w[0], 16)
            double_values(st["l0a"])
            sp.wait_ge(s_w_free, 2)
            sp.dma_start(W["l1x"][:, 0:6], a["w_l1x"].rearrange("p (w c d) -> p w c d", w=6, c=C)).then_inc(s_w[1], 16)
            double_values(st["l0f"])
            sp.wait_ge(s_w_free, 3)
            sp.dma_start(W["l1a"][:, 0], a["w_l1a"].rearrange("p (c d) -> p c d", c=C)).then_inc(s_w[0], 16)
            sp.wait_ge(s_slot, 1)

            def load_block(i, b):
                e = sp.value_load(blk[0:1, bass.ds(i * 2 + b, 1)], min_val=0, max_val=E - 1)
                for g in range(2):
                    sl = 2 * b + g
                    wge(sp, s_wlo, i * 4 * CH + (sl - 3) * CH)
                    sp.dma_start(wraw[:, sl, :], a["we"][bass.ds(e * 2 + g, 1)].rearrange("o p n -> (o p) n")).then_inc(s_e_in[sl], 16)
                    if g == 0:
                        if isinstance(i, int) and i == 0 and b == 0:
                            sp.wait_ge(s_scat, 16 * TOP * TILES)
                        wge(sp, s_xbT, i * 2 + b - 1)
                        src = moe_in.rearrange("(b s p) d -> b p s d", s=2, p=P)[bass.ds(i * 2 + b, 1)].rearrange("o p s d -> (o p) s d")
                        sp.dma_start(xs[:, b], src).then_inc(s_x_in[b], 16)
                wge(sp, s_gelu, i * 2 * UB + (b - 1) * UB)
                sp.dma_start(bb1s[:, b, :], a["bb1"][bass.ds(e, 1)].rearrange("o p m -> (o p) m")).then_inc(s_b_in[b], 16)

            def load_blocks(i):
                for b in range(2):
                    if not (isinstance(i, int) and i * 2 + b >= NBLK):
                        load_block(i, b)
            run_pipelined(sp, load_blocks, (NBLK + 1) // 2)
            ctx_loop(st["l1x"], 3)
            sp.wait_ge(s_y, NBLK * UB)
            sp.dma_start(win[:], a["w_in"].rearrange("p (c w) -> p c w", c=C)).then_inc(s_tree_w, 16)
            sp.dma_start(wout[:], a["w_out"].rearrange("p (j d) -> p j d", j=NB)).then_inc(s_tree_w, 16)
            sp.wait_ge(st["l1x"]["s_done"], B * 4)
            sp.dma_start(bin_b, a["b_in"].partition_broadcast(P)).then_inc(s_tree_w, 16)
            sp.wait_ge(s_tx, TILES)
            sp.dma_start(out.rearrange("b s d -> (b s) d").rearrange("(t p) d -> p t d", p=P), X[:]).then_inc(s_out, 16)
            sp.wait_ge(s_out, 16)

        @block.tensor
        def _(pe):
            ln = [0]

            def transpose_tokens():
                for t in range(TILES):
                    pe.wait_ge(s_xn, ln[0] * TILES + t + 1)
                    if t % 2 == 0:
                        bank = ringA.to_fill(pe)
                    for c in range(C):
                        i = pe.transpose(ps[:, bank, (t % 2 * C + c) * P:(t % 2 * C + c + 1) * P], XN[:, t, c * P:(c + 1) * P], ident)
                    if t % 2:
                        i.then_inc(s_fa, 1)
                ln[0] += 1
                pe.wait_ge(s_xt, ln[0] * TILES // 2)

            def project_features(w, ring, src=XT):
                for o in range(C):
                    for h in range(2):
                        bank = ring.to_fill(pe)
                        for c in range(C):
                            i = pe.matmul(ps[:, bank, :], w[:, c, o * P:(o + 1) * P], src[:, c, h * BANK:(h + 1) * BANK],
                                          start=(c == 0), stop=(c == C - 1))
                        i.then_inc(ring.filled, 1)

            def project_tokens(w, ring, src, free=None):
                for t in range(TILES):
                    if t % 2 == 0:
                        bank = ring.to_fill(pe)
                    for c in range(C):
                        i = pe.matmul(ps[:, bank, t % 2 * D:(t % 2 + 1) * D], src[:, c, t * P:(t + 1) * P], w[:, c, :],
                                      start=(c == 0), stop=(c == C - 1))
                    if t % 2:
                        i.then_inc(ring.filled, 1)
                if free:
                    pe.wait_ge(ring.filled, ring.fills)
                    pe.sem_inc(free, 1)

            def cross(s, maps, wk, lag_ring):
                wv = s["wv"]
                fills = maps + 1

                def project_kv(i, b, item, at):
                    sl = b % 2
                    pe.wait_ge(s[f"ctx{sl}"], (i + b // 2) * 16 + 16)
                    wge(pe, s["kv_drained"], at)
                    if item == "v":
                        for half in range(2):
                            for c in range(C):
                                m = pe.matmul(ps[:, 7, half * D:(half + 1) * D], ctxs[:, sl, c, half * P:(half + 1) * P],
                                              wv[:, c, :], start=(c == 0), stop=(c == C - 1))
                    else:
                        for o in range(C):
                            for c in range(C):
                                m = pe.matmul(ps[:, 7, o * SK:(o + 1) * SK], wk[item][:, c, o * P:(o + 1) * P], ctxs[:, sl, c, :],
                                              start=(c == 0), stop=(c == C - 1))
                    m.then_inc(s["kv_filled"], 1)

                def scores(i, u):
                    U, sl, g, hp = i * 8 + u, u // 4 % 2, u // 2 % 2, u % 2
                    pe.wait_ge(s["qm_ready"], i * 4 + u // 2 + 1)
                    pe.wait_ge(s["kv_drained"], (i * 2 + u // 4 + 1) * fills - 1)
                    wge(pe, s["s_read"] if maps == 1 else s["exp_done"], U - lag_ring + 1)
                    for mp in range(maps):
                        bank = (u % lag_ring) * maps + mp
                        for j in range(2):
                            pr = hp * 2 + j
                            lhs = qm[:, sl, mp, g, 2 * pr:2 * pr + 2, :].rearrange("p h s -> p (h s)")
                            m = pe.matmul(ps[:, bank, j * SK:(j + 1) * SK], lhs, kts[:, sl, mp, g, :], start=True, stop=True)
                    m.then_inc(s["s_done"], 1)

                def transposes(i, u):
                    U = i * 8 + u
                    pe.wait_ge(s["p_ready"], U + 1)
                    wge(pe, s["pt_drained"], U - 1)
                    for j in range(2):
                        for half in range(2):
                            m = pe.transpose(ps[:, 4 + u % 2, (j * 2 + half) * P:(j * 2 + half + 1) * P],
                                             p1[:, u % 4, j * SK + half * P:j * SK + (half + 1) * P], ident)
                    m.then_inc(s["pt_filled"], 1)

                def values(i, u):
                    U, sl, g, hp = i * 8 + u, u // 4 % 2, u // 2 % 2, u % 2
                    pe.wait_ge(s["pt_drained"], U + 1)
                    pe.wait_ge(s["kv_drained"], (i * 2 + u // 4 + 1) * fills)
                    if hp == 0:
                        wge(pe, s["o_drained"], i * 4 + u // 2)
                    for j in range(2):
                        pr = hp * 2 + j
                        for half in range(2):
                            m = pe.matmul(ps[32 * pr:32 * pr + 32, 6, 0:P], vs[:, sl, half, g * P + 32 * pr:g * P + 32 * pr + 32],
                                          pts[:, u % 2, (j * 2 + half) * P:(j * 2 + half + 1) * P],
                                          start=(half == 0), stop=(half == 1), tile_position=(0, 32 * pr))
                    m.then_inc(s["pv_done"], 1)

                for n, (b, item) in enumerate(kv_first(maps)):
                    project_kv(0, b, item, n)
                for u in range(4):
                    scores(0, u)
                transposes(0, 0)

                def body(i):
                    last = isinstance(i, int) and i == B // 2 - 1
                    for u in range(8):
                        if not (last and u + 4 >= 8):
                            scores(i, u + 4)
                        if not (last and u + 1 >= 8):
                            transposes(i, u + 1)
                        values(i, u)
                        for b, item, n in kv_step(maps, u, last):
                            project_kv(i, b, item, i * 2 * fills + n)
                run_pipelined(pe, body, B // 2)

            def self_attention(s):
                def scores(i, u):
                    U = i * 4 + u
                    pe.wait_ge(s["qm_ready"], U + 1)
                    wge(pe, s["s_read"], U - 3)
                    for b in range(2):
                        m = pe.matmul(ps[b * S:(b + 1) * S, u % 4, :], qs[:, u % 4, b * S:(b + 1) * S],
                                      km[:, u % 2, b].rearrange("p h s -> p (h s)"), start=True, stop=True, tile_position=(0, b * S))
                    m.then_inc(s["s_done"], 1)

                def transposes(i, u):
                    U = i * 4 + u
                    pe.wait_ge(s["p_ready"], U + 1)
                    wge(pe, s["pt_drained"], U - 1)
                    for pr in range(PAIRS):
                        m = pe.transpose(ps[:, 4 + u % 2, pr * P:(pr + 1) * P], p1[:, u % 4, pr * P:(pr + 1) * P], ident)
                    m.then_inc(s["pt_filled"], 1)

                def values(i, u):
                    U, g = i * 4 + u, u % 2
                    pe.wait_ge(s["pt_drained"], U + 1)
                    pe.wait_ge(s["v_ready"], i * 2 + u // 2 + 1)
                    wge(pe, s["o_drained"], U - 1)
                    for b in range(2):
                        for pr in range(PAIRS):
                            m = pe.matmul(ps[32 * pr:32 * pr + 32, 6 + u % 2, b * S:(b + 1) * S],
                                          vs[:, u // 2 % 2, b, g * P + 32 * pr:g * P + 32 * pr + 32],
                                          pts[:, u % 2, pr * P + b * S:pr * P + (b + 1) * S], start=True, stop=True,
                                          tile_position=(0, 32 * pr))
                    m.then_inc(s["pv_done"], 1)

                for u in range(4):
                    scores(0, u)
                transposes(0, 0)
                n = TILES // 2

                def body(i):
                    last = isinstance(i, int) and i == n - 1
                    for u in range(4):
                        if not last:
                            scores(i, u + 4)
                        if not (last and u + 1 >= 4):
                            transposes(i, u + 1)
                        values(i, u)
                run_pipelined(pe, body, n)

            def wait_weights(n):
                pe.wait_ge(s_w[WSLOT[n][0]], WSLOT[n][1])

            pe.wait_ge(s_in["con"], 16)
            transpose_tokens()
            wait_weights("l0x")
            w = W["l0x"]
            project_features(w[:, 0], ringA)
            s = st["l0x"]
            s["wv"] = w[:, 2]
            pe.wait_ge(s["qk_ready"], 4)
            cross(s, 1, [w[:, 1]], 4)
            pe.wait_ge(s["o_drained"], B * C)
            project_tokens(w[:, 3], ringD, AT, s_w_free)

            transpose_tokens()
            wait_weights("l0a")
            w = W["l0a"]
            for o in range(C):
                for h in range(2):
                    for n in (0, 3, 1, 4):
                        bank = ringD.to_fill(pe)
                        for c in range(C):
                            i = pe.matmul(ps[:, bank, :], w[:, n, c, o * P:(o + 1) * P], XT[:, c, h * BANK:(h + 1) * BANK],
                                          start=(c == 0), stop=(c == C - 1))
                        i.then_inc(s_fd, 1)
            project_tokens(w[:, 2], ringA, XT)
            s = st["l0a"]
            pe.wait_ge(s["qk_ready"], 1)
            pe.wait_ge(s["kv_drained"], 4)
            self_attention(s)
            pe.wait_ge(s["o_drained"], TILES * C)
            project_tokens(w[:, 5], ringD, AT, s_w_free)

            transpose_tokens()
            wait_weights("l0f")
            w = W["l0f"]
            project_features(w[:, 0], ringA)
            project_features(w[:, 1], ringA)
            project_tokens(w[:, 2], ringA, XT)
            s = st["l0f"]
            pe.wait_ge(s["qk_ready"], 8)
            pe.wait_ge(s["kv_drained"], 4)
            self_attention(s)
            pe.wait_ge(s["o_drained"], TILES * C)
            project_tokens(w[:, 3], ringD, AT, s_w_free)
            transpose_tokens()
            bank = ringD.to_fill(pe)
            pe.wait_ge(s_in["wg"], 16)
            for t in range(TILES):
                for c in range(C):
                    i = pe.matmul(ps[:, bank, t * E:(t + 1) * E], XT[:, c, t * P:(t + 1) * P], wgate[:, c, :],
                                  start=(c == 0), stop=(c == C - 1))
            i.then_inc(s_fd, 1)
            pe.wait_ge(s_sel, 1)
            bank = ringD.to_fill(pe)
            pe.matmul(ps[:, bank, 0:TILES * E], k("earlier"), rt[:, 0, :], start=True, stop=True)
            pe.matmul(ps[:, bank, TILES * E:2 * TILES * E], k("all"), rt[:, 0, :], start=True, stop=True).then_inc(s_fd, 1)
            pe.wait_ge(s_gw, 1)
            for h in range(2):
                bank = ringA.to_fill(pe)
                for t in range(4):
                    i = pe.transpose(ps[0:E, bank, t * P:(t + 1) * P], gw[:, h * 4 + t, :], ident)
                i.then_inc(s_fa, 1)
            pe.wait_ge(s_gwT, 2)
            pe.wait_ge(s_in["bb2"], 16)
            for t in range(TILES):
                if t % 2 == 0:
                    bank = ringD.to_fill(pe)
                i = pe.matmul(ps[:, bank, t % 2 * D:(t % 2 + 1) * D], gwT[:, t * P:(t + 1) * P], bb2[:], start=True, stop=True)
                if t % 2:
                    i.then_inc(s_fd, 1)
            pe.wait_ge(s_dd, ringD.fills)

            def three_passes(out, w, w0, x, x0, start, stop):
                for n, (wp, xp) in enumerate(((0, 0), (0, 1), (1, 0))):
                    i = pe.matmul(out, w[wp][w0], x[xp][x0], start=start and n == 0, stop=stop and n == 2)
                return i

            def block_tokens(i, b):
                sl = b % 2
                pe.wait_ge(s_x_in[sl], i * 16 + (b // 2 + 1) * 16)
                wge(pe, s_xlo, i * 2 + b)
                for c in range(C):
                    for half in range(2):
                        x = pe.transpose(ps[:, 6, (c * 2 + half) * P:(c * 2 + half + 1) * P], xs[:, sl, half, c * P:(c + 1) * P], ident)
                x.then_inc(s_xbT, 1)

            def hidden(i, u):
                sl, b = u // 2 % 4, u // UB % 2
                if u % 2 == 0:
                    pe.wait_ge(s_wlo, i * 4 * CH + (u // 2 + 1) * CH)
                if u % UB == 0:
                    pe.wait_ge(s_xlo, i * 2 + u // UB + 1)
                wge(pe, s_gelu, i * 2 * UB + u - 3)
                for mm in range(2):
                    m = u % 2 * 2 + mm
                    for c in range(C):
                        x = three_passes(ps[:, u % 4, mm * SLOTS:(mm + 1) * SLOTS],
                                         (w_hi, w_lo), (slice(None), sl, slice((c * MG + m) * P, (c * MG + m + 1) * P)),
                                         (xb_hi, xb_lo), (slice(None), b, c, slice(None)), c == 0, c == C - 1)
                x.then_inc(s_hid, 1)

            def expert_out(i, u):
                sl, b = u // 2 % 4, u // UB % 2
                pe.wait_ge(s_h1, i * 2 * UB + u + 1)
                if u % UB == 0:
                    wge(pe, s_yev, i * 2 + u // UB - 1)
                for mm in range(2):
                    at0 = C * MG * P + (u % 2 * 2 + mm) * D
                    for half in range(2):
                        for n, (hp, wp) in enumerate(((h_hi, w_hi), (h_hi, w_lo), (h_lo, w_hi))):
                            first = u % UB == 0 and mm == 0 and half == 0 and n == 0
                            x = pe.matmul(ps[:, 4 + b, half * D:(half + 1) * D],
                                          hp[:, u % 2, mm * SLOTS + half * P:mm * SLOTS + (half + 1) * P],
                                          wp[:, sl, at0:at0 + D], start=first, stop=(u % UB == UB - 1 and mm == 1 and n == 2),
                                          skip_group_check=True)
                x.then_inc(s_y, 1)

            def experts(i):
                for u in range(2 * UB):
                    if u % UB == 2 and left(i, (u // UB + 2) * UB):
                        block_tokens(i, u // UB + 2)
                    if left(i, u + 3):
                        hidden(i, u + 3)
                    if left(i, u):
                        expert_out(i, u)
            block_tokens(0, 0)
            block_tokens(0, 1)
            for u in range(3):
                hidden(0, u)
            run_blocks(pe, experts)

            transpose_tokens()
            wait_weights("l1x")
            w = W["l1x"]
            project_features(w[:, 0], ringA)
            project_features(w[:, 1], ringA)
            s = st["l1x"]
            s["wv"] = w[:, 3]
            pe.wait_ge(s["qk_ready"], 8)
            cross(s, 2, [w[:, 2], w[:, 4]], 2)
            pe.wait_ge(s["o_drained"], B * C)
            pe.wait_ge(s_sq, 1)
            bank = ringD.to_fill(pe)
            for t in range(TILES):
                for c in range(C):
                    i = pe.matmul(ps[:, bank, t:t + 1], QT[:, c, t * P:(t + 1) * P], k("ones"), start=(c == 0), stop=(c == C - 1))
            i.then_inc(s_fd, 1)
            pe.wait_ge(s_projw, 1)
            project_tokens(w[:, 5], ringD, AT)

            transpose_tokens()
            wait_weights("l1a")
            pe.wait_ge(s_ret, 1)
            project_features(W["l1a"][:, 0], ringD, KT)
            pe.wait_ge(s_ret, 2)
            for t in range(TILES):
                if t % 2 == 0:
                    bank = ringD.to_fill(pe)
                for c in range(C):
                    i = pe.transpose(ps[:, bank, (t % 2 * C + c) * P:(t % 2 * C + c + 1) * P], AT[:, c, t * P:(t + 1) * P], ident)
                if t % 2:
                    i.then_inc(s_fd, 1)

            transpose_tokens()
            pe.wait_ge(s_tree_w, 48)

            def tree_logits(i):
                pe.wait_ge(s_xslot, i + 1)
                wge(pe, s_lread, i)
                for q in range(4):
                    w0 = q * (WIDTH // 4)
                    for c in range(C):
                        m = pe.matmul(ps[:, q, 0:WIDTH // 4], xslot[:, c, :], win[:, c, w0:w0 + WIDTH // 4],
                                      start=(c == 0), stop=(c == C - 1))
                m.then_inc(s_logit, 1)

            def tree_rest(i, last):
                if not last:
                    tree_logits(i + 1)
                pe.wait_ge(s_path, i + 1)
                for q in range(4):
                    wge(pe, s_tc, i * 4 + q - 1)
                    for j in range(4):
                        n = q * 4 + j
                        rows_n = min(P, WIDTH - n * P)
                        m = pe.transpose(ps[0:rows_n, 4 + q % 2, j * P:(j + 1) * P], acts[:, n * P:n * P + rows_n], ident)
                    m.then_inc(s_tt, 1)
                pe.wait_ge(s_tc, i * 4 + 4)
                wge(pe, s_tx, i)
                for n in range(NB):
                    rows_n = min(P, WIDTH - n * P)
                    m = pe.matmul(ps[:, 6, 0:D], mT[0:rows_n, n, :], wout[0:rows_n, n, :], start=(n == 0), stop=(n == NB - 1))
                m.then_inc(s_ty, 1)

            tree_logits(0)
            run_pipelined(pe, lambda i: tree_rest(i, isinstance(i, int) and i == TILES - 1), TILES)


        @block.scalar
        def _(act):
            chain = Chain(act, s_act)
            ln = [0]

            def deviation():
                ln[0] += 1
                act.wait_ge(s_var, ln[0])
                act.activation(std[:], rstd[:], ACT.Sqrt).then_inc(s_std, 1)

            def drain_transposes():
                for tt in range(TILES // 2):
                    bank = ringA.to_drain(act)
                    src = ps[:, bank, :].rearrange("p (t c n) -> p t c n", t=2, c=C)
                    dst = XT[:, :, tt * 2 * P:(tt + 1) * 2 * P].rearrange("p c (t n) -> p t c n", t=2)
                    act.activation(dst, src, ACT.Copy).then_inc(s_xt, 1)
                    act.wait_ge(s_xt, ln_x[0] * TILES // 2 + tt + 1)
                    act.sem_inc(s_da, 1)
                ln_x[0] += 1
            ln_x = [0]

            def drain_features(dst, done, bias=None):
                for o in range(C):
                    for h in range(2):
                        bank = ringA.to_drain(act)
                        d = dst[:, o, h * BANK:(h + 1) * BANK]
                        if bias is None:
                            i = act.activation(d, ps[:, bank, :], ACT.Copy)
                        else:
                            i = act.activation(d, ps[:, bank, :], ACT.Identity, bias=bias[:, o:o + 1])
                        i.then_inc(s_da, 1)
                act.wait_ge(s_da, ringA.drains)
                act.sem_inc(done, 4)

            def drain_tokens(dst, done):
                for tt in range(TILES // 2):
                    bank = ringA.to_drain(act)
                    act.activation(dst[:, 2 * tt:2 * tt + 2, :].rearrange("p t d -> p (t d)"), ps[:, bank, :], ACT.Copy).then_inc(s_da, 1)
                act.wait_ge(s_da, ringA.drains)
                act.sem_inc(done, 4)

            def cross(s, maps, bias):
                fills = maps + 1

                def drain_kv(b, item, at):
                    sl = b % 2
                    act.wait_ge(s["kv_filled"], at + 1)
                    if item == "v":
                        x = act.activation(vs[:, sl].rearrange("p h d -> p (h d)"), ps[:, 7, :], ACT.Copy)
                    elif bias is None:
                        x = act.activation(kts[:, sl, item].rearrange("p c n -> p (c n)"), ps[:, 7, :], ACT.Copy)
                    else:
                        for o in range(C):
                            x = act.activation(kts[:, sl, item, o], ps[:, 7, o * SK:(o + 1) * SK], ACT.Identity, bias=bias[:, o:o + 1])
                    x.then_inc(s["kv_drained"], 1)

                def exps(i, u):
                    U = i * 8 + u
                    act.wait_ge(s["mx_ready"], U + 1)
                    for mp in range(maps):
                        for j in range(2):
                            if maps == 1:
                                src = sm[:, u % 4, j * SK:(j + 1) * SK]
                            else:
                                src = ps[:, (u % 2) * 2 + mp, j * SK:(j + 1) * SK]
                            dst = (p1, p2)[mp][:, u % 4, j * SK:(j + 1) * SK]
                            n = mp * 2 + j
                            x = act.activation(dst, src, ACT.Exp, bias=mx[:, u % 4, n:n + 1],
                                               accum_out=rs[:, u % 4, n:n + 1])
                    x.then_inc(s["exp_done"], 1)

                def evac(i, u):
                    U = i * 8 + u
                    act.wait_ge(s["pt_filled"], U + 1)
                    wge(act, s["pv_done"], U - 1)
                    act.activation(pts[:, u % 2, :], ps[:, 4 + u % 2, :], ACT.Copy).then_inc(s["pt_drained"], 1)

                for n, (b, item) in enumerate(kv_first(maps)):
                    drain_kv(b, item, n)
                for u in range(4):
                    exps(0, u)
                evac(0, 0)

                def body(i):
                    last = isinstance(i, int) and i == B // 2 - 1
                    for u in range(8):
                        if not (last and u + 1 >= 8):
                            evac(i, u + 1)
                        if not (last and u + 4 >= 8):
                            exps(i, u + 4)
                        for b, item, n in kv_step(maps, u, last):
                            drain_kv(b, item, i * 2 * fills + n)
                run_pipelined(act, body, B // 2)

            def self_attention(s):
                def exps(i, u):
                    U = i * 4 + u
                    act.wait_ge(s["mx_ready"], U + 1)
                    act.activation(p1[:, u % 4, :], sm[:, u % 4, :], ACT.Exp).then_inc(s["exp_done"], 1)

                def evac(i, u):
                    U = i * 4 + u
                    act.wait_ge(s["pt_filled"], U + 1)
                    wge(act, s["pv_done"], U - 1)
                    act.activation(pts[:, u % 2, :], ps[:, 4 + u % 2, :], ACT.Copy).then_inc(s["pt_drained"], 1)

                for u in range(4):
                    exps(0, u)
                evac(0, 0)
                n = TILES // 2

                def body(i):
                    last = isinstance(i, int) and i == n - 1
                    for u in range(4):
                        if not (last and u + 1 >= 4):
                            evac(i, u + 1)
                        if not last:
                            exps(i, u + 4)
                run_pipelined(act, body, n)

            deviation()
            drain_transposes()
            act.wait_ge(s_in["vec"], 16)
            drain_features(QT, st["l0x"]["qk_ready"], v("bq"))
            cross(st["l0x"], 1, v("bk"))
            deviation()
            drain_transposes()
            drain_tokens(VT, st["l0a"]["kv_drained"])
            self_attention(st["l0a"])
            deviation()
            drain_transposes()
            drain_features(QT, st["l0f"]["qk_ready"])
            drain_features(KT, st["l0f"]["qk_ready"])
            drain_tokens(VT, st["l0f"]["kv_drained"])
            self_attention(st["l0f"])
            deviation()
            drain_transposes()
            act.wait_ge(s_router, 1)
            act.activation(router[:, 1], router[:, 0], ACT.Exp).then_inc(s_router, 1)
            for h in range(2):
                bank = ringA.to_drain(act)
                act.activation(gwT[:, h * BANK:(h + 1) * BANK], ps[0:E, bank, :], ACT.Copy).then_inc(s_da, 1)
                act.wait_ge(s_da, ringA.drains)
                act.sem_inc(s_gwT, 1)

            def round_tokens(i, b):
                sl = b % 2
                act.wait_ge(s_xbT, i * 2 + b + 1)
                act.activation(xb_hi[:, sl].rearrange("p c n -> p (c n)"), ps[:, 6, :], ACT.Copy).then_inc(s_xhi, 1)

            def gelu(i, u):
                b = u // UB
                act.wait_ge(s_hid, i * 2 * UB + u + 1)
                wge(act, s_h1, i * 2 * UB + u - 1)
                if u % UB == 0:
                    act.wait_ge(s_b_in[b % 2], i * 16 + (b // 2 + 1) * 16)
                for mm in range(2):
                    m = u % UB * 2 + mm
                    x = act.activation(gact[:, u % 2, mm * SLOTS:(mm + 1) * SLOTS], ps[:, u % 4, mm * SLOTS:(mm + 1) * SLOTS],
                                       ACT.Gelu_apprx_tanh, bias=bb1s[:, b % 2, m:m + 1])
                x.then_inc(s_gelu, 1)

            def round_hidden(i, u):
                act.wait_ge(s_gelu, i * 2 * UB + u + 1)
                wge(act, s_y, i * 2 * UB + u - 1)
                act.activation(h_hi[:, u % 2, :], gact[:, u % 2, :], ACT.Copy).then_inc(s_hhi, 1)

            def store_block(i, b):
                sl = b % 2
                act.wait_ge(s_y, (i * 2 + b + 1) * UB)
                if b == 0:
                    wge(act, s_ys[0], i * 16)
                    wge(act, s_ys[1], i * 16)
                act.activation(yb[:, sl].rearrange("p s d -> p (s d)"), ps[:, 4 + sl, :], ACT.Copy).then_inc(s_yev, 1)
                act.wait_ge(s_yev, i * 2 + b + 1)
                dst = moe_out.rearrange("(b s p) d -> b p s d", s=2, p=P)[bass.ds(i * 2 + b, 1)].rearrange("o p s d -> (o p) s d")
                act.dma_start(dst, yb[:, sl]).then_inc(s_ys[sl], 16)

            def gelus(i):
                for u in range(2 * UB):
                    if left(i, u + 2):
                        gelu(i, u + 2)
                    if left(i, u + 1):
                        round_hidden(i, u + 1)
                    if u % UB == 0 and left(i, u - UB) and not (isinstance(i, int) and i == 0 and u == 0):
                        store_block(i, u // UB - 1)
                    if u % UB == 2 and left(i, (u // UB + 2) * UB):
                        round_tokens(i, u // UB + 2)
            round_tokens(0, 0)
            round_tokens(0, 1)
            gelu(0, 0)
            gelu(0, 1)
            round_hidden(0, 0)
            run_blocks(act, gelus)
            deviation()
            deviation()
            drain_transposes()
            drain_features(QT, st["l1x"]["qk_ready"])
            drain_features(KT, st["l1x"]["qk_ready"])
            cross(st["l1x"], 2, None)
            act.wait_ge(st["l1x"]["o_drained"], B * C)
            act.activation(QT[:], AT[:], ACT.Square).then_inc(s_sq, 1)
            deviation()
            act.wait_ge(s_in["vec"], 16)
            act.activation(dk[:, 0:2], v("decay"), ACT.Exp, scale=-1.0).then_inc(s_norm, 1)
            deviation()
            drain_transposes()
            deviation()
            drain_transposes()

            def trees(i):
                act.wait_ge(s_lread, i + 1)
                act.activation(acts, logit, ACT.Silu).then_inc(s_silu, 1)
                for q in range(4):
                    act.wait_ge(s_tt, i * 4 + q + 1)
                    if q == 0:
                        wge(act, s_ty, i)
                    full = 4 if q < 3 else 3
                    x = act.activation(mT[:, 4 * q:4 * q + full, :].rearrange("p j t -> p (j t)"), ps[:, 4 + q % 2, 0:full * P], ACT.Copy)
                    if q == 3:
                        r = WIDTH - (NB - 1) * P
                        x = act.activation(mT[0:r, NB - 1, :], ps[0:r, 4 + q % 2, 3 * P:4 * P], ACT.Copy)
                    x.then_inc(s_tc, 1)
            run_pipelined(act, trees, TILES)


        @block.vector
        def _(dve):
            chain = Chain(dve, s_dve)
            link = chain.link
            ln = [0]

            def stats(src):
                for t in range(TILES):
                    i = dve.bn_stats(stat[:, t, :], src[:, t, :])
                link(i)
                for t in range(TILES):
                    i = dve.bn_aggr(mv[:, t, :], stat[:, t, :])
                link(i)
                ln[0] += 1
                dve.tensor_scalar(rstd[:], mv[:, :, 1], 1e-5, None, ALU.add).then_inc(s_var, 1)
                dve.wait_ge(s_std, ln[0])
                link(dve.reciprocal(rstd[:], std[:]))

            def normalise(src, dst, done=None):
                for t in range(TILES):
                    i = dve.tensor_scalar(dst[:, t, :], src[:, t, :], mv[:, t, 0:1], rstd[:, t:t + 1], ALU.subtract, ALU.mult)
                    if done is not None:
                        i.then_inc(done, 1)
                if done is None:
                    link(i)

            def row(n):
                return rows[:, ROWS.index(n), :].unsqueeze(1).broadcast_to([P, TILES, D])

            def add_tokens(dst):
                for tt in range(TILES // 2):
                    bank = ringD.to_drain(dve)
                    d = dst[:, 2 * tt:2 * tt + 2, :].rearrange("p t d -> p (t d)")
                    i = dve.tensor_tensor(d, ps[:, bank, :], d, ALU.add)
                    i.then_inc(s_dd, 1)
                dve.wait_ge(s_dd, ringD.drains)

            def cross(s, maps, bias):
                rows3 = lambda x: x.rearrange("p (j n) -> p j n", j=2)

                def mask_scores(i, u):
                    U = i * 8 + u
                    dve.wait_ge(s["s_done"], U + 1)
                    wge(dve, s["exp_done"], U - 3)
                    dve.tensor_tensor(rows3(sm[:, u % 4, :]), rows3(ps[:, u % 4, :]),
                                      bias_x[:].unsqueeze(1).broadcast_to([P, 2, SK]), ALU.add).then_inc(s["s_read"], 1)

                def maxes(i, u):
                    U = i * 8 + u
                    if maps == 1:
                        dve.wait_ge(s["s_read"], U + 1)
                        dve.tensor_reduce(mx[:, u % 4, 0:2], rows3(sm[:, u % 4, :]), X_AXIS, ALU.max, negate=True).then_inc(s["mx_ready"], 1)
                    else:
                        dve.wait_ge(s["s_done"], U + 1)
                        dve.tensor_reduce(mx[:, u % 4, 0:2], rows3(ps[:, u % 2 * 2, :]), X_AXIS, ALU.max, negate=True)
                        dve.tensor_reduce(mx[:, u % 4, 2:4], rows3(ps[:, u % 2 * 2 + 1, :]), X_AXIS, ALU.max, negate=True)\
                           .then_inc(s["mx_ready"], 1)

                def sums_inverse(i, u):
                    U = i * 8 + u
                    dve.wait_ge(s["exp_done"], U + 1)
                    dve.reciprocal(ri[:, u % 2, 0:2 * maps], rs[:, u % 4, 0:2 * maps]).then_inc(s["ri_ready"], 1)

                def divide(i, u, j):
                    U = i * 8 + u
                    if j == 0:
                        dve.wait_ge(s["ri_ready"], U + 1)
                    d = p1[:, u % 4, j * SK:(j + 1) * SK]
                    x = dve.tensor_scalar(d, d, ri[:, u % 2, j:j + 1], None, ALU.mult)
                    if j == 1:
                        x.then_inc(s["p_ready"], 1)

                def divide_second(i, u):
                    U, pr = i * 8 + u, u % 4 * 2
                    dve.wait_ge(s["ri_ready"], U + 1)
                    for j in range(2):
                        x = dve.tensor_scalar(p2[:, u % 4, j * SK:(j + 1) * SK], p2[:, u % 4, j * SK:(j + 1) * SK],
                                              ri[:, u % 2, 2 + j:3 + j], lam[:, pr + j:pr + j + 1], ALU.mult, ALU.mult)
                    x.then_inc(s["p2_ready"], 1)

                def subtract_second(i, u):
                    dve.wait_ge(s["p2_ready"], i * 8 + u + 1)
                    for j in range(2):
                        d = p1[:, u % 4, j * SK:(j + 1) * SK]
                        x = dve.scalar_tensor_tensor(out=d, in0=d, scalar=ri[:, u % 2, j:j + 1],
                                                     in1=p2[:, u % 4, j * SK:(j + 1) * SK], op0=ALU.mult, op1=ALU.subtract)
                    x.then_inc(s["p_ready"], 1)

                def extract_even(i, u):
                    dve.wait_ge(s["pv_done"], i * 8 + u + 1)
                    if bias is None:
                        x = dve.tensor_scalar(tmp[:, 0, :], ps[:, 6, 0:S], k("even"), None, ALU.mult)
                    else:
                        g = u // 2 % 2
                        x = dve.tensor_scalar(tmp[:, 0, :], ps[:, 6, 0:S], k("even"), bias[:, g:g + 1], ALU.mult, ALU.add)
                    x.then_inc(s["even_ready"], 1)

                def extract_odd(i, u):
                    g, b = u // 2 % 2, i * 2 + u // 4
                    dve.wait_ge(s["even_ready"], i * 4 + (u + 1) // 2)
                    dve.scalar_tensor_tensor(out=AT[:, g, bass.ds(b * S, S)], in0=ps[:, 6, S:2 * S], scalar=k("odd"), in1=tmp[:, 0, :],
                                             op0=ALU.mult, op1=ALU.add).then_inc(s["o_drained"], 1)

                def step(i, u):
                    top = i * 8 + u + 4 < B * 4 if isinstance(i, int) else True
                    mid = i * 8 + u + 2 < B * 4 and i * 8 + u + 2 >= 0 if isinstance(i, int) else True
                    own = u % 2 == 0 and not (isinstance(i, int) and i * 8 + u <= 0)
                    if mid:
                        sums_inverse(i, u + 2)
                    if own:
                        extract_even(i, u - 1)
                    if maps == 1:
                        if mid:
                            divide(i, u + 2, 0)
                        if own:
                            extract_odd(i, u - 1)
                        if top:
                            mask_scores(i, u + 4)
                        if mid:
                            divide(i, u + 2, 1)
                    else:
                        if mid:
                            divide_second(i, u + 2)
                        if own:
                            extract_odd(i, u - 1)
                        if mid:
                            subtract_second(i, u + 2)
                    if top:
                        maxes(i, u + 4)

                for u in range(-4, 0):
                    step(0, u)

                def body(i):
                    for u in range(8):
                        step(i, u)
                run_pipelined(dve, body, B // 2)
                extract_even(B // 2 - 1, 7)
                extract_odd(B // 2 - 1, 7)

            def self_attention(s):
                causal = k("causal").unsqueeze(1).broadcast_to([P, 8, S])
                rows8 = lambda x: x.rearrange("p (j n) -> p j n", j=8)


                def mask_scores(i, u):
                    U = i * 4 + u
                    dve.wait_ge(s["s_done"], U + 1)
                    wge(dve, s["exp_done"], U - 3)
                    dve.tensor_tensor(rows8(sm[:, u % 4, :]), rows8(ps[:, u % 4, :]), causal, ALU.add).then_inc(s["s_read"], 1)

                def maxes(i, u):
                    dve.wait_ge(s["s_read"], i * 4 + u + 1)
                    dve.tensor_reduce(mx[:, u % 4, :], rows8(sm[:, u % 4, :]), X_AXIS, ALU.max, negate=True).then_inc(s["max_ready"], 1)

                def subtract_maxes(i, u):
                    dve.wait_ge(s["max_ready"], i * 4 + u + 1)
                    m3 = rows8(sm[:, u % 4, :])
                    dve.tensor_tensor(m3, m3, mx[:, u % 4, :].unsqueeze(2).broadcast_to([P, 8, S]), ALU.add).then_inc(s["mx_ready"], 1)

                def sums(i, u):
                    dve.wait_ge(s["exp_done"], i * 4 + u + 1)
                    dve.tensor_reduce(rs[:, u % 4, :], rows8(p1[:, u % 4, :]), X_AXIS, ALU.add).then_inc(s["sum_ready"], 1)

                def sums_inverse(i, u):
                    dve.wait_ge(s["sum_ready"], i * 4 + u + 1)
                    dve.reciprocal(ri[:, u % 2, :], rs[:, u % 4, :]).then_inc(s["ri_ready"], 1)

                def divide(i, u):
                    dve.wait_ge(s["ri_ready"], i * 4 + u + 1)
                    p3 = rows8(p1[:, u % 4, :])
                    dve.tensor_tensor(p3, p3, ri[:, u % 2, :].unsqueeze(2).broadcast_to([P, 8, S]), ALU.mult).then_inc(s["p_ready"], 1)

                def extract(i, u):
                    dve.wait_ge(s["pv_done"], i * 4 + u + 1)
                    dve.tensor_tensor(AT[:, u % 2, bass.ds((i * 2 + u // 2) * P, P)], ps[:, 6 + u % 2, 0:P],
                                      k("ones").broadcast_to([P, P]), ALU.mult).then_inc(s["o_drained"], 1)

                n = TILES // 2

                def step(i, u):
                    top = i * 4 + u + 4 < n * 4 if isinstance(i, int) else True
                    mid = 0 <= i * 4 + u + 2 < n * 4 if isinstance(i, int) else True
                    own = not (isinstance(i, int) and i * 4 + u <= 0)
                    if mid:
                        sums(i, u + 2)
                    if own:
                        extract(i, u - 1)
                    if mid:
                        sums_inverse(i, u + 2)
                    if top:
                        mask_scores(i, u + 4)
                    if mid:
                        divide(i, u + 2)
                    if top:
                        maxes(i, u + 4)
                        subtract_maxes(i, u + 4)

                for u in range(-4, 0):
                    step(0, u)

                def body(i):
                    for u in range(4):
                        step(i, u)
                run_pipelined(dve, body, n)
                extract(n - 1, 3)

            dve.wait_ge(s_in["x"], 16)
            stats(X)
            normalise(X, XN, s_xn)
            dve.wait_ge(s_in["mask"], 16)
            dve.wait_ge(s_in["con"], 16)
            dve.wait_ge(s_in["vec"], 16)
            dve.wait_ge(s_in["rows"], 16)
            link(dve.tensor_scalar(bias_x[:], maskb[:], 1.0, -MASKED, ALU.subtract, ALU.mult))
            dve.wait_ge(s_xn, TILES)
            link(dve.tensor_tensor(X[:], X[:], row("xattn_bo"), ALU.add))
            link(dve.tensor_tensor(lam[:], v("lam1"), v("lam2"), ALU.subtract))
            link(dve.tensor_scalar(lam[:], lam[:], 0.1, None, ALU.add))
            cross(st["l0x"], 1, v("bv"))
            add_tokens(X)

            stats(X)
            normalise(X, XN, s_xn)
            cos = k("cos").unsqueeze(1).broadcast_to([P, BANK // S, S])
            sin = k("sin").unsqueeze(1).broadcast_to([P, BANK // S, S])
            dve.wait_ge(s_xn, 2 * TILES)
            for o in range(C):
                for h in range(2):
                    for dst in (QT, KT):
                        d = dst[:, o, h * BANK:(h + 1) * BANK].rearrange("p (b s) -> p b s", s=S)
                        bank = ringD.to_drain(dve)
                        dve.tensor_tensor(d, ps[:, bank, :].rearrange("p (b s) -> p b s", s=S), cos, ALU.mult).then_inc(s_dd, 1)
                        bank = ringD.to_drain(dve)
                        t3 = sm[:, 0, :].rearrange("p (b s) -> p b s", s=S)
                        dve.tensor_tensor(t3, ps[:, bank, :].rearrange("p (b s) -> p b s", s=S), sin, ALU.mult).then_inc(s_dd, 1)
                        dve.wait_ge(s_dd, ringD.drains)
                        i = dve.tensor_tensor(d, d, t3, ALU.add)
                        if o == C - 1 and h == 1 and dst is KT:
                            i.then_inc(st["l0a"]["qk_ready"], 1)
                        else:
                            link(i)
            dve.wait_ge(st["l0a"]["qk_ready"], 1)
            self_attention(st["l0a"])
            add_tokens(X)

            stats(X)
            normalise(X, XN, s_xn)
            dve.wait_ge(s_xn, 3 * TILES)
            self_attention(st["l0f"])
            add_tokens(XN)
            stats(XN)
            normalise(XN, XN)
            link(dve.tensor_tensor(XN[:], XN[:], row("ffn_g1"), ALU.mult))
            dve.tensor_tensor(XN[:], XN[:], row("ffn_b1"), ALU.add).then_inc(s_xn, TILES)
            bank = ringD.to_drain(dve)
            lg = ps[:, bank, 0:TILES * E].rearrange("p (t e) -> p t e", e=E)
            r0, r1, r2, r3 = (router[:, n] for n in range(4))
            link(dve.tensor_reduce(ri[:, 0, :], lg, X_AXIS, ALU.max))
            dve.tensor_tensor(r0, lg, ri[:, 0, :].unsqueeze(2).broadcast_to([P, TILES, E]), ALU.subtract).then_inc(s_router, 1)
            dve.wait_ge(s_router, 2)
            dve.sem_inc(s_dd, 1)
            link(dve.tensor_reduce(ri[:, 0, :], r1, X_AXIS, ALU.add))
            link(dve.reciprocal(ri[:, 1, :], ri[:, 0, :]))
            link(dve.tensor_tensor(r2, r1, ri[:, 1, :].unsqueeze(2).broadcast_to([P, TILES, E]), ALU.mult))
            mine = r2.unsqueeze(3).broadcast_to([P, TILES, E, E])
            other = r2.unsqueeze(2).broadcast_to([P, TILES, E, E])
            g4 = rk[:, 0, :].rearrange("p (t e j) -> p t e j", t=TILES, e=E)
            e4 = rk[:, 1, :].rearrange("p (t e j) -> p t e j", t=TILES, e=E)
            dve.tensor_tensor(g4, other, mine, ALU.is_gt)
            link(dve.tensor_tensor(e4, other, mine, ALU.is_equal))
            bef = k("before").unsqueeze(1).broadcast_to([P, TILES, E * E])
            e3 = rk[:, 1, :].rearrange("p (t n) -> p t n", t=TILES)
            link(dve.tensor_tensor(e3, e3, bef, ALU.mult))
            link(dve.tensor_tensor(rk[:, 0, :], rk[:, 0, :], rk[:, 1, :], ALU.add))
            link(dve.tensor_reduce(r3, g4, X_AXIS, ALU.add))
            chosen = rt[:, 0, :].rearrange("p (t e) -> p t e", e=E)
            dve.tensor_scalar(chosen, r3, TOP - 0.5, None, ALU.is_lt).then_inc(s_sel, 1)
            dve.wait_ge(s_sel, 1)
            link(dve.tensor_tensor(r3, chosen, r2, ALU.mult))
            link(dve.tensor_reduce(ri[:, 0, :], r3, X_AXIS, ALU.add))
            link(dve.reciprocal(ri[:, 1, :], ri[:, 0, :]))
            dve.tensor_tensor(gw[:], r3, ri[:, 1, :].unsqueeze(2).broadcast_to([P, TILES, E]), ALU.mult).then_inc(s_gw, 1)
            bank = ringD.to_drain(dve)
            rank = ps[:, bank, 0:TILES * E]
            link(dve.memset(off[:, 0, :], 0.0))
            for t in range(TILES):
                link(dve.tensor_tensor(off[:, t + 1, :], off[:, t, :], ps[:, bank, (TILES + t) * E:(TILES + t + 1) * E], ALU.add))
            steps, nb, end, base = N // SLOTS, rb[:, 0, :], rb[:, 1, :], rb[:, 2, :]
            over = rc[:, 0:E * steps].rearrange("p (e j) -> p e j", j=steps)
            link(dve.tensor_tensor(over, off[:, TILES, :].unsqueeze(2).broadcast_to([P, E, steps]),
                                   k("steps").unsqueeze(1).broadcast_to([P, E, steps]), ALU.is_gt))
            link(dve.tensor_reduce(nb, over, X_AXIS, ALU.add))
            link(dve.memset(rb[:, 3, :], 1.0))
            link(dve.tensor_tensor_scan(end, rb[:, 3, :], nb, 0.0, ALU.mult, ALU.add))
            link(dve.tensor_tensor(base, end, nb, ALU.subtract))
            link(dve.tensor_scalar(base, base, float(SLOTS), None, ALU.mult))
            bl = rc[:, :].rearrange("p (b e) -> p b e", e=E)
            link(dve.tensor_tensor(bl, k("blocks").unsqueeze(2).broadcast_to([P, NBLK, E]),
                                   end.unsqueeze(1).broadcast_to([P, NBLK, E]), ALU.is_ge))
            link(dve.tensor_reduce(blkf[:], bl, X_AXIS, ALU.add))
            link(dve.tensor_scalar(blkf[:], blkf[:], float(E - 1), None, ALU.min))
            link(dve.tensor_copy(blk[:], blkf[:]))
            o3 = rt[:, 1, :].rearrange("p (t e) -> p t e", e=E)
            link(dve.tensor_tensor(o3, off[:, 0:TILES, :], base.unsqueeze(1).broadcast_to([P, TILES, E]), ALU.add))
            dve.tensor_tensor(rt[:, 2, :], rank, rt[:, 1, :], ALU.add).then_inc(s_dd, 1)
            dve.wait_ge(s_dd, ringD.drains)
            for n, (op, far) in enumerate(((ALU.min, FAR), (ALU.max, 0.0))):
                key = rt[:, 3, :].rearrange("p (t e) -> p t e", e=E)
                link(dve.scalar_tensor_tensor(out=rt[:, 3, :], in0=rt[:, 2, :], scalar=-far, in1=rt[:, 0, :], op0=ALU.add, op1=ALU.mult))
                link(dve.tensor_reduce(slotf[:, n, :], key, X_AXIS, op))
                own = rt[:, 4, :].rearrange("p (t e) -> p t e", e=E)
                link(dve.tensor_tensor(own, key, slotf[:, n, :].unsqueeze(2).broadcast_to([P, TILES, E]), ALU.is_equal))
                link(dve.tensor_tensor(own, own, gw[:], ALU.mult))
                link(dve.tensor_reduce(gate[:, n, :], own, X_AXIS, ALU.add))
                link(dve.tensor_scalar(slotf[:, n, :], slotf[:, n, :], far, float(NSLOT - 1), ALU.add, ALU.min))
            dve.tensor_copy(slot[:], slotf[:]).then_inc(s_slot, 1)
            dve.wait_ge(s_scat, 16 * TOP * TILES)
            add_tokens(XN)

            def tokens_rest(i, b):
                sl = b % 2
                dve.wait_ge(s_xhi, i * 2 + b + 1)
                dve.tensor_tensor(xb_lo[:, sl].rearrange("p c n -> p (c n)"), ps[:, 6, :],
                                  xb_hi[:, sl].bitcast(F32).rearrange("p c n -> p (c n)"), ALU.subtract).then_inc(s_xlo, 1)

            def hidden_rest(i, u):
                dve.wait_ge(s_hhi, i * 2 * UB + u + 1)
                dve.tensor_tensor(h_lo[:, u % 2, :], gact[:, u % 2, :], h_hi[:, u % 2, :].bitcast(F32), ALU.subtract)\
                   .then_inc(s_h1, 1)

            def weights_rest(i, g, n):
                dve.wait_ge(s_whi, i * 4 * CH + g * CH + n + 1)
                cols = slice(n * WG // CH, (n + 1) * WG // CH)
                dve.tensor_tensor(w_lo[:, g % 4, cols], wraw[:, g % 4, cols], w_hi[:, g % 4, cols].bitcast(F32), ALU.subtract)\
                   .then_inc(s_wlo, 1)

            def rests(i):
                for u in range(2 * UB):
                    if left(i, u + 1):
                        hidden_rest(i, u + 1)
                    if left(i, (u // 2 + 3) * 2):
                        for n in range(2):
                            weights_rest(i, u // 2 + 3, u % 2 * 2 + n)
                    if u % UB == 2 and left(i, (u // UB + 2) * UB):
                        tokens_rest(i, u // UB + 2)
            tokens_rest(0, 0)
            tokens_rest(0, 1)
            for g in range(3):
                for n in range(CH):
                    weights_rest(0, g, n)
            hidden_rest(0, 0)
            run_blocks(dve, rests)
            for t in range(TILES):
                dve.wait_ge(s_pick[t], 16 * TOP)
                for n in range(TOP):
                    link(dve.scalar_tensor_tensor(out=XN[:, t, :], in0=picked[:, n, t, :], scalar=gate[:, n, t:t + 1],
                                                  in1=XN[:, t, :], op0=ALU.mult, op1=ALU.add))
            stats(XN)
            normalise(XN, XN)
            link(dve.tensor_tensor(XN[:], XN[:], row("ffn_g2"), ALU.mult))
            link(dve.tensor_tensor(XN[:], XN[:], row("ffn_b2"), ALU.add))
            link(dve.tensor_tensor(X[:], X[:], XN[:], ALU.add))

            stats(X)
            normalise(X, XN, s_xn)
            dve.wait_ge(s_xn, 5 * TILES)
            link(dve.tensor_tensor(X[:], X[:], row("proj_b"), ALU.add))
            cross(st["l1x"], 2, None)
            dve.wait_ge(s_w[1], 32)
            for c in range(C):
                wp = W["l1x"][:, 5, c, :]
                i = dve.tensor_scalar(wp, wp, v("norm_w")[:, c:c + 1], None, ALU.mult)
            i.then_inc(s_projw, 1)
            bank = ringD.to_drain(dve)
            ln[0] += 1
            dve.tensor_scalar(rstd[:], ps[:, bank, 0:TILES], 1.0 / D, 1e-6, ALU.mult, ALU.add).then_inc(s_var, 1)
            dve.wait_ge(s_std, ln[0])
            dve.sem_inc(s_dd, 1)
            link(dve.reciprocal(rstd[:], std[:]))
            for tt in range(TILES // 2):
                bank = ringD.to_drain(dve)
                for t in range(2):
                    i = dve.scalar_tensor_tensor(out=X[:, 2 * tt + t, :], in0=ps[:, bank, t * D:(t + 1) * D],
                                                 scalar=rstd[:, 2 * tt + t:2 * tt + t + 1], in1=X[:, 2 * tt + t, :],
                                                 op0=ALU.mult, op1=ALU.add)
                i.then_inc(s_dd, 1)
            dve.wait_ge(s_dd, ringD.drains)

            stats(X)
            normalise(X, XN, s_xn)
            dve.wait_ge(s_norm, 1)
            dve.wait_ge(s_xn, 6 * TILES)
            link(dve.tensor_scalar(dk[:, 2:4], dk[:, 0:2], 1.0, None, ALU.add))
            link(dve.reciprocal(dk[:, 4:6], dk[:, 2:4]))
            link(dve.tensor_scalar(dk[:, 6:8], dk[:, 4:6], -1.0, 1.0, ALU.mult, ALU.add))
            link(dve.tensor_tensor(dk[:, 0:2], v("ret_b"), v("conv_b"), ALU.add))
            da = big_b[:, 0:C * N].rearrange("p (c n) -> p c n", c=C)
            dx = big_b[:, C * N:2 * C * N].rearrange("p (c n) -> p c n", c=C)
            dve.wait_ge(s_xt, 6 * TILES // 2)
            for c in range(C):
                dve.tensor_scalar(dx[:, c, :], XT[:, c, :], dk[:, 6 + c:7 + c], None, ALU.mult)
                dve.tensor_scalar(da[:, c, :], XT[:, c, :], 0.0, dk[:, 4 + c:5 + c], ALU.mult, ALU.add)
            link(dve.memset(tmp[:, 0, :], 0.0))
            link(dve.tensor_copy(da.rearrange("p c (b s) -> p (c b) s", s=S)[:, :, 0], tmp[:, 0, 0:C * B]))
            for c in range(C):
                i = dve.tensor_tensor_scan(KT[:, c, :], da[:, c, :], dx[:, c, :], 0.0, ALU.mult, ALU.add)
            i.then_inc(s_ret, 1)
            for c in range(C):
                xt = XT[:, c, :].rearrange("p (b s) -> p b s", s=S)
                y = QT[:, c, :].rearrange("p (b s) -> p b s", s=S)
                for tap in (2, 0, 1, 3, 4):
                    w = v("conv_w")[:, c * TAPS + tap:c * TAPS + tap + 1]
                    sh = tap - TAPS // 2
                    if sh == 0:
                        link(dve.tensor_scalar(y, xt, w, dk[:, c:c + 1], ALU.mult, ALU.add))
                    else:
                        lo, hi = max(0, -sh), S - max(0, sh)
                        link(dve.scalar_tensor_tensor(out=y[:, :, lo:hi], in0=xt[:, :, lo + sh:hi + sh], scalar=w,
                                                      in1=y[:, :, lo:hi], op0=ALU.mult, op1=ALU.add))
            for o in range(C):
                for h in range(2):
                    bank = ringD.to_drain(dve)
                    i = dve.tensor_tensor(AT[:, o, h * BANK:(h + 1) * BANK], ps[:, bank, :], QT[:, o, h * BANK:(h + 1) * BANK], ALU.add)
                    i.then_inc(s_dd, 1)
            dve.wait_ge(s_dd, ringD.drains)
            dve.sem_inc(s_ret, 1)
            add_tokens(X)

            stats(X)
            normalise(X, XN, s_xn)
            dve.wait_ge(s_tree_w, 48)

            def tree3(ap):
                return ap.rearrange("p (t n) -> p t n", t=TREES)

            def trees(i):
                dve.wait_ge(s_logit, i + 1)
                wge(dve, s_silu, i)
                q3 = ps[:, 0:4, 0:WIDTH // 4]
                dve.tensor_tensor(logit.rearrange("p (q n) -> p q n", q=4), q3, bin_b.rearrange("p (q n) -> p q n", q=4), ALU.add)\
                   .then_inc(s_lread, 1)
                dve.wait_ge(s_lread, i + 1)
                link(dve.tensor_scalar(dec, logit, 0.0, None, ALU.is_gt))
                link(dve.tensor_scalar(tree3(path)[:, :, 0:1], tree3(logit)[:, :, 0:1], 0.0, 1.0, ALU.mult, ALU.add))
                for d in range(DEPTH):
                    n0, n1, w = 2 ** d - 1, 2 ** (d + 1) - 1, 2 ** d
                    par, de = tree3(path)[:, :, n0:n0 + w], tree3(dec)[:, :, n0:n0 + w]
                    kids = tree3(path)[:, :, n1:n1 + 2 * w]
                    left, right = kids[:, :, 0:2 * w:2], kids[:, :, 1:2 * w:2]
                    link(dve.tensor_tensor(right, par, de, ALU.mult))
                    link(dve.tensor_tensor(left, par, right, ALU.subtract))
                dve.wait_ge(s_silu, i + 1)
                dve.tensor_tensor(acts, acts, path, ALU.mult).then_inc(s_path, 1)
                if not (isinstance(i, int) and i == 0):
                    add_trees(i - 1)

            def add_trees(i):
                dve.wait_ge(s_ty, i + 1)
                xt = X[:].rearrange("p t d -> p (t d)")[:, bass.ds(i * D, D)]
                dve.tensor_tensor(xt, ps[:, 6, 0:D], xt, ALU.add).then_inc(s_tx, 1)
            run_pipelined(dve, trees, TILES, chain)
            add_trees(TILES - 1)

        @block.gpsimd
        def _(pool):
            head = k("head").unsqueeze(2).broadcast_to([P, HG, S])

            def queries(src, off):
                return src[:, bass.ds(off, S)].unsqueeze(1).broadcast_to([P, HG, S])

            def mask_cross(s, maps):
                pool.wait_ge(s["qk_ready"], 4 * maps)

                def body(i):
                    for sl in range(2):
                        wge(pool, s["s_done"], i * 8 + 4 * (sl - 1))
                        for g in range(C):
                            for mp in range(maps):
                                src = (QT, KT)[mp][:, g, :]
                                x = pool.tensor_tensor(qm[:, sl, mp, g], queries(src, (i * 2 + sl) * S), head, ALU.mult)
                            x.then_inc(s["qm_ready"], 1)
                run_pipelined(pool, body, B // 2)

            def mask_self(s):
                pool.wait_ge(s["kv_drained"], 4)
                half = k("half").unsqueeze(1).unsqueeze(3).broadcast_to([P, 2 * D // (2 * HD), 2, HD])

                def tile_values(i, tu):
                    wge(pool, s["pv_done"], i * 4 + tu * 2 - 2)
                    src = VH.rearrange("p t b d -> p (t b d)")[:, bass.ds(i * (4 * D) + tu * 2 * D, 2 * D)]
                    pool.tensor_tensor(vs[:, tu % 2].rearrange("p b (j n d) -> p (b j) n d", n=2, d=HD),
                                       src.rearrange("p (j n d) -> p j n d", n=2, d=HD), half, ALU.mult).then_inc(s["v_ready"], 1)

                def body(i):
                    for u in range(4):
                        wge(pool, s["s_done"], i * 4 + u - 1)
                        here = bass.ds((i * 2 + u // 2) * P, P)
                        pool.tensor_tensor(qs[:, u % 4, :], QT[:, u % 2, here], k("ones").broadcast_to([P, P]), ALU.mult)
                        pool.tensor_tensor(km[:, u % 2], KT[:, u % 2, here].rearrange("p (b s) -> p b s", b=2).unsqueeze(2).broadcast_to([P, 2, HG, S]),
                                           head.unsqueeze(1).broadcast_to([P, 2, HG, S]), ALU.mult).then_inc(s["qm_ready"], 1)
                        if u % 2 == 0 and not (isinstance(i, int) and i == 0 and u == 0):
                            if isinstance(i, int) and i == 0 and u == 2:
                                pool.wait_ge(s["v_doubled"], 4 * 16)
                            tile_values(i, u // 2 - 1)
                run_pipelined(pool, body, TILES // 2)
                tile_values(TILES // 2, -1)

            pool.memset(big_b[:, 0:NSLOT // P * D], 0.0).then_inc(s_zmem, 1)
            pool.wait_ge(s_in["con"], 16)
            mask_cross(st["l0x"], 1)
            pool.wait_ge(st["l0a"]["qk_ready"], 1)
            mask_self(st["l0a"])
            pool.wait_ge(st["l0f"]["qk_ready"], 8)
            mask_self(st["l0f"])


            pool.wait_ge(s_slot, 1)
            pool.wait_ge(s_zero, 16)
            for n in range(TOP):
                for t in range(TILES):
                    pool.indirect_dma_start(moe_in, bass.IndirectOffsetOnAxis(slot[:, n, t:t + 1], 0), XN[:, t, :], None).then_inc(s_scat, 16)

            def round_weights(i, g):
                pool.wait_ge(s_e_in[g], i * 16 + 16)
                wge(pool, s_y, i * 2 * UB + 2 * (g - 3))
                for n in range(CH):
                    cols = slice(n * WG // CH, (n + 1) * WG // CH)
                    pool.tensor_tensor(w_hi[:, g, cols], wraw[:, g, cols], k("ones").broadcast_to([P, WG // CH]), ALU.mult).then_inc(s_whi, 1)

            def rounds(i):
                for g in range(4):
                    if left(i, 2 * g):
                        round_weights(i, g)
            run_blocks(pool, rounds)
            pool.wait_ge(s_ys[0], 16 * ((NBLK + 1) // 2))
            pool.wait_ge(s_ys[1], 16 * (NBLK // 2))
            for t in range(TILES):
                for n in range(TOP):
                    pool.indirect_dma_start(picked[:, n, t, :], None, moe_out, bass.IndirectOffsetOnAxis(slot[:, n, t:t + 1], 0)).then_inc(s_pick[t], 16)
            mask_cross(st["l1x"], 2)
            pool.wait_ge(s_xt, 7 * TILES // 2)

            def slots(i):
                wge(pool, s_logit, i)
                pool.tensor_copy(xslot, XT[:, :, bass.ds(i * P, P)]).then_inc(s_xslot, 1)
            run_pipelined(pool, slots, TILES)


def _kmaj(w):
    i, o = w.shape
    return np.ascontiguousarray(w.reshape(i // P, P, o).transpose(1, 0, 2).reshape(P, -1))


def _col(v):
    return np.ascontiguousarray(v.reshape(-1, P).T)


def _constants():
    con = np.zeros((P, NCON), np.float32)
    p = np.arange(P)

    def put(name, val):
        lo, hi = CON[name]
        con[:, lo:hi] = val
    put("ident", np.eye(P))
    put("head", SCALE * ((p[:, None] // HD) == np.arange(HG)[None, :]))
    put("even", ((p // HD) % 2 == 0)[:, None])
    put("odd", ((p // HD) % 2 == 1)[:, None])
    put("causal", np.where(np.arange(S)[None, :] <= (p % S)[:, None], 0.0, MASKED))
    freqs = np.exp(np.arange(HD // 2, dtype=np.float32) * np.float32(-np.log(10000.0) * 2.0 / HD)).astype(np.float32)
    ang = (np.arange(S, dtype=np.float32)[None, :] * freqs[(p % HD) // 2][:, None]).astype(np.float32)
    put("cos", np.cos(ang))
    put("sin", np.sin(ang) * np.where(p % 2 == 0, -1.0, 1.0)[:, None])
    put("ones", 1.0)
    put("half", (p // S)[:, None] == np.arange(2)[None, :])
    put("earlier", p[:, None] < p[None, :])
    put("all", 1.0)
    put("steps", SLOTS * np.arange(N // SLOTS)[None, :])
    put("blocks", np.arange(NBLK)[None, :])
    put("before", np.broadcast_to((np.arange(E)[None, :] < np.arange(E)[:, None]).reshape(1, -1), (P, E * E)))
    return con


def kernel(**inputs):
    import concourse.bacc as _bacc
    from concourse.bass_utils import run_bass_kernel_spmd as _run

    i = {n: np.asarray(x) for n, x in inputs.items()}
    con = _constants()
    swap = np.arange(D) ^ 1
    ipw = i["L0_attn_in_proj_w"]
    kv1, kv2 = i["L1_xattn_kv1_w"], i["L1_xattn_kv2_w"]

    def pair_rows(v):
        return np.concatenate([np.broadcast_to(v.reshape(-1)[n::2], (P // 2, H // 2)) for n in range(2)], 0)

    arrays = {
        "x": i["x"],
        "ctxT": np.ascontiguousarray(i["ctx_1024"].transpose(0, 2, 1).reshape(B, C, P, SK).transpose(0, 2, 1, 3).reshape(B, P, C * SK)),
        "mask": np.ascontiguousarray(np.concatenate([i["mask_1x1xSxS2_bk0"][0, 0]] * 2, 0)),
        "con": con,
        "w_l0x": np.concatenate([_kmaj(i["L0_xattn_" + n].T) for n in ("Wq", "Wk", "Wv", "Wo")], 1),
        "w_l0a": np.concatenate([_kmaj(w.T) for w in (ipw[:D], ipw[D:2 * D], ipw[2 * D:], ipw[:D][swap], ipw[D:2 * D][swap],
                                                      i["L0_attn_out_proj_w"])], 1),
        "w_l0f": np.concatenate([_kmaj(w) for w in (i["L0_ffn_w_qkv"][:, :D], i["L0_ffn_w_qkv"][:, D:2 * D],
                                                    i["L0_ffn_w_qkv"][:, 2 * D:], i["L0_ffn_w_o"])], 1),
        "w_l1x": np.concatenate([_kmaj(w.T) for w in (i["L1_xattn_q1_w"], i["L1_xattn_q2_w"], kv1[:D], kv1[D:], kv2[:D],
                                                      i["L1_xattn_proj_w"])], 1),
        "w_l1a": _kmaj(i["L1_attn_W"].T),
        "wg": _kmaj(i["L0_ffn_wg"]),
        "we": np.concatenate([
            i["L0_ffn_w1"].reshape(E, C, P, M // MG, MG * P).transpose(0, 3, 2, 1, 4).reshape(E * M // MG, P, C * MG * P),
            i["L0_ffn_w2"].reshape(E, M // MG, MG, P, D).transpose(0, 1, 3, 2, 4).reshape(E * M // MG, P, MG * D)], 2),
        "bb2": i["L0_ffn_bb2"],
        "w_in": _kmaj(i["L1_ffn_W_in"].T),
        "w_out": _kmaj(np.concatenate([i["L1_ffn_W_out"].T, np.zeros((NB * P - WIDTH, D), np.float32)], 0)),
        "b_in": i["L1_ffn_b_in"],
        "rows": np.concatenate([i[n] for n in ("L0_xattn_bo", "L0_ffn_g1", "L0_ffn_b1", "L0_ffn_g2", "L0_ffn_b2", "L1_xattn_proj_b")]),
        "vec": np.concatenate([
            _col(i["L0_xattn_bq"]), _col(i["L0_xattn_bk"]), _col(i["L0_xattn_bv"]), _col(i["L1_attn_decay_logit"]),
            _col(i["L1_attn_b"]), _col(i["L1_attn_conv_b"]),
            i["L1_attn_conv_w"].reshape(C, P, TAPS).transpose(1, 0, 2).reshape(P, -1),
            pair_rows(i["L1_xattn_lambda_1"]), pair_rows(i["L1_xattn_lambda_2"]), _col(i["L1_xattn_norm_w"])], 1),
        "bb1": i["L0_ffn_bb1"].reshape(E, M, P).transpose(0, 2, 1),
    }
    nc = _bacc.Bacc("TRN2", target_bir_lowering=False, num_devices=1)
    feeds, args = {}, {}
    for n, arr in arrays.items():
        arr = np.ascontiguousarray(arr)
        feeds["in_" + n] = arr
        args[n] = nc.dram_tensor("in_" + n, arr.shape, mybir.dt.from_np(arr.dtype), kind="ExternalInput").ap()
    out = nc.dram_tensor("out_0", (B, S, D), F32, kind="ExternalOutput").ap()
    build(nc, args, out)
    r = _run(nc, [feeds], core_ids=[0])
    return r.results[0]["out_0"]
```

```python
from contextlib import ExitStack

import numpy as np

import concourse.bass as bass
from concourse import mybir

F32 = mybir.dt.float32
I32 = mybir.dt.int32
BF16 = mybir.dt.bfloat16
F32R = mybir.dt.float32r
U8 = mybir.dt.uint8
ALU = mybir.AluOpType
ACT = mybir.ActivationFunctionType
X_AXIS = mybir.AxisListType.X

P = 128
B, S, D = 16, 64, 256
SK = 256
N = B * S
H, HD = 16, 16
C = D // P
TILES = N // P
HG = H // C
PAIRS = HG // 2
E, F = 8, 1024
M = F // P
TREES, NODES, DEPTH = 8, 255, 7
WIDTH = TREES * NODES
NB = (WIDTH + P - 1) // P
TAPS = 5
TOP = 2
SLOTS = 256
NBLK = (N * TOP - E) // SLOTS + E
NSLOT = NBLK * SLOTS
UB = M // 2
CH = 4
FAR = 8192.0
SCALE = float(HD) ** -0.5
MASKED = -1.0e30
BANK = 512
MG = 4
WG = C * MG * P + MG * D


VEC = {}
_at = 0
for _name, _n in (("bq", C), ("bk", C), ("bv", C), ("decay", C), ("ret_b", C), ("conv_b", C), ("conv_w", C * TAPS),
                  ("lam1", 2 * PAIRS), ("lam2", 2 * PAIRS), ("norm_w", C)):
    VEC[_name] = (_at, _at + _n)
    _at += _n
NVEC = _at
CON = {}
_at = 0
for _name, _n in (("ident", P), ("head", HG), ("even", 1), ("odd", 1), ("causal", S), ("cos", S), ("sin", S),
                  ("ones", 1), ("eps", 1), ("half", 2),
                  ("earlier", P), ("all", P), ("steps", N // SLOTS), ("blocks", NBLK), ("before", E * E)):
    CON[_name] = (_at, _at + _n)
    _at += _n
NCON = _at
ROWS = ["xattn_bo", "ffn_g1", "ffn_b1", "ffn_g2", "ffn_b2", "proj_b"]


def wge(eng, sem, value):
    if not isinstance(value, int) or value > 0:
        eng.wait_ge(sem, value)


def run_pipelined(eng, body, n, chain=None):
    base = chain.at if chain else 0
    body(0)
    per = chain.at - base if chain else 0
    if n > 2:
        with eng.Fori(1, n - 1) as i:
            if chain:
                chain.at = i * per + base
            body(i)
        if chain:
            assert isinstance(base, int)
            chain.at = base + (n - 1) * per
    body(n - 1)


def staggered(stages):
    return [(j, k - j) for k in range(TILES // 2 + stages - 1) for j in range(stages) if 0 <= k - j < TILES // 2]


KV_ROWS = {0: 0, "v": 1, 1: 2}


def half_tiles(h):
    return range(h * TILES // 2, (h + 1) * TILES // 2)


def kv_first(maps):
    return [(0, m) for m in range(maps)] + [(0, "v")] + [(1, m) for m in range(maps)]


def kv_step(maps, u, last):
    b, first = u // 4, 2 * maps + 1 + u // 4 * (maps + 1)
    if last and b == 1:
        return []
    if u % 4 == 0:
        return [(b + 1, "v", first)]
    return [(b + 2, u % 4 - 1, first + u % 4)] if u % 4 <= maps and not last else []


class Chain:

    def __init__(self, eng, sem):
        self.eng, self.sem, self.at = eng, sem, 0

    def link(self, ins):
        ins.then_inc(self.sem, 1)
        self.at = self.at + 1
        self.eng.wait_ge(self.sem, self.at)


class Ring:

    def __init__(self, filled, drained, banks):
        self.filled, self.drained, self.banks = filled, drained, banks
        self.fills = self.drains = 0

    def to_fill(self, pe):
        wge(pe, self.drained, self.fills - len(self.banks) + 1)
        self.fills += 1
        return self.banks[(self.fills - 1) % len(self.banks)]

    def to_drain(self, eng):
        self.drains += 1
        eng.wait_ge(self.filled, self.drains)
        return self.banks[(self.drains - 1) % len(self.banks)]


def build(nc, a, out):
    ctx = ExitStack()
    with ctx:
        def sb(name, shape, dt=F32):
            return ctx.enter_context(nc.sbuf_tensor(name, shape, dt))

        def sem(name):
            return ctx.enter_context(nc.semaphore(name))

        X = sb("X", [P, TILES, D])
        KB = 1024
        slab = nc.sbuf_base
        sb("slab", [P, 68 * KB // 4])

        def at(name, kb, shape, dt=F32):
            return nc.alloc_sbuf_tensor_at(name, shape, dt, offset=slab + kb * KB)

        QT = at("QT", 0, [P, C, N])
        KT = at("KT", 8, [P, C, N])
        AT = at("AT", 16, [P, C, N])
        kts = at("kts", 24, [P, 2, 2, C, SK])
        qm = at("qm", 32, [P, 2, 2, C, HG, S])
        p1 = at("p1", 48, [P, 4, BANK])
        p2 = at("p2", 56, [P, 4, BANK])
        sm = p2
        pts = at("pts", 64, [P, 2, BANK])
        w_hi = at("w_hi", 0, [P, 4, WG], F32R)
        w_lo = at("w_lo", 32, [P, 4, WG], F32R)
        gwT = at("gwT", 64, [E, N])
        XN = sb("XN", [P, TILES, D])
        XT = sb("XT", [P, C, N])
        weights = sb("weights", [P, 2, 6, C, D])
        wgate = sb("wgate", [P, C, E])
        ctxs = sb("ctxs", [P, 2, C, SK])
        km = at("km", 24, [P, 2, 2, HG, S])
        qs = at("qs", 32, [P, 4, P])
        vs = sb("vs", [P, 2, 2, D])
        stat = sb("stat", [P, TILES, 6])
        mv = sb("mv", [P, TILES, 2])
        rstd = sb("rstd", [P, TILES])
        std = sb("std", [P, TILES])
        rstd_rms = sb("rstd_rms", [P, TILES])
        mx = sb("mx", [P, 4, 8])
        rs = sb("rs", [P, 4, 8])
        ri = sb("ri", [P, 2, 8])
        tmp = sb("tmp", [P, 2, S])
        vec = sb("vec", [P, NVEC])
        con = sb("con", [P, NCON])
        mask16 = sb("mask16", [P, S], BF16)
        ident16 = sb("ident16", [P, P], BF16)
        rows = sb("rows", [P, len(ROWS), D])
        bb2 = sb("bb2", [E, D])
        maskb = sb("maskb", [P, SK], U8)
        bias_x = sb("bias_x", [P, SK])
        lam = sb("lam", [P, 2 * PAIRS])
        slab_a, slab_w = slab, nc.sbuf_base
        big_a = sb("big_a", [P, 8192])
        slab = nc.sbuf_base
        big_b = sb("big_b", [P, 8192])
        xb_hi = at("xb_hi", 0, [P, 2, C, SLOTS], F32R)
        xb_lo = at("xb_lo", 4, [P, 2, C, SLOTS], F32R)
        gact = at("gact", 8, [P, 2, BANK])
        h_hi = at("h_hi", 12, [P, 2, BANK], F32R)
        h_lo = at("h_lo", 16, [P, 2, BANK], F32R)
        yb = at("yb", 20, [P, 2, 2, D])
        xs = at("xs", 24, [P, 2, 2, D])
        picked = big_b[:, :].rearrange("p (k t d) -> p k t d", k=2, t=2 * TILES)[:, :, 0:TILES, :]
        VT = big_a[:, 0:TILES * D].rearrange("p (t d) -> p t d", t=TILES)
        VH = big_a[:, TILES * D:3 * TILES * D].rearrange("p (t b d) -> p t b d", t=TILES, b=2)
        wraw = big_a[:, :].rearrange("p (s w) -> p s w", s=4)
        ps = ctx.enter_context(nc.psum_tensor("ps", [P, 8, BANK], F32))

        def v(name):
            lo, hi = VEC[name]
            return vec[:, lo:hi]

        def k(name):
            lo, hi = CON[name]
            return con[:, lo:hi]

        ident = k("ident")

        s_in = {n: sem("in_" + n) for n in ("x", "con", "vec", "rows", "mask", "bb2", "wg")}
        s_w = [sem(f"weights_in_{i}") for i in range(2)]
        s_tree_w = sem("tree_weights_in")
        s_tree_b = sem("tree_biases_in")
        s_tree_hi = sem("tree_weights_rounded")
        s_tree_lo = sem("tree_weights_split")
        s_xh = sem("tile_rounded")
        s_th = sem("tree_block_rounded")
        s_out = sem("out_stored")
        s_dve = sem("vector_step")
        s_var = sem("variance_ready")
        s_std = sem("deviation_ready")
        s_xn = sem("normalised_tile")
        s_xt = sem("transposed_block_in_sbuf")
        s_fa, s_da = sem("bank_filled_for_scalar"), sem("bank_drained_by_scalar")
        s_fd, s_dd = sem("bank_filled_for_vector"), sem("bank_drained_by_vector")
        s_w_free = sem("stage_weights_free")
        ringA = Ring(s_fa, s_da, [0, 1, 2, 3])
        ringD = Ring(s_fd, s_dd, [4, 5, 6, 7])

        names = ["l0x", "l0a", "l0f", "l1x"]
        st = {}
        for n in names:
            st[n] = {m: sem(f"{n}_{m}") for m in (
                "qk_ready", "qm_ready", "s_done", "mx_ready", "exp_done", "p_ready", "pt_filled", "pt_drained",
                "pv_done", "o_drained", "kv_drained", "ri_ready")
                + (("kv_filled", "ctx0", "ctx1", "even_ready", "ctx_rounded", "ctx_split", "w_split") if n in ("l0x", "l1x") else ("v_ready", "v_doubled", "max_ready", "sum_ready", "proj_filled", "proj_drained"))
                + {"l0x": ("s_read",), "l1x": ("p2_ready",)}.get(n, ())}
        s_mask16 = sem("causal_mask_ready")
        s_router = sem("router_ready")
        s_sel = sem("chosen_experts_ready")
        s_gw = sem("gate_weights_ready")
        s_gwT = sem("gate_weights_transposed")
        s_slot = sem("slots_ready")
        s_blk = sem("blocks_experts_ready")
        s_zero = sem("slots_zeroed")
        s_zmem = sem("zeros_ready")
        s_scat = sem("tokens_scattered")
        s_pick = [sem(f"outputs_picked_{pair}") for pair in range(TILES // 2)]
        s_e_in = [sem(f"expert_weights_in_{i}") for i in range(4)]
        s_b_in = [sem(f"hidden_biases_in_{i}") for i in range(2)]
        s_x_in = [sem(f"block_tokens_in_{i}") for i in range(2)]
        s_xbT = sem("block_tokens_transposed")
        s_xhi = sem("block_tokens_rounded")
        s_xlo = sem("block_tokens_split")
        s_whi = sem("weights_rounded")
        s_wlo = sem("weights_split")
        s_hid = sem("hidden_filled")
        s_gelu = sem("gelu_done")
        s_hhi = sem("hidden_rounded")
        s_h1 = sem("hidden_split")
        s_y = sem("expert_unit_done")
        s_yev = sem("block_output_in_sbuf")
        s_ys = [sem(f"block_output_stored_{b}") for b in range(2)]
        s_ret = sem("retention_ready")
        s_sq = sem("squares_ready")
        s_squares = sem("sums_of_squares_filled")
        s_dk = sem("decays_ready")
        s_norm = sem("rms_ready")
        s_projw = sem("scaled_projection_ready")
        s_xslot = sem("tile_copied")
        s_logit = sem("logits_filled")
        s_lread = sem("logits_read")
        s_silu = sem("silu_done")
        s_path = sem("path_masked")
        s_tt = sem("tree_block_transposed")
        s_tc = sem("tree_block_in_sbuf")
        s_ty = sem("tree_out_filled")
        s_tx = sem("tree_out_added")

        W = {"l0x": weights[:, 0], "l0a": weights[:, 1], "l0f": weights[:, 0], "l1x": weights[:, 1], "l1a": weights[:, 0]}
        WSLOT = {"l0x": (0, 16), "l0a": (1, 16), "l0f": (0, 32), "l1x": (1, 32), "l1a": (0, 48)}

        win = big_a[:, 0:C * WIDTH]
        wout = big_a[:, 4096:4096 + NB * D]
        slab = slab_a
        mt_hi = at("mt_hi", 0, [P, NB, P], F32R)
        mt_lo = at("mt_lo", 8, [P, NB, P], F32R)
        mt = at("mt", 16, [P, NB, P])
        wi_hi = at("wi_hi", 24, [P, C * WIDTH], F32R)
        wo_hi = at("wo_hi", 40, [P, NB * D], F32R)
        bin_b = at("bin_b", 56, [P, WIDTH])
        x_hi = at("x_hi", 64, [P, C, P], F32R)
        x_lo = at("x_lo", 65, [P, C, P], F32R)
        xslot = at("xslot", 66, [P, C, P])
        slab = slab_w
        wi_lo = at("wi_lo", 0, [P, C * WIDTH], F32R)
        wo_lo = at("wo_lo", 16, [P, NB * D], F32R)
        kv_hi = at("kv_hi", 0, [P, 3, C, D], F32R)
        kv_lo = at("kv_lo", 6, [P, 3, C, D], F32R)
        ctx_hi = at("ctx_hi", 12, [P, 2, C, SK], F32R)
        ctx_lo = at("ctx_lo", 16, [P, 2, C, SK], F32R)
        logit, dec, path = (big_b[:, 2048 * i:2048 * i + WIDTH] for i in range(3))
        acts = big_b[:, 6144:6144 + NB * P]
        nodes = acts[:, 0:WIDTH]

        gw = sb("gw", [P, TILES, E])
        router = sb("router", [P, 4, TILES, E])
        rk = sm[:, 0:2, :]
        bb1s = sb("bb1s", [P, 2, M])
        rt = sb("rt", [P, 6, TILES * E])
        off = sb("off", [P, TILES + 1, E])
        rb = sb("rb", [P, 6, E])
        rc = sb("rc", [P, NBLK * E])
        gate = sb("gate", [P, TOP, TILES])
        slotf = sb("slotf", [P, TOP, TILES])
        slotc = sb("slotc", [P, TOP, TILES])
        slot = sb("slot", [P, TOP, TILES], I32)
        blkf = sb("blkf", [P, NBLK])
        blk = sb("blk", [P, NBLK], I32)
        moe_in = nc.dram_tensor("moe_in", (NSLOT, D), F32, kind="Internal").ap()
        moe_out = nc.dram_tensor("moe_out", (NSLOT, D), F32, kind="Internal").ap()
        dk = sb("dk", [P, 8])

        PAIRS_B = (NBLK + 1) // 2

        def run_blocks(eng, body):
            body(0)
            with eng.Fori(1, PAIRS_B - 2) as i:
                body(i)
            body(PAIRS_B - 2)
            body(PAIRS_B - 1)

        def left(i, u):
            return not isinstance(i, int) or i * 2 * UB + u < NBLK * UB

        def convolution(eng, c):
            xt = XT[:, c, :].rearrange("p (b s) -> p b s", s=S)
            y = QT[:, c, :].rearrange("p (b s) -> p b s", s=S)
            for tap in sorted(range(TAPS), key=lambda tap: tap != TAPS // 2):
                w = v("conv_w")[:, c * TAPS + tap:c * TAPS + tap + 1]
                sh = tap - TAPS // 2
                if sh == 0:
                    yield eng.tensor_scalar(y, xt, w, dk[:, c:c + 1], ALU.mult, ALU.add)
                else:
                    lo, hi = max(0, -sh), S - max(0, sh)
                    yield eng.scalar_tensor_tensor(out=y[:, :, lo:hi], in0=xt[:, :, lo + sh:hi + sh], scalar=w,
                                                   in1=y[:, :, lo:hi], op0=ALU.mult, op1=ALU.add)

        block = ctx.enter_context(nc.Block())

        @block.sync
        def _(sp):
            sp.dma_start(con[:], a["con"]).then_inc(s_in["con"], 16)
            sp.dma_start(X[:], a["x"].rearrange("b s d -> (b s) d").rearrange("(t p) d -> p t d", p=P)).then_inc(s_in["x"], 16)
            sp.dma_start(W["l0x"][:, 0:4], a["w_l0x"].rearrange("p (w c d) -> p w c d", w=4, c=C)).then_inc(s_w[0], 16)
            sp.dma_start(vec[:], a["vec"]).then_inc(s_in["vec"], 16)
            sp.dma_start(maskb[:], a["mask"]).then_inc(s_in["mask"], 16)

            def load_ctx(s, b, sl):
                dst = ctxs[:, sl]
                src = a["ctxT"][b] if isinstance(b, int) else a["ctxT"][bass.ds(b, 1)].rearrange("o p n -> (o p) n")
                sp.dma_start(dst, src.rearrange("p (c n) -> p c n", c=C)).then_inc(s[f"ctx{sl}"], 16)

            def ctx_loop(s):

                def body(i):
                    for sl in range(2):
                        sp.wait_ge(s["ctx_split"], i * 2 + sl + 1)
                        load_ctx(s, i * 2 + 2 + sl, sl)
                with sp.Fori(0, B // 2 - 1) as i:
                    body(i)

            def double_values(s):
                sp.wait_ge(s["kv_drained"], 4)
                for half in range(2):
                    for b in range(2):
                        sp.dma_start(VH[half * S:(half + 1) * S, :, b, :], VT[b * S:(b + 1) * S]).then_inc(s["v_doubled"], 16)

            load_ctx(st["l0x"], 0, 0)
            load_ctx(st["l0x"], 1, 1)
            sp.dma_start(rows[:], a["rows"].partition_broadcast(P).rearrange("p (r d) -> p r d", d=D)).then_inc(s_in["rows"], 16)
            sp.dma_start(W["l0a"][:, 0:6], a["w_l0a"].rearrange("p (w c d) -> p w c d", w=6, c=C)).then_inc(s_w[1], 16)
            ctx_loop(st["l0x"])
            sp.wait_ge(s_zmem, 1)
            sp.dma_start(moe_in.rearrange("(p a) d -> p (a d)", p=P), big_b[:, 0:NSLOT // P * D]).then_inc(s_zero, 16)
            for n, key, dst in (("bb2", "bb2", bb2[:]), ("wg", "wg", wgate[:].rearrange("p c e -> p (c e)"))):
                sp.dma_start(dst, a[key]).then_inc(s_in[n], 16)

            sp.wait_ge(s_w_free, 1)
            sp.dma_start(W["l0f"][:, 0:4], a["w_l0f"].rearrange("p (w c d) -> p w c d", w=4, c=C)).then_inc(s_w[0], 16)
            double_values(st["l0a"])
            sp.wait_ge(s_w_free, 2)
            sp.dma_start(W["l1x"][:, 0:6], a["w_l1x"].rearrange("p (w c d) -> p w c d", w=6, c=C)).then_inc(s_w[1], 16)
            double_values(st["l0f"])
            sp.wait_ge(s_w_free, 3)
            sp.dma_start(W["l1a"][:, 0], a["w_l1a"].rearrange("p (c d) -> p c d", c=C)).then_inc(s_w[0], 16)
            sp.wait_ge(s_blk, 1)

            def load_block(i, b):
                e = sp.value_load(blk[0:1, bass.ds(i * 2 + b, 1)], min_val=0, max_val=E - 1)
                for g in range(2):
                    sl = 2 * b + g
                    wge(sp, s_wlo, i * 4 * CH + (sl - 3) * CH)
                    sp.dma_start(wraw[:, sl, :], a["we"][bass.ds(e * 2 + g, 1)].rearrange("o p n -> (o p) n")).then_inc(s_e_in[sl], 16)
                    if g == 0:
                        if isinstance(i, int) and i == 0 and b == 0:
                            sp.wait_ge(s_scat, 16 * TOP * TILES)
                        wge(sp, s_xbT, i * 2 + b - 1)
                        src = moe_in.rearrange("(b s p) d -> b p s d", s=2, p=P)[bass.ds(i * 2 + b, 1)].rearrange("o p s d -> (o p) s d")
                        sp.dma_start(xs[:, b], src).then_inc(s_x_in[b], 16)
                wge(sp, s_gelu, i * 2 * UB + (b - 1) * UB)
                sp.dma_start(bb1s[:, b, :], a["bb1"][bass.ds(e, 1)].rearrange("o p m -> (o p) m")).then_inc(s_b_in[b], 16)

            def load_blocks(i):
                for b in range(2):
                    if not (isinstance(i, int) and i * 2 + b >= NBLK):
                        load_block(i, b)
            run_pipelined(sp, load_blocks, (NBLK + 1) // 2)
            load_ctx(st["l1x"], 0, 0)
            load_ctx(st["l1x"], 1, 1)
            ctx_loop(st["l1x"])
            sp.wait_ge(st["l1x"]["kv_filled"], B * 3)
            sp.dma_start(win, a["w_in"]).then_inc(s_tree_w, 16)
            sp.dma_start(wout, a["w_out"]).then_inc(s_tree_w, 16)
            sp.wait_ge(st["l1x"]["p_ready"], B * 4)
            sp.dma_start(bin_b[:], a["b_in"].partition_broadcast(P)).then_inc(s_tree_b, 16)
            stored = 0
            for upto in (TILES - 2, TILES - 1, TILES):
                sp.wait_ge(s_tx, upto)
                tt = slice(stored, upto)
                sp.dma_start(out.rearrange("b s d -> (b s) d").rearrange("(t p) d -> p t d", p=P)[:, tt, :], X[:, tt, :]).then_inc(s_out, 16)
                stored = upto
            sp.wait_ge(s_out, 3 * 16)

        @block.tensor
        def _(pe):
            ln = [0]

            def transpose_tokens(h):
                for t in range(h * TILES // 2, (h + 1) * TILES // 2):
                    pe.wait_ge(s_xn, ln[0] * TILES + t + 1)
                    if t % 2 == 0:
                        bank = ringA.to_fill(pe)
                    for c in range(C):
                        i = pe.transpose(ps[:, bank, (t % 2 * C + c) * P:(t % 2 * C + c + 1) * P], XN[:, t, c * P:(c + 1) * P], ident)
                    if t % 2:
                        i.then_inc(s_fa, 1)
                ln[0] += h
                pe.wait_ge(s_xt, (2 * ln[0] + 1 - h) * TILES // 4)

            def project_features(h, w, ring, src=XT):
                for o in range(C):
                    bank = ring.to_fill(pe)
                    for c in range(C):
                        i = pe.matmul(ps[:, bank, :], w[:, c, o * P:(o + 1) * P], src[:, c, h * BANK:(h + 1) * BANK],
                                      start=(c == 0), stop=(c == C - 1))
                    i.then_inc(ring.filled, 1)

            def project_tokens(w, ring, src, free=None, tiles=range(TILES)):
                for t in tiles:
                    if t % 2 == 0:
                        bank = ring.to_fill(pe)
                    for c in range(C):
                        i = pe.matmul(ps[:, bank, t % 2 * D:(t % 2 + 1) * D], src[:, c, t * P:(t + 1) * P], w[:, c, :],
                                      start=(c == 0), stop=(c == C - 1))
                    if t % 2:
                        i.then_inc(ring.filled, 1)
                if free:
                    pe.wait_ge(ring.filled, ring.fills)
                    pe.sem_inc(free, 1)

            def three_passes(out, w, w0, x, x0, start, stop):
                for n, (wp, xp) in enumerate(((0, 0), (0, 1), (1, 0))):
                    i = pe.matmul(out, w[wp][w0], x[xp][x0], start=start and n == 0, stop=stop and n == 2)
                return i

            def kv_projection(s, maps):
                w, x = (kv_hi, kv_lo), (ctx_hi, ctx_lo)

                def project_kv(i, b, item, at):
                    sl, row = b % 2, KV_ROWS[item]
                    pe.wait_ge(s["ctx_split"], i * 2 + b + 1)
                    wge(pe, s["kv_drained"], at)
                    for part in range(2):
                        for c in range(C):
                            if item == "v":
                                m = three_passes(ps[:, 7, part * D:(part + 1) * D], x, (slice(None), sl, c, slice(part * P, (part + 1) * P)),
                                                 w, (slice(None), row, c, slice(None)), c == 0, c == C - 1)
                            else:
                                m = three_passes(ps[:, 7, part * SK:(part + 1) * SK], w, (slice(None), row, c, slice(part * P, (part + 1) * P)),
                                                 x, (slice(None), sl, c, slice(None)), c == 0, c == C - 1)
                    m.then_inc(s["kv_filled"], 1)

                pe.wait_ge(s["w_split"], 2 * (maps + 1))
                for n, (b, item) in enumerate(kv_first(maps)):
                    project_kv(0, b, item, n)
                return project_kv

            def cross(s, maps, project_kv, lag_ring):
                fills = maps + 1

                def scores(i, u):
                    U, sl, g, hp = i * 8 + u, u // 4 % 2, u // 2 % 2, u % 2
                    pe.wait_ge(s["qm_ready"], i * 4 + u // 2 + 1)
                    pe.wait_ge(s["kv_drained"], (i * 2 + u // 4 + 1) * fills - 1)
                    wge(pe, s["s_read"] if maps == 1 else s["exp_done"], U - lag_ring + 1)
                    for mp in range(maps):
                        bank = (u % lag_ring) * maps + mp
                        for j in range(2):
                            pr = hp * 2 + j
                            lhs = qm[:, sl, mp, g, 2 * pr:2 * pr + 2, :].rearrange("p h s -> p (h s)")
                            m = pe.matmul(ps[:, bank, j * SK:(j + 1) * SK], lhs, kts[:, sl, mp, g, :], start=True, stop=True)
                    m.then_inc(s["s_done"], 1)

                def transposes(i, u):
                    U = i * 8 + u
                    pe.wait_ge(s["p_ready"], U + 1)
                    wge(pe, s["pt_drained"], U - 1)
                    for j in range(2):
                        for half in range(2):
                            m = pe.transpose(ps[:, 4 + u % 2, (j * 2 + half) * P:(j * 2 + half + 1) * P],
                                             p1[:, u % 4, j * SK + half * P:j * SK + (half + 1) * P], ident)
                    m.then_inc(s["pt_filled"], 1)

                def values(i, u):
                    U, sl, g, hp = i * 8 + u, u // 4 % 2, u // 2 % 2, u % 2
                    pe.wait_ge(s["pt_drained"], U + 1)
                    pe.wait_ge(s["kv_drained"], (i * 2 + u // 4 + 1) * fills)
                    if hp == 0:
                        wge(pe, s["o_drained"], i * 4 + u // 2)
                    for j in range(2):
                        pr = hp * 2 + j
                        for half in range(2):
                            m = pe.matmul(ps[32 * pr:32 * pr + 32, 6, 0:P], vs[:, sl, half, g * P + 32 * pr:g * P + 32 * pr + 32],
                                          pts[:, u % 2, (j * 2 + half) * P:(j * 2 + half + 1) * P],
                                          start=(half == 0), stop=(half == 1), tile_position=(0, 32 * pr))
                    m.then_inc(s["pv_done"], 1)

                for u in range(4):
                    scores(0, u)
                transposes(0, 0)

                def body(i):
                    last = isinstance(i, int) and i == B // 2 - 1
                    for u in range(8):
                        if not (last and u + 4 >= 8):
                            scores(i, u + 4)
                        if not (last and u + 1 >= 8):
                            transposes(i, u + 1)
                        values(i, u)
                        for b, item, n in kv_step(maps, u, last):
                            project_kv(i, b, item, i * 2 * fills + n)
                run_pipelined(pe, body, B // 2)

            def self_attention(s, wo):
                def scores(i, u):
                    U = i * 4 + u
                    pe.wait_ge(s["qm_ready"], U + 1)
                    wge(pe, s["mx_ready"], U - 3)
                    pe.matmul(ps[:, u % 4, :].rearrange("p (h s) -> p h s", s=S), ident16[:], mask16[:].unsqueeze(1).broadcast_to([P, BANK // S, S]),
                              start=True, stop=False, skip_group_check=True)
                    for b in range(2):
                        m = pe.matmul(ps[b * S:(b + 1) * S, u % 4, :], qs[:, u % 4, b * S:(b + 1) * S],
                                      km[:, u % 2, b].rearrange("p h s -> p (h s)"), start=False, stop=True, tile_position=(0, b * S),
                                      skip_group_check=True)
                    m.then_inc(s["s_done"], 1)

                def transposes(i, u):
                    U = i * 4 + u
                    pe.wait_ge(s["p_ready"], U + 1)
                    wge(pe, s["pt_drained"], U - 1)
                    for pr in range(PAIRS):
                        m = pe.transpose(ps[:, 4 + u % 2, pr * P:(pr + 1) * P], p1[:, u % 4, pr * P:(pr + 1) * P], ident)
                    m.then_inc(s["pt_filled"], 1)

                def values(i, u):
                    U, g = i * 4 + u, u % 2
                    pe.wait_ge(s["pt_drained"], U + 1)
                    pe.wait_ge(s["v_ready"], i * 2 + u // 2 + 1)
                    wge(pe, s["o_drained"], U - 1)
                    for b in range(2):
                        for pr in range(PAIRS):
                            m = pe.matmul(ps[32 * pr:32 * pr + 32, 6 + u % 2, b * S:(b + 1) * S],
                                          vs[:, u // 2 % 2, b, g * P + 32 * pr:g * P + 32 * pr + 32],
                                          pts[:, u % 2, pr * P + b * S:pr * P + (b + 1) * S], start=True, stop=True,
                                          tile_position=(0, 32 * pr))
                    m.then_inc(s["pv_done"], 1)

                def project_out(i, tt):
                    T = i * 2 + tt
                    pe.wait_ge(s["o_drained"], (T + 1) * C)
                    wge(pe, s["proj_drained"], T)
                    for c in range(C):
                        m = pe.matmul(ps[:, 7, P:P + D], AT[:, c, tt % 2 * P:(tt % 2 + 1) * P], wo[:, c, :], start=(c == 0), stop=(c == C - 1))
                    m.then_inc(s["proj_filled"], 1)

                pe.wait_ge(s_mask16, 2)
                for u in range(4):
                    scores(0, u)
                transposes(0, 0)
                n = TILES // 2

                def body(i):
                    last = isinstance(i, int) and i == n - 1
                    for u in range(4):
                        if not last:
                            scores(i, u + 4)
                        if not (last and u + 1 >= 4):
                            transposes(i, u + 1)
                        if u % 2 == 1 and not (isinstance(i, int) and i == 0 and u == 1):
                            project_out(i, u // 2 - 1)
                        values(i, u)
                run_pipelined(pe, body, n)
                project_out(n, -1)
                pe.wait_ge(s["proj_filled"], TILES)
                pe.sem_inc(s_w_free, 1)

            def wait_weights(n):
                pe.wait_ge(s_w[WSLOT[n][0]], WSLOT[n][1])

            pe.wait_ge(s_in["con"], 16)
            wait_weights("l0x")
            w = W["l0x"]
            project_kv = kv_projection(st["l0x"], 1)
            for h in range(2):
                transpose_tokens(h)
                project_features(h, w[:, 0], ringA)
            s = st["l0x"]
            pe.wait_ge(s["qk_ready"], 4)
            cross(s, 1, project_kv, 4)
            pe.wait_ge(s["o_drained"], B * C)
            project_tokens(w[:, 3], ringD, AT, s_w_free)

            wait_weights("l0a")
            w = W["l0a"]
            for h in range(2):
                transpose_tokens(h)
                for o in range(C):
                    for n in (0, 3, 1, 4):
                        bank = ringD.to_fill(pe)
                        for c in range(C):
                            i = pe.matmul(ps[:, bank, :], w[:, n, c, o * P:(o + 1) * P], XT[:, c, h * BANK:(h + 1) * BANK],
                                          start=(c == 0), stop=(c == C - 1))
                        i.then_inc(s_fd, 1)
                project_tokens(w[:, 2], ringA, XT, tiles=half_tiles(h))
            s = st["l0a"]
            pe.wait_ge(s["qk_ready"], 2)
            pe.wait_ge(s["kv_drained"], 4)
            self_attention(s, w[:, 5])

            wait_weights("l0f")
            w = W["l0f"]
            for h in range(2):
                transpose_tokens(h)
                project_features(h, w[:, 0], ringA)
                project_features(h, w[:, 1], ringA)
                project_tokens(w[:, 2], ringA, XT, tiles=half_tiles(h))
            s = st["l0f"]
            pe.wait_ge(s["qk_ready"], 8)
            pe.wait_ge(s["kv_drained"], 4)
            self_attention(s, w[:, 3])
            pe.wait_ge(s_in["wg"], 16)
            bank = ringD.to_fill(pe)
            for h in range(2):
                transpose_tokens(h)
                for t in half_tiles(h):
                    for c in range(C):
                        i = pe.matmul(ps[:, bank, t * E:(t + 1) * E], XT[:, c, t * P:(t + 1) * P], wgate[:, c, :],
                                      start=(c == 0), stop=(c == C - 1))
            i.then_inc(s_fd, 1)
            pe.wait_ge(s_sel, 1)
            bank = ringD.to_fill(pe)
            pe.matmul(ps[:, bank, 0:TILES * E], k("earlier"), rt[:, 0, :], start=True, stop=True)
            pe.matmul(ps[:, bank, TILES * E:2 * TILES * E], k("all"), rt[:, 0, :], start=True, stop=True).then_inc(s_fd, 1)
            pe.wait_ge(s_gw, 1)
            for h in range(2):
                bank = ringA.to_fill(pe)
                for t in range(4):
                    i = pe.transpose(ps[0:E, bank, t * P:(t + 1) * P], gw[:, h * 4 + t, :], ident)
                i.then_inc(s_fa, 1)
            pe.wait_ge(s_gwT, 2)
            pe.wait_ge(s_in["bb2"], 16)
            for t in range(TILES):
                if t % 2 == 0:
                    bank = ringD.to_fill(pe)
                i = pe.matmul(ps[:, bank, t % 2 * D:(t % 2 + 1) * D], gwT[:, t * P:(t + 1) * P], bb2[:], start=True, stop=True)
                if t % 2:
                    i.then_inc(s_fd, 1)
            pe.wait_ge(s_dd, ringD.fills)

            def block_tokens(i, b):
                sl = b % 2
                pe.wait_ge(s_x_in[sl], i * 16 + (b // 2 + 1) * 16)
                wge(pe, s_xlo, i * 2 + b)
                for c in range(C):
                    for half in range(2):
                        x = pe.transpose(ps[:, 6, (c * 2 + half) * P:(c * 2 + half + 1) * P], xs[:, sl, half, c * P:(c + 1) * P], ident)
                x.then_inc(s_xbT, 1)

            def hidden(i, u):
                sl, b = u // 2 % 4, u // UB % 2
                if u % 2 == 0:
                    pe.wait_ge(s_wlo, i * 4 * CH + (u // 2 + 1) * CH)
                if u % UB == 0:
                    pe.wait_ge(s_xlo, i * 2 + u // UB + 1)
                wge(pe, s_gelu, i * 2 * UB + u - 3)
                for mm in range(2):
                    m = u % 2 * 2 + mm
                    for c in range(C):
                        x = three_passes(ps[:, u % 4, mm * SLOTS:(mm + 1) * SLOTS],
                                         (w_hi, w_lo), (slice(None), sl, slice((c * MG + m) * P, (c * MG + m + 1) * P)),
                                         (xb_hi, xb_lo), (slice(None), b, c, slice(None)), c == 0, c == C - 1)
                x.then_inc(s_hid, 1)

            def expert_out(i, u):
                sl, b = u // 2 % 4, u // UB % 2
                pe.wait_ge(s_h1, i * 2 * UB + u + 1)
                if u % UB == 0:
                    wge(pe, s_yev, i * 2 + u // UB - 1)
                for mm in range(2):
                    at0 = C * MG * P + (u % 2 * 2 + mm) * D
                    for half in range(2):
                        for n, (hp, wp) in enumerate(((h_hi, w_hi), (h_hi, w_lo), (h_lo, w_hi))):
                            first = u % UB == 0 and mm == 0 and half == 0 and n == 0
                            x = pe.matmul(ps[:, 4 + b, half * D:(half + 1) * D],
                                          hp[:, u % 2, mm * SLOTS + half * P:mm * SLOTS + (half + 1) * P],
                                          wp[:, sl, at0:at0 + D], start=first, stop=(u % UB == UB - 1 and mm == 1 and n == 2),
                                          skip_group_check=True)
                x.then_inc(s_y, 1)

            def experts(i):
                for u in range(2 * UB):
                    if u % UB == 2 and left(i, (u // UB + 2) * UB):
                        block_tokens(i, u // UB + 2)
                    if left(i, u + 3):
                        hidden(i, u + 3)
                    if left(i, u):
                        expert_out(i, u)
                    if isinstance(i, int) and i == 0 and u == 0:
                        block_tokens(0, 1)
            block_tokens(0, 0)
            for u in range(3):
                hidden(0, u)
            run_blocks(pe, experts)

            wait_weights("l1x")
            w = W["l1x"]
            project_kv = kv_projection(st["l1x"], 2)
            for h in range(2):
                transpose_tokens(h)
                project_features(h, w[:, 0], ringA)
                project_features(h, w[:, 1], ringA)
            s = st["l1x"]
            pe.wait_ge(s["qk_ready"], 8)
            cross(s, 2, project_kv, 2)
            pe.wait_ge(s["o_drained"], B * C)
            pe.wait_ge(s_projw, 1)
            project_tokens(w[:, 5], ringD, AT)
            pe.wait_ge(s_sq, 1)
            for t in range(TILES):
                for c in range(C):
                    i = pe.matmul(ps[:, 0, t:t + 1], QT[:, c, t * P:(t + 1) * P], k("ones"), start=(c == 0), stop=(c == C - 1))
            i.then_inc(s_squares, 1)

            transpose_tokens(0)
            transpose_tokens(1)
            wait_weights("l1a")
            pe.wait_ge(s_ret, 1)
            for h in range(2):
                project_features(h, W["l1a"][:, 0], ringD, KT)
            pe.wait_ge(s_ret, 2)
            for t in range(TILES):
                if t % 2 == 0:
                    bank = ringD.to_fill(pe)
                for c in range(C):
                    i = pe.transpose(ps[:, bank, (t % 2 * C + c) * P:(t % 2 * C + c + 1) * P], AT[:, c, t * P:(t + 1) * P], ident)
                if t % 2:
                    i.then_inc(s_fd, 1)

            transpose_tokens(0)
            transpose_tokens(1)
            pe.wait_ge(s_tree_lo, CH)

            def tree_logits(i):
                pe.wait_ge(s_xslot, i + 1)
                wge(pe, s_lread, i)
                for q in range(4):
                    for c in range(C):
                        w0 = c * WIDTH + q * (WIDTH // 4)
                        m = three_passes(ps[:, q, 0:WIDTH // 4], (x_hi, x_lo), (slice(None), c, slice(None)),
                                         (wi_hi, wi_lo), (slice(None), slice(w0, w0 + WIDTH // 4)), c == 0, c == C - 1)
                m.then_inc(s_logit, 1)

            def tree_rest(i, last):
                if not last:
                    tree_logits(i + 1)
                pe.wait_ge(s_path, i + 1)
                for q in range(4):
                    wge(pe, s_th, i * 4 + q - 1)
                    for j in range(4):
                        n = q * 4 + j
                        m = pe.transpose(ps[:, 4 + q % 2, j * P:(j + 1) * P], acts[:, n * P:(n + 1) * P], ident)
                    m.then_inc(s_tt, 1)
                if isinstance(i, int) and i == 0:
                    pe.wait_ge(s_tree_lo, 2 * CH)
                wge(pe, s_tx, i)
                for n in range(NB):
                    if n % 4 == 0:
                        pe.wait_ge(s_tc, i * 4 + n // 4 + 1)
                    m = three_passes(ps[:, 6, 0:D], (mt_hi, mt_lo), (slice(None), n, slice(None)),
                                     (wo_hi, wo_lo), (slice(None), slice(n * D, (n + 1) * D)), n == 0, n == NB - 1)
                m.then_inc(s_ty, 1)

            tree_logits(0)
            run_pipelined(pe, lambda i: tree_rest(i, isinstance(i, int) and i == TILES - 1), TILES)


        @block.scalar
        def _(act):
            ln = [0]

            def deviations(norms=1, drain=True):
                for stage, pair in staggered(2 * norms):
                    if stage % 2 == 0:
                        if drain and stage == 2 * norms - 2 and pair == TILES // 2 - 1:
                            drain_transposed(0)
                        ln[0] += 1
                        act.wait_ge(s_var, ln[0])
                        tt = slice(2 * pair, 2 * pair + 2)
                        act.activation(std[:, tt], mv[:, tt, 1], ACT.Sqrt, bias=k("eps")).then_inc(s_std, 1)

            def deviation_rms():
                ln[0] += 1
                act.wait_ge(s_var, ln[0])
                act.activation(std[:], rstd[:], ACT.Sqrt).then_inc(s_std, 1)

            def drain_transposed(pair):
                bank = ringA.to_drain(act)
                src = ps[:, bank, :].rearrange("p (t c n) -> p t c n", t=2, c=C)
                dst = XT[:, :, pair * 2 * P:(pair + 1) * 2 * P].rearrange("p c (t n) -> p t c n", t=2)
                act.activation(dst, src, ACT.Copy).then_inc(s_xt, 1)
                act.wait_ge(s_xt, ln_x[0] * TILES // 2 + pair + 1)
                act.sem_inc(s_da, 1)

            def drain_transposes(h):
                for pair in range(max(1, h * TILES // 4), (h + 1) * TILES // 4):
                    drain_transposed(pair)
                ln_x[0] += h
            ln_x = [0]

            def drain_features(h, dst, done, bias=None):
                for o in range(C):
                    bank = ringA.to_drain(act)
                    d = dst[:, o, h * BANK:(h + 1) * BANK]
                    if bias is None:
                        i = act.activation(d, ps[:, bank, :], ACT.Copy)
                    else:
                        i = act.activation(d, ps[:, bank, :], ACT.Identity, bias=bias[:, o:o + 1])
                    i.then_inc(s_da, 1)
                act.wait_ge(s_da, ringA.drains)
                act.sem_inc(done, 2)

            def drain_tokens(h, dst, done):
                for tt in range(h * TILES // 4, (h + 1) * TILES // 4):
                    bank = ringA.to_drain(act)
                    act.activation(dst[:, 2 * tt:2 * tt + 2, :].rearrange("p t d -> p (t d)"), ps[:, bank, :], ACT.Copy).then_inc(s_da, 1)
                act.wait_ge(s_da, ringA.drains)
                act.sem_inc(done, 2)

            def kv_drain(s, maps, bias):
                def drain_kv(b, item, at):
                    sl = b % 2
                    act.wait_ge(s["kv_filled"], at + 1)
                    if item == "v":
                        x = act.activation(vs[:, sl].rearrange("p h d -> p (h d)"), ps[:, 7, :], ACT.Copy)
                    elif bias is None:
                        x = act.activation(kts[:, sl, item].rearrange("p c n -> p (c n)"), ps[:, 7, :], ACT.Copy)
                    else:
                        for o in range(C):
                            x = act.activation(kts[:, sl, item, o], ps[:, 7, o * SK:(o + 1) * SK], ACT.Identity, bias=bias[:, o:o + 1])
                    x.then_inc(s["kv_drained"], 1)

                for n, (b, item) in enumerate(kv_first(maps)):
                    drain_kv(b, item, n)
                return drain_kv

            def cross(s, maps, drain_kv):
                fills = maps + 1

                def exps(i, u):
                    U = i * 8 + u
                    act.wait_ge(s["mx_ready"], U + 1)
                    for mp in range(maps):
                        for j in range(2):
                            if maps == 1:
                                src = sm[:, u % 4, j * SK:(j + 1) * SK]
                            else:
                                src = ps[:, (u % 2) * 2 + mp, j * SK:(j + 1) * SK]
                            dst = (p1, p2)[mp][:, u % 4, j * SK:(j + 1) * SK]
                            n = mp * 2 + j
                            x = act.activation(dst, src, ACT.Exp, bias=mx[:, u % 4, n:n + 1],
                                               accum_out=rs[:, u % 4, n:n + 1])
                    x.then_inc(s["exp_done"], 1)

                def evac(i, u):
                    U = i * 8 + u
                    act.wait_ge(s["pt_filled"], U + 1)
                    wge(act, s["pv_done"], U - 1)
                    act.activation(pts[:, u % 2, :], ps[:, 4 + u % 2, :], ACT.Copy).then_inc(s["pt_drained"], 1)

                for u in range(4):
                    exps(0, u)
                evac(0, 0)

                def body(i):
                    last = isinstance(i, int) and i == B // 2 - 1
                    for u in range(8):
                        if not (last and u + 1 >= 8):
                            evac(i, u + 1)
                        if not (last and u + 4 >= 8):
                            exps(i, u + 4)
                        for b, item, n in kv_step(maps, u, last):
                            drain_kv(b, item, i * 2 * fills + n)
                run_pipelined(act, body, B // 2)

            def self_attention(s):
                def exps(i, u):
                    U = i * 4 + u
                    act.wait_ge(s["mx_ready"], U + 1)
                    act.activation(p1[:, u % 4, :], sm[:, u % 4, :], ACT.Exp).then_inc(s["exp_done"], 1)

                def evac(i, u):
                    U = i * 4 + u
                    act.wait_ge(s["pt_filled"], U + 1)
                    wge(act, s["pv_done"], U - 1)
                    act.activation(pts[:, u % 2, :], ps[:, 4 + u % 2, :], ACT.Copy).then_inc(s["pt_drained"], 1)

                def extract(i, u):
                    act.wait_ge(s["pv_done"], i * 4 + u + 1)
                    if u % 2 == 0:
                        wge(act, s["proj_filled"], i * 2 + u // 2 - 1)
                    act.activation(AT[:, u % 2, u // 2 % 2 * P:(u // 2 % 2 + 1) * P], ps[:, 6 + u % 2, 0:P], ACT.Copy).then_inc(s["o_drained"], 1)

                for u in range(4):
                    exps(0, u)
                evac(0, 0)
                n = TILES // 2

                def body(i):
                    last = isinstance(i, int) and i == n - 1
                    for u in range(4):
                        if not (isinstance(i, int) and i == 0 and u == 0):
                            extract(i, u - 1)
                        if not (last and u + 1 >= 4):
                            evac(i, u + 1)
                        if not last:
                            exps(i, u + 4)
                run_pipelined(act, body, n)
                extract(n - 1, 3)

            act.wait_ge(s_in["vec"], 16)
            act.wait_ge(s_in["con"], 16)
            deviations(drain=False)
            drain_kv = kv_drain(st["l0x"], 1, v("bk"))
            drain_transposed(0)
            for h in range(2):
                drain_transposes(h)
                drain_features(h, QT, st["l0x"]["qk_ready"], v("bq"))
            cross(st["l0x"], 1, drain_kv)
            deviations()
            for h in range(2):
                drain_transposes(h)
                drain_tokens(h, VT, st["l0a"]["kv_drained"])
            self_attention(st["l0a"])
            deviations()
            for h in range(2):
                drain_transposes(h)
                drain_features(h, QT, st["l0f"]["qk_ready"])
                drain_features(h, KT, st["l0f"]["qk_ready"])
                drain_tokens(h, VT, st["l0f"]["kv_drained"])
            self_attention(st["l0f"])
            deviations()
            drain_transposes(0)
            drain_transposes(1)
            act.wait_ge(s_router, 1)
            act.activation(router[:, 1], router[:, 0], ACT.Exp).then_inc(s_router, 1)
            for h in range(2):
                bank = ringA.to_drain(act)
                act.activation(gwT[:, h * BANK:(h + 1) * BANK], ps[0:E, bank, :], ACT.Copy).then_inc(s_da, 1)
                act.wait_ge(s_da, ringA.drains)
                act.sem_inc(s_gwT, 1)

            def round_tokens(i, b):
                sl = b % 2
                act.wait_ge(s_xbT, i * 2 + b + 1)
                act.activation(xb_hi[:, sl].rearrange("p c n -> p (c n)"), ps[:, 6, :], ACT.Copy).then_inc(s_xhi, 1)

            def gelu(i, u):
                b = u // UB
                act.wait_ge(s_hid, i * 2 * UB + u + 1)
                wge(act, s_h1, i * 2 * UB + u - 1)
                if u % UB == 0:
                    act.wait_ge(s_b_in[b % 2], i * 16 + (b // 2 + 1) * 16)
                for mm in range(2):
                    m = u % UB * 2 + mm
                    x = act.activation(gact[:, u % 2, mm * SLOTS:(mm + 1) * SLOTS], ps[:, u % 4, mm * SLOTS:(mm + 1) * SLOTS],
                                       ACT.Gelu_apprx_tanh, bias=bb1s[:, b % 2, m:m + 1])
                x.then_inc(s_gelu, 1)

            def round_hidden(i, u):
                act.wait_ge(s_gelu, i * 2 * UB + u + 1)
                wge(act, s_y, i * 2 * UB + u - 1)
                act.activation(h_hi[:, u % 2, :], gact[:, u % 2, :], ACT.Copy).then_inc(s_hhi, 1)

            def store_block(i, b):
                sl = b % 2
                act.wait_ge(s_y, (i * 2 + b + 1) * UB)
                if b == 0:
                    wge(act, s_ys[0], i * 16)
                    wge(act, s_ys[1], i * 16)
                act.activation(yb[:, sl].rearrange("p s d -> p (s d)"), ps[:, 4 + sl, :], ACT.Copy).then_inc(s_yev, 1)
                act.wait_ge(s_yev, i * 2 + b + 1)
                dst = moe_out.rearrange("(b s p) d -> b p s d", s=2, p=P)[bass.ds(i * 2 + b, 1)].rearrange("o p s d -> (o p) s d")
                act.dma_start(dst, yb[:, sl]).then_inc(s_ys[sl], 16)

            def gelus(i):
                for u in range(2 * UB):
                    if left(i, u + 2):
                        gelu(i, u + 2)
                    if left(i, u + 1):
                        round_hidden(i, u + 1)
                    if u % UB == 0 and left(i, u - UB) and not (isinstance(i, int) and i == 0 and u == 0):
                        store_block(i, u // UB - 1)
                    if isinstance(i, int) and i == 0 and u == 0:
                        round_tokens(0, 1)
                    if u % UB == 2 and left(i, (u // UB + 2) * UB):
                        round_tokens(i, u // UB + 2)
            round_tokens(0, 0)
            gelu(0, 0)
            gelu(0, 1)
            round_hidden(0, 0)
            run_blocks(act, gelus)
            drain_kv = kv_drain(st["l1x"], 2, None)
            deviations(2)
            for h in range(2):
                drain_transposes(h)
                drain_features(h, QT, st["l1x"]["qk_ready"])
                drain_features(h, KT, st["l1x"]["qk_ready"])
            cross(st["l1x"], 2, drain_kv)
            act.wait_ge(s_in["vec"], 16)
            act.activation(dk[:, 0:2], v("decay"), ACT.Exp, scale=-1.0).then_inc(s_norm, 1)
            act.wait_ge(st["l1x"]["o_drained"], B * C)
            act.activation(QT[:], AT[:], ACT.Square).then_inc(s_sq, 1)
            deviation_rms()
            deviations()
            drain_transposes(0)
            drain_transposes(1)
            deviations()
            drain_transposes(0)
            drain_transposes(1)

            def trees(i):
                act.wait_ge(s_lread, i + 1)
                act.activation(nodes, logit, ACT.Silu).then_inc(s_silu, 1)
                for q in range(4):
                    act.wait_ge(s_tt, i * 4 + q + 1)
                    if q == 0:
                        wge(act, s_ty, i)
                    blocks = slice(4 * q, 4 * q + 4)
                    act.activation(mt_hi[:, blocks, :].rearrange("p j t -> p (j t)"), ps[:, 4 + q % 2, :], ACT.Copy)
                    act.activation(mt[:, blocks, :].rearrange("p j t -> p (j t)"), ps[:, 4 + q % 2, :], ACT.Copy).then_inc(s_th, 1)
            run_pipelined(act, trees, TILES)


        @block.vector
        def _(dve):
            chain = Chain(dve, s_dve)
            link = chain.link
            ln = [0]

            def layer_norms(*norms):
                def stats(src, dst, make, affine, done, pair):
                    if make is not None:
                        make(pair)
                    for t in (2 * pair, 2 * pair + 1):
                        i = dve.bn_stats(stat[:, t, :], src[:, t, :])
                    link(i)
                    for t in (2 * pair, 2 * pair + 1):
                        i = dve.bn_aggr(mv[:, t, :], stat[:, t, :])
                    i.then_inc(s_var, 1)
                    ln[0] += 1
                    ready[pair] = ln[0]

                def normalise(src, dst, make, affine, done, pair):
                    dve.wait_ge(s_std, ready[pair])
                    link(dve.reciprocal(rstd[:, 2 * pair:2 * pair + 2], std[:, 2 * pair:2 * pair + 2]))
                    for t in (2 * pair, 2 * pair + 1):
                        if affine is None:
                            i = dve.tensor_scalar(dst[:, t, :], src[:, t, :], mv[:, t, 0:1], rstd[:, t:t + 1], ALU.subtract, ALU.mult)
                        else:
                            i = dve.scalar_tensor_tensor(out=dst[:, t, :], in0=src[:, t, :], scalar=mv[:, t, 0:1],
                                                         in1=rows[:, ROWS.index(affine[0]), :], op0=ALU.subtract, op1=ALU.mult)
                        if affine is None and done is not None:
                            i.then_inc(done, 1)
                    if affine is not None:
                        link(i)
                        for t in (2 * pair, 2 * pair + 1):
                            i = dve.scalar_tensor_tensor(out=dst[:, t, :], in0=dst[:, t, :], scalar=rstd[:, t:t + 1],
                                                         in1=rows[:, ROWS.index(affine[1]), :], op0=ALU.mult, op1=ALU.add)
                            if done is not None:
                                i.then_inc(done, 1)
                    if done is None:
                        link(i)

                ready = {}
                for stage, pair in staggered(2 * len(norms)):
                    (stats, normalise)[stage % 2](*norms[stage // 2], pair)

            def add_bank(dst):
                def make(pair):
                    bank = ringD.to_drain(dve)
                    d = dst[:, 2 * pair:2 * pair + 2, :].rearrange("p t d -> p (t d)")
                    dve.tensor_tensor(d, ps[:, bank, :], d, ALU.add).then_inc(s_dd, 1)
                    dve.wait_ge(s_dd, ringD.drains)
                return make

            def row(n):
                return rows[:, ROWS.index(n), :].unsqueeze(1).broadcast_to([P, TILES, D])

            def add_tokens(dst):
                for tt in range(TILES // 2):
                    bank = ringD.to_drain(dve)
                    d = dst[:, 2 * tt:2 * tt + 2, :].rearrange("p t d -> p (t d)")
                    i = dve.tensor_tensor(d, ps[:, bank, :], d, ALU.add)
                    i.then_inc(s_dd, 1)
                dve.wait_ge(s_dd, ringD.drains)

            def cross(s, maps, bias):
                rows3 = lambda x: x.rearrange("p (j n) -> p j n", j=2)

                def mask_scores(i, u):
                    U = i * 8 + u
                    dve.wait_ge(s["s_done"], U + 1)
                    wge(dve, s["exp_done"], U - 3)
                    dve.tensor_tensor(rows3(sm[:, u % 4, :]), rows3(ps[:, u % 4, :]),
                                      bias_x[:].unsqueeze(1).broadcast_to([P, 2, SK]), ALU.add).then_inc(s["s_read"], 1)

                def maxes(i, u):
                    U = i * 8 + u
                    if maps == 1:
                        dve.wait_ge(s["s_read"], U + 1)
                        dve.tensor_reduce(mx[:, u % 4, 0:2], rows3(sm[:, u % 4, :]), X_AXIS, ALU.max, negate=True).then_inc(s["mx_ready"], 1)
                    else:
                        dve.wait_ge(s["s_done"], U + 1)
                        dve.tensor_reduce(mx[:, u % 4, 0:2], rows3(ps[:, u % 2 * 2, :]), X_AXIS, ALU.max, negate=True)
                        dve.tensor_reduce(mx[:, u % 4, 2:4], rows3(ps[:, u % 2 * 2 + 1, :]), X_AXIS, ALU.max, negate=True)\
                           .then_inc(s["mx_ready"], 1)

                def sums_inverse(i, u):
                    U = i * 8 + u
                    dve.wait_ge(s["exp_done"], U + 1)
                    dve.reciprocal(ri[:, u % 2, 0:2 * maps], rs[:, u % 4, 0:2 * maps]).then_inc(s["ri_ready"], 1)

                def divide(i, u, j):
                    U = i * 8 + u
                    if j == 0:
                        dve.wait_ge(s["ri_ready"], U + 1)
                    d = p1[:, u % 4, j * SK:(j + 1) * SK]
                    x = dve.tensor_scalar(d, d, ri[:, u % 2, j:j + 1], None, ALU.mult)
                    if j == 1:
                        x.then_inc(s["p_ready"], 1)

                def divide_second(i, u):
                    U, pr = i * 8 + u, u % 4 * 2
                    dve.wait_ge(s["ri_ready"], U + 1)
                    for j in range(2):
                        x = dve.tensor_scalar(p2[:, u % 4, j * SK:(j + 1) * SK], p2[:, u % 4, j * SK:(j + 1) * SK],
                                              ri[:, u % 2, 2 + j:3 + j], lam[:, pr + j:pr + j + 1], ALU.mult, ALU.mult)
                    x.then_inc(s["p2_ready"], 1)

                def subtract_second(i, u):
                    dve.wait_ge(s["p2_ready"], i * 8 + u + 1)
                    for j in range(2):
                        d = p1[:, u % 4, j * SK:(j + 1) * SK]
                        x = dve.scalar_tensor_tensor(out=d, in0=d, scalar=ri[:, u % 2, j:j + 1],
                                                     in1=p2[:, u % 4, j * SK:(j + 1) * SK], op0=ALU.mult, op1=ALU.subtract)
                    x.then_inc(s["p_ready"], 1)

                def extract_even(i, u):
                    dve.wait_ge(s["pv_done"], i * 8 + u + 1)
                    if bias is None:
                        x = dve.tensor_scalar(tmp[:, 0, :], ps[:, 6, 0:S], k("even"), None, ALU.mult)
                    else:
                        g = u // 2 % 2
                        x = dve.tensor_scalar(tmp[:, 0, :], ps[:, 6, 0:S], k("even"), bias[:, g:g + 1], ALU.mult, ALU.add)
                    x.then_inc(s["even_ready"], 1)

                def extract_odd(i, u):
                    g, b = u // 2 % 2, i * 2 + u // 4
                    dve.wait_ge(s["even_ready"], i * 4 + (u + 1) // 2)
                    dve.scalar_tensor_tensor(out=AT[:, g, bass.ds(b * S, S)], in0=ps[:, 6, S:2 * S], scalar=k("odd"), in1=tmp[:, 0, :],
                                             op0=ALU.mult, op1=ALU.add).then_inc(s["o_drained"], 1)

                def step(i, u):
                    top = i * 8 + u + 4 < B * 4 if isinstance(i, int) else True
                    mid = i * 8 + u + 2 < B * 4 and i * 8 + u + 2 >= 0 if isinstance(i, int) else True
                    own = u % 2 == 0 and not (isinstance(i, int) and i * 8 + u <= 0)
                    if mid:
                        sums_inverse(i, u + 2)
                    if own:
                        extract_even(i, u - 1)
                    if maps == 1:
                        if mid:
                            divide(i, u + 2, 0)
                        if own:
                            extract_odd(i, u - 1)
                        if top:
                            mask_scores(i, u + 4)
                        if mid:
                            divide(i, u + 2, 1)
                    else:
                        if mid:
                            divide_second(i, u + 2)
                        if own:
                            extract_odd(i, u - 1)
                        if mid:
                            subtract_second(i, u + 2)
                    if top:
                        maxes(i, u + 4)

                for u in range(-4, 0):
                    step(0, u)

                def body(i):
                    for u in range(8):
                        step(i, u)
                run_pipelined(dve, body, B // 2)
                extract_even(B // 2 - 1, 7)
                extract_odd(B // 2 - 1, 7)

            def self_attention(s, resid):
                rows8 = lambda x: x.rearrange("p (j n) -> p j n", j=8)


                def maxes(i, u):
                    dve.wait_ge(s["s_done"], i * 4 + u + 1)
                    dve.tensor_reduce(mx[:, u % 4, :], rows8(ps[:, u % 4, :]), X_AXIS, ALU.max, negate=True).then_inc(s["max_ready"], 1)

                def subtract_maxes(i, u):
                    U = i * 4 + u
                    dve.wait_ge(s["max_ready"], U + 1)
                    wge(dve, s["exp_done"], U - 3)
                    dve.tensor_tensor(rows8(sm[:, u % 4, :]), rows8(ps[:, u % 4, :]),
                                      mx[:, u % 4, :].unsqueeze(2).broadcast_to([P, 8, S]), ALU.add).then_inc(s["mx_ready"], 1)

                def sums(i, u):
                    dve.wait_ge(s["exp_done"], i * 4 + u + 1)
                    dve.tensor_reduce(rs[:, u % 4, :], rows8(p1[:, u % 4, :]), X_AXIS, ALU.add).then_inc(s["sum_ready"], 1)

                def sums_inverse(i, u):
                    dve.wait_ge(s["sum_ready"], i * 4 + u + 1)
                    dve.reciprocal(ri[:, u % 2, :], rs[:, u % 4, :]).then_inc(s["ri_ready"], 1)

                def divide(i, u):
                    dve.wait_ge(s["ri_ready"], i * 4 + u + 1)
                    p3 = rows8(p1[:, u % 4, :])
                    dve.tensor_tensor(p3, p3, ri[:, u % 2, :].unsqueeze(2).broadcast_to([P, 8, S]), ALU.mult).then_inc(s["p_ready"], 1)

                def add_projected(i, tt):
                    T = i * 2 + tt
                    dve.wait_ge(s["proj_filled"], T + 1)
                    dve.wait_ge(s["o_drained"], min(T * 2 + 4, TILES * C) if isinstance(T, int) else T * 2 + 4)
                    x = resid[:].rearrange("p t d -> p (t d)")[:, bass.ds(T * D, D)] if not isinstance(T, int) else resid[:, T, :]
                    dve.tensor_tensor(x, ps[:, 7, P:P + D], x, ALU.add).then_inc(s["proj_drained"], 1)

                n = TILES // 2

                def step(i, u):
                    top = i * 4 + u + 4 < n * 4 if isinstance(i, int) else True
                    mid = 0 <= i * 4 + u + 2 < n * 4 if isinstance(i, int) else True
                    if mid:
                        sums(i, u + 2)
                    if mid:
                        sums_inverse(i, u + 2)
                    if top:
                        maxes(i, u + 4)
                    if mid:
                        divide(i, u + 2)
                    if top:
                        subtract_maxes(i, u + 4)
                    if u % 2 == 0 and not (isinstance(i, int) and i * 4 + u <= 2):
                        add_projected(i, u // 2 - 2)

                for u in range(-4, 0):
                    step(0, u)

                def body(i):
                    for u in range(4):
                        step(i, u)
                run_pipelined(dve, body, n)
                add_projected(n, -2)
                add_projected(n, -1)
                dve.wait_ge(s["proj_drained"], TILES)

            dve.wait_ge(s_in["x"], 16)
            layer_norms((X, XN, None, None, s_xn))
            dve.wait_ge(s_in["con"], 16)
            dve.tensor_copy(mask16[:], k("causal")).then_inc(s_mask16, 1)
            dve.tensor_copy(ident16[:], ident).then_inc(s_mask16, 1)
            dve.wait_ge(s_in["mask"], 16)
            dve.wait_ge(s_in["con"], 16)
            dve.wait_ge(s_in["vec"], 16)
            dve.wait_ge(s_in["rows"], 16)
            link(dve.tensor_scalar(bias_x[:], maskb[:], 1.0, -MASKED, ALU.subtract, ALU.mult))
            dve.wait_ge(s_xn, TILES)
            link(dve.tensor_tensor(X[:], X[:], row("xattn_bo"), ALU.add))
            link(dve.tensor_tensor(lam[:], v("lam1"), v("lam2"), ALU.subtract))
            link(dve.tensor_scalar(lam[:], lam[:], 0.1, None, ALU.add))
            cross(st["l0x"], 1, v("bv"))

            layer_norms((X, XN, add_bank(X), None, s_xn))
            cos = k("cos").unsqueeze(1).broadcast_to([P, BANK // S, S])
            sin = k("sin").unsqueeze(1).broadcast_to([P, BANK // S, S])
            dve.wait_ge(s_xn, 2 * TILES)
            for h in range(2):
                for o in range(C):
                    for dst in (QT, KT):
                        d = dst[:, o, h * BANK:(h + 1) * BANK].rearrange("p (b s) -> p b s", s=S)
                        bank = ringD.to_drain(dve)
                        dve.tensor_tensor(d, ps[:, bank, :].rearrange("p (b s) -> p b s", s=S), cos, ALU.mult).then_inc(s_dd, 1)
                        bank = ringD.to_drain(dve)
                        t3 = sm[:, 0, :].rearrange("p (b s) -> p b s", s=S)
                        dve.tensor_tensor(t3, ps[:, bank, :].rearrange("p (b s) -> p b s", s=S), sin, ALU.mult).then_inc(s_dd, 1)
                        dve.wait_ge(s_dd, ringD.drains)
                        i = dve.tensor_tensor(d, d, t3, ALU.add)
                        if o == C - 1 and dst is KT:
                            i.then_inc(st["l0a"]["qk_ready"], 1)
                            dve.wait_ge(st["l0a"]["qk_ready"], h + 1)
                        else:
                            link(i)
            self_attention(st["l0a"], X)

            layer_norms((X, XN, None, None, s_xn))
            dve.wait_ge(s_xn, 3 * TILES)
            self_attention(st["l0f"], XN)
            layer_norms((XN, XN, None, ("ffn_g1", "ffn_b1"), s_xn))
            bank = ringD.to_drain(dve)
            lg = ps[:, bank, 0:TILES * E].rearrange("p (t e) -> p t e", e=E)
            r0, r1, r2, r3 = (router[:, n] for n in range(4))
            link(dve.tensor_reduce(ri[:, 0, :], lg, X_AXIS, ALU.max))
            dve.tensor_tensor(r0, lg, ri[:, 0, :].unsqueeze(2).broadcast_to([P, TILES, E]), ALU.subtract).then_inc(s_router, 1)
            dve.wait_ge(s_router, 2)
            dve.sem_inc(s_dd, 1)
            link(dve.tensor_reduce(ri[:, 0, :], r1, X_AXIS, ALU.add))
            link(dve.reciprocal(ri[:, 1, :], ri[:, 0, :]))
            link(dve.tensor_tensor(r2, r1, ri[:, 1, :].unsqueeze(2).broadcast_to([P, TILES, E]), ALU.mult))
            mine = r2.unsqueeze(3).broadcast_to([P, TILES, E, E])
            other = r2.unsqueeze(2).broadcast_to([P, TILES, E, E])
            g4 = rk[:, 0, :].rearrange("p (t e j) -> p t e j", t=TILES, e=E)
            e4 = rk[:, 1, :].rearrange("p (t e j) -> p t e j", t=TILES, e=E)
            dve.tensor_tensor(g4, other, mine, ALU.is_gt)
            link(dve.tensor_tensor(e4, other, mine, ALU.is_equal))
            bef = k("before").unsqueeze(1).broadcast_to([P, TILES, E * E])
            e3 = rk[:, 1, :].rearrange("p (t n) -> p t n", t=TILES)
            link(dve.tensor_tensor(e3, e3, bef, ALU.mult))
            link(dve.tensor_tensor(rk[:, 0, :], rk[:, 0, :], rk[:, 1, :], ALU.add))
            link(dve.tensor_reduce(r3, g4, X_AXIS, ALU.add))
            chosen = rt[:, 0, :].rearrange("p (t e) -> p t e", e=E)
            dve.tensor_scalar(chosen, r3, TOP - 0.5, None, ALU.is_lt).then_inc(s_sel, 1)
            dve.wait_ge(s_sel, 1)
            link(dve.tensor_tensor(r3, chosen, r2, ALU.mult))
            link(dve.tensor_reduce(ri[:, 0, :], r3, X_AXIS, ALU.add))
            link(dve.reciprocal(ri[:, 1, :], ri[:, 0, :]))
            dve.tensor_tensor(gw[:], r3, ri[:, 1, :].unsqueeze(2).broadcast_to([P, TILES, E]), ALU.mult).then_inc(s_gw, 1)
            bank = ringD.to_drain(dve)
            rank = ps[:, bank, 0:TILES * E]
            link(dve.memset(off[:, 0, :], 0.0))
            for t in range(TILES):
                link(dve.tensor_tensor(off[:, t + 1, :], off[:, t, :], ps[:, bank, (TILES + t) * E:(TILES + t + 1) * E], ALU.add))
            steps, nb, end, base = N // SLOTS, rb[:, 0, :], rb[:, 1, :], rb[:, 2, :]
            over = rc[:, 0:E * steps].rearrange("p (e j) -> p e j", j=steps)
            link(dve.tensor_tensor(over, off[:, TILES, :].unsqueeze(2).broadcast_to([P, E, steps]),
                                   k("steps").unsqueeze(1).broadcast_to([P, E, steps]), ALU.is_gt))
            link(dve.tensor_reduce(nb, over, X_AXIS, ALU.add))
            link(dve.memset(rb[:, 3, :], 1.0))
            link(dve.tensor_tensor_scan(end, rb[:, 3, :], nb, 0.0, ALU.mult, ALU.add))
            link(dve.tensor_tensor(base, end, nb, ALU.subtract))
            link(dve.tensor_scalar(base, base, float(SLOTS), None, ALU.mult))
            o3 = rt[:, 1, :].rearrange("p (t e) -> p t e", e=E)
            link(dve.tensor_tensor(o3, off[:, 0:TILES, :], base.unsqueeze(1).broadcast_to([P, TILES, E]), ALU.add))
            dve.tensor_tensor(rt[:, 2, :], rank, rt[:, 1, :], ALU.add).then_inc(s_dd, 1)
            dve.wait_ge(s_dd, ringD.drains)
            picks = ((ALU.min, FAR), (ALU.max, 0.0))
            keys = [rt[:, 3 + n, :] for n in range(TOP)]
            for n, (op, far) in enumerate(picks):
                i = dve.scalar_tensor_tensor(out=keys[n], in0=rt[:, 2, :], scalar=-far, in1=rt[:, 0, :], op0=ALU.add, op1=ALU.mult)
            link(i)
            for n, (op, far) in enumerate(picks):
                i = dve.tensor_reduce(slotf[:, n, :], keys[n].rearrange("p (t e) -> p t e", e=E), X_AXIS, op)
            link(i)
            for n, (op, far) in enumerate(picks):
                i = dve.tensor_scalar(slotc[:, n, :], slotf[:, n, :], far, float(NSLOT - 1), ALU.add, ALU.min)
            link(i)
            dve.tensor_copy(slot[:], slotc[:]).then_inc(s_slot, 1)
            bl = rc[:, :].rearrange("p (b e) -> p b e", e=E)
            link(dve.tensor_tensor(bl, k("blocks").unsqueeze(2).broadcast_to([P, NBLK, E]),
                                   end.unsqueeze(1).broadcast_to([P, NBLK, E]), ALU.is_ge))
            link(dve.tensor_reduce(blkf[:], bl, X_AXIS, ALU.add))
            link(dve.tensor_scalar(blkf[:], blkf[:], float(E - 1), None, ALU.min))
            dve.tensor_copy(blk[:], blkf[:]).then_inc(s_blk, 1)
            own = rt[:, 5, :].rearrange("p (t e) -> p t e", e=E)
            for n in range(TOP):
                link(dve.tensor_tensor(own, keys[n].rearrange("p (t e) -> p t e", e=E),
                                       slotf[:, n, :].unsqueeze(2).broadcast_to([P, TILES, E]), ALU.is_equal))
                link(dve.tensor_tensor(own, own, gw[:], ALU.mult))
                link(dve.tensor_reduce(gate[:, n, :], own, X_AXIS, ALU.add))
            dve.wait_ge(s_scat, 16 * TOP * TILES)
            add_tokens(XN)

            def tokens_rest(i, b):
                sl = b % 2
                dve.wait_ge(s_xhi, i * 2 + b + 1)
                dve.tensor_tensor(xb_lo[:, sl].rearrange("p c n -> p (c n)"), ps[:, 6, :],
                                  xb_hi[:, sl].bitcast(F32).rearrange("p c n -> p (c n)"), ALU.subtract).then_inc(s_xlo, 1)

            def hidden_rest(i, u):
                dve.wait_ge(s_hhi, i * 2 * UB + u + 1)
                dve.tensor_tensor(h_lo[:, u % 2, :], gact[:, u % 2, :], h_hi[:, u % 2, :].bitcast(F32), ALU.subtract)\
                   .then_inc(s_h1, 1)

            def weights_rest(i, g, n):
                dve.wait_ge(s_whi, i * 4 * CH + g * CH + n + 1)
                cols = slice(n * WG // CH, (n + 1) * WG // CH)
                dve.tensor_tensor(w_lo[:, g % 4, cols], wraw[:, g % 4, cols], w_hi[:, g % 4, cols].bitcast(F32), ALU.subtract)\
                   .then_inc(s_wlo, 1)

            def rests(i):
                for u in range(2 * UB):
                    if left(i, u + 1):
                        hidden_rest(i, u + 1)
                    if left(i, (u // 2 + 3) * 2):
                        for n in range(2):
                            weights_rest(i, u // 2 + 3, u % 2 * 2 + n)
                    if isinstance(i, int) and i == 0 and u == 0:
                        tokens_rest(0, 1)
                    if u % UB == 2 and left(i, (u // UB + 2) * UB):
                        tokens_rest(i, u // UB + 2)
            tokens_rest(0, 0)
            for g in range(3):
                if g == 2:
                    hidden_rest(0, 0)
                for n in range(CH):
                    weights_rest(0, g, n)
            run_blocks(dve, rests)
            def add_outputs(pair):
                dve.wait_ge(s_pick[pair], 2 * 16 * TOP)
                for n in range(TOP):
                    for t in (2 * pair, 2 * pair + 1):
                        i = dve.scalar_tensor_tensor(out=XN[:, t, :], in0=picked[:, n, t, :], scalar=gate[:, n, t:t + 1],
                                                     in1=XN[:, t, :], op0=ALU.mult, op1=ALU.add)
                    link(i)

            def add_residual(pair):
                tt = slice(2 * pair, 2 * pair + 2)
                link(dve.tensor_tensor(X[:, tt, :], X[:, tt, :], XN[:, tt, :], ALU.add))

            layer_norms((XN, XN, add_outputs, ("ffn_g2", "ffn_b2"), None), (X, XN, add_residual, None, s_xn))
            dve.wait_ge(s_xn, 5 * TILES)
            link(dve.tensor_tensor(X[:], X[:], row("proj_b"), ALU.add))
            cross(st["l1x"], 2, None)
            dve.wait_ge(s_w[1], 32)
            for c in range(C):
                wp = W["l1x"][:, 5, c, :]
                i = dve.tensor_scalar(wp, wp, v("norm_w")[:, c:c + 1], None, ALU.mult)
            i.then_inc(s_projw, 1)
            dve.wait_ge(s_squares, 1)
            ln[0] += 1
            dve.tensor_scalar(rstd[:], ps[:, 0, 0:TILES], 1.0 / D, 1e-6, ALU.mult, ALU.add).then_inc(s_var, 1)
            dve.wait_ge(s_std, ln[0])
            link(dve.reciprocal(rstd_rms[:], std[:]))

            def add_projected(pair):
                bank = ringD.to_drain(dve)
                for t in range(2):
                    i = dve.scalar_tensor_tensor(out=X[:, 2 * pair + t, :], in0=ps[:, bank, t * D:(t + 1) * D],
                                                 scalar=rstd_rms[:, 2 * pair + t:2 * pair + t + 1], in1=X[:, 2 * pair + t, :],
                                                 op0=ALU.mult, op1=ALU.add)
                i.then_inc(s_dd, 1)
                dve.wait_ge(s_dd, ringD.drains)

            layer_norms((X, XN, add_projected, None, s_xn))
            dve.wait_ge(s_norm, 1)
            dve.wait_ge(s_xn, 6 * TILES)
            link(dve.tensor_scalar(dk[:, 2:4], dk[:, 0:2], 1.0, None, ALU.add))
            link(dve.reciprocal(dk[:, 4:6], dk[:, 2:4]))
            link(dve.tensor_scalar(dk[:, 6:8], dk[:, 4:6], -1.0, 1.0, ALU.mult, ALU.add))
            dve.tensor_tensor(dk[:, 0:2], v("ret_b"), v("conv_b"), ALU.add).then_inc(s_dk, 1)
            dve.wait_ge(s_dk, 1)
            da = big_b[:, 0:C * N].rearrange("p (c n) -> p c n", c=C)
            dx = big_b[:, C * N:2 * C * N].rearrange("p (c n) -> p c n", c=C)
            dve.wait_ge(s_xt, 6 * TILES // 2)
            for c in range(C):
                dve.tensor_scalar(dx[:, c, :], XT[:, c, :], dk[:, 6 + c:7 + c], None, ALU.mult)
                dve.tensor_scalar(da[:, c, :], XT[:, c, :], 0.0, dk[:, 4 + c:5 + c], ALU.mult, ALU.add)
            link(dve.memset(tmp[:, 0, :], 0.0))
            link(dve.tensor_copy(da.rearrange("p c (b s) -> p (c b) s", s=S)[:, :, 0], tmp[:, 0, 0:C * B]))
            for c in range(C):
                i = dve.tensor_tensor_scan(KT[:, c, :], da[:, c, :], dx[:, c, :], 0.0, ALU.mult, ALU.add)
            i.then_inc(s_ret, 1)
            for pair in zip(convolution(dve, 0), convolution(dve, 1)):
                link(pair[1])
            for h in range(2):
                for o in range(C):
                    bank = ringD.to_drain(dve)
                    i = dve.tensor_tensor(AT[:, o, h * BANK:(h + 1) * BANK], ps[:, bank, :], QT[:, o, h * BANK:(h + 1) * BANK], ALU.add)
                    i.then_inc(s_dd, 1)
            dve.wait_ge(s_dd, ringD.drains)
            dve.sem_inc(s_ret, 1)

            layer_norms((X, XN, add_bank(X), None, s_xn))
            link(dve.memset(acts[:, WIDTH:], 0.0))
            dve.wait_ge(s_tree_b, 16)

            def tree3(ap):
                return ap.rearrange("p (t n) -> p t n", t=TREES)

            def split_tile(i):
                wge(dve, s_logit, i)
                dve.tensor_tensor(xslot[:], XT[:, :, bass.ds(i * P, P)], k("ones").unsqueeze(2).broadcast_to([P, C, P]), ALU.mult).then_inc(s_xh, 1)
                dve.wait_ge(s_xh, i * 2 + 1)
                dve.tensor_tensor(x_hi[:], xslot[:], k("ones").unsqueeze(2).broadcast_to([P, C, P]), ALU.mult).then_inc(s_xh, 1)
                dve.wait_ge(s_xh, i * 2 + 2)
                dve.tensor_tensor(x_lo[:], xslot[:], x_hi[:].bitcast(F32), ALU.subtract).then_inc(s_xslot, 1)

            def trees(i):
                dve.wait_ge(s_logit, i + 1)
                wge(dve, s_silu, i)
                q3 = ps[:, 0:4, 0:WIDTH // 4]
                dve.tensor_tensor(logit.rearrange("p (q n) -> p q n", q=4), q3, bin_b.rearrange("p (q n) -> p q n", q=4), ALU.add)\
                   .then_inc(s_lread, 1)
                if not (isinstance(i, int) and i == TILES - 1):
                    split_tile(i + 1)
                dve.wait_ge(s_lread, i + 1)
                link(dve.tensor_scalar(dec, logit, 0.0, None, ALU.is_gt))
                link(dve.tensor_scalar(tree3(path)[:, :, 0:1], tree3(logit)[:, :, 0:1], 0.0, 1.0, ALU.mult, ALU.add))
                for d in range(DEPTH):
                    n0, n1, w = 2 ** d - 1, 2 ** (d + 1) - 1, 2 ** d
                    par, de = tree3(path)[:, :, n0:n0 + w], tree3(dec)[:, :, n0:n0 + w]
                    kids = tree3(path)[:, :, n1:n1 + 2 * w]
                    left, right = kids[:, :, 0:2 * w:2], kids[:, :, 1:2 * w:2]
                    link(dve.tensor_tensor(right, par, de, ALU.mult))
                    link(dve.tensor_tensor(left, par, right, ALU.subtract))
                dve.wait_ge(s_silu, i + 1)
                dve.tensor_tensor(nodes, nodes, path, ALU.mult).then_inc(s_path, 1)
                if not (isinstance(i, int) and i == 0):
                    add_trees(i - 1)

            def add_trees(i):
                dve.wait_ge(s_ty, i + 1)
                xt = X[:].rearrange("p t d -> p (t d)")[:, bass.ds(i * D, D)]
                dve.tensor_tensor(xt, ps[:, 6, 0:D], xt, ALU.add).then_inc(s_tx, 1)
            dve.wait_ge(s_xt, 7 * TILES // 2)
            split_tile(0)
            run_pipelined(dve, trees, TILES, chain)
            add_trees(TILES - 1)

        @block.gpsimd
        def _(pool):
            head = k("head").unsqueeze(2).broadcast_to([P, HG, S])

            def queries(src, off):
                return src[:, bass.ds(off, S)].unsqueeze(1).broadcast_to([P, HG, S])

            def split_ctx(s, maps, i, b):
                sl = b % 2
                pool.wait_ge(s[f"ctx{sl}"], (i + b // 2) * 16 + 16)
                wge(pool, s["kv_filled"], (i * 2 + b - 1) * (maps + 1))
                pool.tensor_tensor(ctx_hi[:, sl].rearrange("p c n -> p (c n)"), ctxs[:, sl].rearrange("p c n -> p (c n)"),
                                   k("ones").broadcast_to([P, C * SK]), ALU.mult).then_inc(s["ctx_rounded"], 1)
                pool.wait_ge(s["ctx_rounded"], i * 2 + b + 1)
                pool.tensor_tensor(ctx_lo[:, sl], ctxs[:, sl], ctx_hi[:, sl].bitcast(F32), ALU.subtract).then_inc(s["ctx_split"], 1)

            def split_projections(s, w, maps):
                for n in range(maps + 1):
                    pool.tensor_tensor(kv_hi[:, n].rearrange("p c d -> p (c d)"), w[:, n].rearrange("p c d -> p (c d)"),
                                       k("ones").broadcast_to([P, C * D]), ALU.mult).then_inc(s["w_split"], 1)
                for n in range(maps + 1):
                    pool.wait_ge(s["w_split"], n + 1)
                    pool.tensor_tensor(kv_lo[:, n], w[:, n], kv_hi[:, n].bitcast(F32), ALU.subtract).then_inc(s["w_split"], 1)
                for b in range(2):
                    split_ctx(s, maps, 0, b)

            def mask_cross(s, maps):
                pool.wait_ge(s["qk_ready"], 2 * maps)

                def body(i):
                    for sl in range(2):
                        wge(pool, s["s_done"], i * 8 + 4 * (sl - 1))
                        for g in range(C):
                            for mp in range(maps):
                                src = (QT, KT)[mp][:, g, :]
                                x = pool.tensor_tensor(qm[:, sl, mp, g], queries(src, (i * 2 + sl) * S), head, ALU.mult)
                            x.then_inc(s["qm_ready"], 1)
                        if not (isinstance(i, int) and (i * 2 + sl == 0 or i * 2 + sl == B - 1)):
                            split_ctx(s, maps, i, sl + 1)
                    if isinstance(i, int) and i == 0:
                        pool.wait_ge(s["qk_ready"], 4 * maps)
                run_pipelined(pool, body, B // 2)

            def mask_self(s, ready):
                pool.wait_ge(s["qk_ready"], ready // 2)
                half = k("half").unsqueeze(1).unsqueeze(3).broadcast_to([P, 2 * D // (2 * HD), 2, HD])

                def tile_values(i, tu):
                    before = i * 4 + tu * 2 - 2
                    if isinstance(before, int):
                        wge(pool, s["pv_done"], before)
                    else:
                        pool.wait_ge(s["s_done"], before + 5)
                    src = VH.rearrange("p t b d -> p (t b d)")[:, bass.ds(i * (4 * D) + tu * 2 * D, 2 * D)]
                    pool.tensor_tensor(vs[:, tu % 2].rearrange("p b (j n d) -> p (b j) n d", n=2, d=HD),
                                       src.rearrange("p (j n d) -> p j n d", n=2, d=HD), half, ALU.mult).then_inc(s["v_ready"], 1)

                def body(i):
                    for u in range(4):
                        wge(pool, s["s_done"], i * 4 + u - 1)
                        here = bass.ds((i * 2 + u // 2) * P, P)
                        pool.tensor_tensor(qs[:, u % 4, :], QT[:, u % 2, here], k("ones").broadcast_to([P, P]), ALU.mult)
                        pool.tensor_tensor(km[:, u % 2], KT[:, u % 2, here].rearrange("p (b s) -> p b s", b=2).unsqueeze(2).broadcast_to([P, 2, HG, S]),
                                           head.unsqueeze(1).broadcast_to([P, 2, HG, S]), ALU.mult).then_inc(s["qm_ready"], 1)
                        if u % 2 == 1 and not (isinstance(i, int) and i == 0 and u == 1):
                            if isinstance(i, int) and i == 0 and u == 3:
                                pool.wait_ge(s["v_doubled"], 4 * 16)
                            tile_values(i, u // 2 - 1)
                    if isinstance(i, int) and i == 0:
                        pool.wait_ge(s["qk_ready"], ready)
                run_pipelined(pool, body, TILES // 2)
                tile_values(TILES // 2, -1)

            pool.memset(big_b[:, 0:NSLOT // P * D], 0.0).then_inc(s_zmem, 1)
            pool.wait_ge(s_in["con"], 16)
            pool.wait_ge(s_w[0], 16)
            split_projections(st["l0x"], W["l0x"][:, 1:3], 1)
            mask_cross(st["l0x"], 1)
            mask_self(st["l0a"], 2)
            mask_self(st["l0f"], 8)


            pool.wait_ge(s_slot, 1)
            pool.wait_ge(s_zero, 16)
            for n in range(TOP):
                for t in range(TILES):
                    pool.indirect_dma_start(moe_in, bass.IndirectOffsetOnAxis(slot[:, n, t:t + 1], 0), XN[:, t, :], None).then_inc(s_scat, 16)

            def round_weights(i, g):
                pool.wait_ge(s_e_in[g], i * 16 + 16)
                wge(pool, s_y, i * 2 * UB + 2 * (g - 3))
                for n in range(CH):
                    cols = slice(n * WG // CH, (n + 1) * WG // CH)
                    pool.tensor_tensor(w_hi[:, g, cols], wraw[:, g, cols], k("ones").broadcast_to([P, WG // CH]), ALU.mult).then_inc(s_whi, 1)

            def rounds(i):
                for g in range(4):
                    if left(i, 2 * g):
                        round_weights(i, g)
            run_blocks(pool, rounds)
            pool.wait_ge(s_wlo, CH * 2 * NBLK)
            pool.wait_ge(s_w[1], 32)
            split_projections(st["l1x"], W["l1x"][:, 2:5], 2)
            pool.wait_ge(s_ys[0], 16 * ((NBLK + 1) // 2))
            pool.wait_ge(s_ys[1], 16 * (NBLK // 2))
            for t in range(TILES):
                for n in range(TOP):
                    pool.indirect_dma_start(picked[:, n, t, :], None, moe_out, bass.IndirectOffsetOnAxis(slot[:, n, t:t + 1], 0)).then_inc(s_pick[t // 2], 16)
            mask_cross(st["l1x"], 2)
            pool.wait_ge(st["l1x"]["o_drained"], B * C)
            pool.wait_ge(s_tree_w, 32)
            for r, (raw, hi, lo) in enumerate(((win, wi_hi, wi_lo), (wout, wo_hi, wo_lo))):
                w = raw.shape[1] // CH
                for n in range(CH):
                    cols = slice(n * w, (n + 1) * w)
                    pool.tensor_tensor(hi[:, cols], raw[:, cols], k("ones").broadcast_to([P, w]), ALU.mult).then_inc(s_tree_hi, 1)
                for n in range(CH):
                    cols = slice(n * w, (n + 1) * w)
                    pool.wait_ge(s_tree_hi, r * CH + n + 1)
                    pool.tensor_tensor(lo[:, cols], raw[:, cols], hi[:, cols].bitcast(F32), ALU.subtract).then_inc(s_tree_lo, 1)

            def split_nodes(i):
                for q in range(4):
                    pool.wait_ge(s_th, i * 4 + q + 1)
                    if q == 0:
                        wge(pool, s_ty, i)
                    blocks = slice(4 * q, 4 * q + 4)
                    pool.tensor_tensor(mt_lo[:, blocks, :], mt[:, blocks, :], mt_hi[:, blocks, :].bitcast(F32), ALU.subtract).then_inc(s_tc, 1)

            run_pipelined(pool, split_nodes, TILES)


def _kmaj(w):
    i, o = w.shape
    return np.ascontiguousarray(w.reshape(i // P, P, o).transpose(1, 0, 2).reshape(P, -1))


def _col(v):
    return np.ascontiguousarray(v.reshape(-1, P).T)


def _constants():
    con = np.zeros((P, NCON), np.float32)
    p = np.arange(P)

    def put(name, val):
        lo, hi = CON[name]
        con[:, lo:hi] = val
    put("ident", np.eye(P))
    put("head", SCALE * ((p[:, None] // HD) == np.arange(HG)[None, :]))
    put("even", ((p // HD) % 2 == 0)[:, None])
    put("odd", ((p // HD) % 2 == 1)[:, None])
    put("causal", np.where(np.arange(S)[None, :] <= (p % S)[:, None], 0.0, MASKED))
    freqs = np.exp(np.arange(HD // 2, dtype=np.float32) * np.float32(-np.log(10000.0) * 2.0 / HD)).astype(np.float32)
    ang = (np.arange(S, dtype=np.float32)[None, :] * freqs[(p % HD) // 2][:, None]).astype(np.float32)
    put("cos", np.cos(ang))
    put("sin", np.sin(ang) * np.where(p % 2 == 0, -1.0, 1.0)[:, None])
    put("ones", 1.0)
    put("eps", 1e-5)
    put("half", (p // S)[:, None] == np.arange(2)[None, :])
    put("earlier", p[:, None] < p[None, :])
    put("all", 1.0)
    put("steps", SLOTS * np.arange(N // SLOTS)[None, :])
    put("blocks", np.arange(NBLK)[None, :])
    put("before", np.broadcast_to((np.arange(E)[None, :] < np.arange(E)[:, None]).reshape(1, -1), (P, E * E)))
    return con


def kernel(**inputs):
    import concourse.bacc as _bacc
    from concourse.bass_utils import run_bass_kernel_spmd as _run

    i = {n: np.asarray(x) for n, x in inputs.items()}
    con = _constants()
    swap = np.arange(D) ^ 1
    ipw = i["L0_attn_in_proj_w"]
    kv1, kv2 = i["L1_xattn_kv1_w"], i["L1_xattn_kv2_w"]

    def pair_rows(v):
        return np.concatenate([np.broadcast_to(v.reshape(-1)[n::2], (P // 2, H // 2)) for n in range(2)], 0)

    arrays = {
        "x": i["x"],
        "ctxT": np.ascontiguousarray(i["ctx_1024"].transpose(0, 2, 1).reshape(B, C, P, SK).transpose(0, 2, 1, 3).reshape(B, P, C * SK)),
        "mask": np.ascontiguousarray(np.concatenate([i["mask_1x1xSxS2_bk0"][0, 0]] * 2, 0)),
        "con": con,
        "w_l0x": np.concatenate([_kmaj(i["L0_xattn_" + n].T) for n in ("Wq", "Wk", "Wv", "Wo")], 1),
        "w_l0a": np.concatenate([_kmaj(w.T) for w in (ipw[:D], ipw[D:2 * D], ipw[2 * D:], ipw[:D][swap], ipw[D:2 * D][swap],
                                                      i["L0_attn_out_proj_w"])], 1),
        "w_l0f": np.concatenate([_kmaj(w) for w in (i["L0_ffn_w_qkv"][:, :D], i["L0_ffn_w_qkv"][:, D:2 * D],
                                                    i["L0_ffn_w_qkv"][:, 2 * D:], i["L0_ffn_w_o"])], 1),
        "w_l1x": np.concatenate([_kmaj(w.T) for w in (i["L1_xattn_q1_w"], i["L1_xattn_q2_w"], kv1[:D], kv1[D:], kv2[:D],
                                                      i["L1_xattn_proj_w"])], 1),
        "w_l1a": _kmaj(i["L1_attn_W"].T),
        "wg": _kmaj(i["L0_ffn_wg"]),
        "we": np.concatenate([
            i["L0_ffn_w1"].reshape(E, C, P, M // MG, MG * P).transpose(0, 3, 2, 1, 4).reshape(E * M // MG, P, C * MG * P),
            i["L0_ffn_w2"].reshape(E, M // MG, MG, P, D).transpose(0, 1, 3, 2, 4).reshape(E * M // MG, P, MG * D)], 2),
        "bb2": i["L0_ffn_bb2"],
        "w_in": _kmaj(i["L1_ffn_W_in"].T),
        "w_out": _kmaj(np.concatenate([i["L1_ffn_W_out"].T, np.zeros((NB * P - WIDTH, D), np.float32)], 0)),
        "b_in": i["L1_ffn_b_in"],
        "rows": np.concatenate([i[n] for n in ("L0_xattn_bo", "L0_ffn_g1", "L0_ffn_b1", "L0_ffn_g2", "L0_ffn_b2", "L1_xattn_proj_b")]),
        "vec": np.concatenate([
            _col(i["L0_xattn_bq"]), _col(i["L0_xattn_bk"]), _col(i["L0_xattn_bv"]), _col(i["L1_attn_decay_logit"]),
            _col(i["L1_attn_b"]), _col(i["L1_attn_conv_b"]),
            i["L1_attn_conv_w"].reshape(C, P, TAPS).transpose(1, 0, 2).reshape(P, -1),
            pair_rows(i["L1_xattn_lambda_1"]), pair_rows(i["L1_xattn_lambda_2"]), _col(i["L1_xattn_norm_w"])], 1),
        "bb1": i["L0_ffn_bb1"].reshape(E, M, P).transpose(0, 2, 1),
    }
    nc = _bacc.Bacc("TRN2", target_bir_lowering=False, num_devices=1)
    feeds, args = {}, {}
    for n, arr in arrays.items():
        arr = np.ascontiguousarray(arr)
        feeds["in_" + n] = arr
        args[n] = nc.dram_tensor("in_" + n, arr.shape, mybir.dt.from_np(arr.dtype), kind="ExternalInput").ap()
    out = nc.dram_tensor("out_0", (B, S, D), F32, kind="ExternalOutput").ap()
    build(nc, args, out)
    r = _run(nc, [feeds], core_ids=[0])
    return r.results[0]["out_0"]
```
